# Optimizing a Trainium2 kernel written in Bass

```python
import numpy as np
import jax
import jax.numpy as jnp

def _softmax(x, axis=-1):
    return jax.nn.softmax(x, axis=axis)

def _gelu(x):
    return jax.nn.gelu(x, approximate=True)

def _silu(x):
    return jax.nn.silu(x)

def _sigmoid(x):
    return jax.nn.sigmoid(x)

def _layernorm(x, axis=-1, eps=1e-05):
    m = jnp.mean(x, axis=axis, keepdims=True)
    v = jnp.var(x, axis=axis, keepdims=True)
    return (x - m) / jnp.sqrt(v + eps)

def _scatter_add(tgt, idx, src, axis=0):
    return tgt.at[idx].add(src)

def _segment_sum(src, seg, n):
    return jax.ops.segment_sum(src, seg, n)
kernel_name = 'mk_seq_postln_d1_jaxref_r4_ab91af'

def setup_inputs(seed: int=0):
    np.random.seed(seed)
    _w = jnp.asarray

    def _L0_attn_setup():
        import jax, jax.numpy as jnp
        import numpy as np
        H, HKV, HD = (16, 4, 128)

        def _rope(x, cos, sin):
            xr = x.reshape(*x.shape[:-1], HD // 2, 2)
            a, b = (xr[..., 0], xr[..., 1])
            c = cos[None, :, None, :]
            s = sin[None, :, None, :]
            return jnp.stack([a * c - b * s, a * s + b * c], axis=-1).reshape(x.shape)
        key = jax.random.key(seed)
        ks = jax.random.split(key, 5)
        B, T, C = (2, 512, 512)
        std = 0.02
        return {'x': jax.random.normal(ks[0], (B, T, C), jnp.float32), 'Wq': jax.random.normal(ks[1], (C, H * HD), jnp.float32) * std, 'bq': jnp.zeros((H * HD,), jnp.float32), 'Wk': jax.random.normal(ks[2], (C, HKV * HD), jnp.float32) * std, 'bk': jnp.zeros((HKV * HD,), jnp.float32), 'Wv': jax.random.normal(ks[3], (C, HKV * HD), jnp.float32) * std, 'bv': jnp.zeros((HKV * HD,), jnp.float32), 'Wo': jax.random.normal(ks[4], (H * HD, C), jnp.float32) * std, 'bo': jnp.zeros((C,), jnp.float32)}
    _L0_attn_in = _L0_attn_setup()

    def _L0_ffn_setup():
        import jax, jax.numpy as jnp
        import numpy as np
        TOP_K = 8
        CAPACITY = 256
        key = jax.random.key(seed)
        k1, k2, k3, k4 = jax.random.split(key, 4)
        B, S, H, E, I = (2, 256, 512, 64, 192)
        hidden_states = jax.random.normal(k1, (B, S, H), dtype=jnp.float32)
        router_weight = jax.random.normal(k2, (E, H), dtype=jnp.float32) * 0.02
        gate_up_proj = jax.random.normal(k3, (E, H, 2 * I), dtype=jnp.float32) * 0.02
        down_proj = jax.random.normal(k4, (E, I, H), dtype=jnp.float32) * 0.02
        return {'hidden_states': hidden_states, 'router_weight': router_weight, 'gate_up_proj': gate_up_proj, 'down_proj': down_proj}
    _L0_ffn_in = _L0_ffn_setup()
    _d = {'L0_attn_x': _L0_attn_in['x'], 'L0_attn_Wq': _L0_attn_in['Wq'], 'L0_attn_bq': _L0_attn_in['bq'], 'L0_attn_Wk': _L0_attn_in['Wk'], 'L0_attn_bk': _L0_attn_in['bk'], 'L0_attn_Wv': _L0_attn_in['Wv'], 'L0_attn_bv': _L0_attn_in['bv'], 'L0_attn_Wo': _L0_attn_in['Wo'], 'L0_attn_bo': _L0_attn_in['bo'], 'L0_ffn_router_weight': _L0_ffn_in['router_weight'], 'L0_ffn_gate_up_proj': _L0_ffn_in['gate_up_proj'], 'L0_ffn_down_proj': _L0_ffn_in['down_proj']}
    _x0 = _d['L0_attn_x']
    _d['L0_attn_x'] = jax.random.normal(jax.random.fold_in(jax.random.key(seed), 1), (1, 2048, 512), dtype=_x0.dtype)
    del _x0
    return _d

def reference(L0_attn_x, L0_attn_Wq, L0_attn_bq, L0_attn_Wk, L0_attn_bk, L0_attn_Wv, L0_attn_bv, L0_attn_Wo, L0_attn_bo, L0_ffn_router_weight, L0_ffn_gate_up_proj, L0_ffn_down_proj):

    def _L0_attn_ref(x, Wq, bq, Wk, bk, Wv, bv, Wo, bo):
        import jax, jax.numpy as jnp
        import numpy as np
        H, HKV, HD = (16, 4, 128)

        def _rope(x, cos, sin):
            xr = x.reshape(*x.shape[:-1], HD // 2, 2)
            a, b = (xr[..., 0], xr[..., 1])
            c = cos[None, :, None, :]
            s = sin[None, :, None, :]
            return jnp.stack([a * c - b * s, a * s + b * c], axis=-1).reshape(x.shape)
        B, T, C = x.shape
        G = H // HKV
        q = (x @ Wq + bq).reshape(B, T, H, HD)
        k = (x @ Wk + bk).reshape(B, T, HKV, HD)
        v = (x @ Wv + bv).reshape(B, T, HKV, HD)
        theta = 1.0 / 10000.0 ** (jnp.arange(0, HD, 2, dtype=jnp.float32) / HD)
        freqs = jnp.arange(T, dtype=jnp.float32)[:, None] * theta[None, :]
        cos, sin = (jnp.cos(freqs), jnp.sin(freqs))
        q = _rope(q, cos, sin)
        k = _rope(k, cos, sin)
        q = q.transpose(0, 2, 1, 3).reshape(B, G, HKV, T, HD)
        k = k.transpose(0, 2, 1, 3)
        v = v.transpose(0, 2, 1, 3)
        scale = 1.0 / np.sqrt(H).astype(np.float32)
        scores = jnp.einsum('bgjtd,bjsd->bgjts', q, k) * scale
        mask = jnp.tril(jnp.ones((T, T), dtype=bool))
        scores = jnp.where(mask[None, None, None], scores, -jnp.inf)
        wei = jax.nn.softmax(scores, axis=-1)
        out = jnp.einsum('bgjts,bjsd->bgjtd', wei, v)
        out = out.transpose(0, 3, 1, 2, 4).reshape(B, T, H * HD)
        return out @ Wo + bo

    def _L0_ffn_ref(hidden_states, router_weight, gate_up_proj, down_proj):
        import jax, jax.numpy as jnp
        import numpy as np
        TOP_K = 8
        CAPACITY = 256
        B, S, H = hidden_states.shape
        E = router_weight.shape[0]
        K, C = (TOP_K, CAPACITY)
        x = hidden_states.reshape(-1, H)
        logits = x @ router_weight.T
        probs = jax.nn.softmax(logits, axis=-1)
        topw, topi = jax.lax.top_k(probs, K)
        topw = topw / jnp.sum(topw, axis=-1, keepdims=True)
        flat_e = topi.reshape(-1)
        oh = jax.nn.one_hot(flat_e, E, dtype=jnp.int32)
        pos = jnp.take_along_axis(jnp.cumsum(oh, axis=0), flat_e[:, None], axis=1)[:, 0] - 1
        x_rep = jnp.repeat(x, K, axis=0)
        xe = jnp.zeros((E, C, H), x.dtype).at[flat_e, pos].set(x_rep, mode='drop')
        gu = jnp.einsum('ech,ehf->ecf', xe, gate_up_proj)
        g, u = jnp.split(gu, 2, axis=-1)
        h = jax.nn.silu(g) * u
        ye = jnp.einsum('eci,eih->ech', h, down_proj)
        valid = pos < C
        y_flat = jnp.where(valid[:, None], ye[flat_e, jnp.minimum(pos, C - 1)], 0.0)
        y = jnp.sum(y_flat.reshape(-1, K, H) * topw.reshape(-1, K)[..., None], axis=1)
        return y.reshape(B, S, H)
    x = L0_attn_x
    x = _layernorm(x + _L0_attn_ref(x, L0_attn_Wq, L0_attn_bq, L0_attn_Wk, L0_attn_bk, L0_attn_Wv, L0_attn_bv, L0_attn_Wo, L0_attn_bo), axis=-1)
    x = _layernorm(x + _L0_ffn_ref(x, L0_ffn_router_weight, L0_ffn_gate_up_proj, L0_ffn_down_proj), axis=-1)
    return x

_drawn_inputs = setup_inputs


def setup_inputs(seed=0):
    import zlib

    import numpy as np

    out = dict(_drawn_inputs(seed))
    spreads = {'L0_attn_bq': (0.0, 0.8),
     'L0_attn_bk': (0.0, 0.8),
     'L0_attn_bv': (0.0, 0.1),
     'L0_attn_bo': (0.0, 0.1)}
    factors = {'L0_attn_Wq': 3.572,
     'L0_attn_Wk': 3.514,
     'L0_ffn_router_weight': 5.471,
     'L0_ffn_gate_up_proj': 4.936,
     'L0_ffn_down_proj': 4.934}
    for name, (base, spread) in spreads.items():
        noise = np.random.default_rng([zlib.crc32(name.encode()), seed]).standard_normal(out[name].shape)
        drawn = base * np.exp(spread * noise) if base else spread * noise
        out[name] = jnp.asarray(drawn.astype(out[name].dtype))
    for name, factor in factors.items():
        out[name] = (out[name] * factor).astype(out[name].dtype)
    return out
```

```python
from contextlib import ExitStack

import numpy as np

import concourse.bass as bass
from concourse import mybir

F32 = mybir.dt.float32
F32R = mybir.dt.float32r
BF16 = mybir.dt.bfloat16
I32 = mybir.dt.int32
U32 = mybir.dt.uint32
ALU = mybir.AluOpType
ACT = mybir.ActivationFunctionType
AX_X = mybir.AxisListType.X

P = 128
T = 2048
C = 512
H, HKV, HD = 16, 4, 128
G = H // HKV
E, TOPK, CAP = 64, 8, 256
I = 192
IT = I - P
NB = T // P
NC = C // P
NT = T // 512
EPS = 1e-5
MASKED = -1.0e30
HI, LO = 0, 1
SLOTS = E * CAP
CH = CAP // P


def loop(eng, n, body):
    body(0, True)
    with eng.Fori(1, n) as i:
        body(i, False)


def wait_alone(eng, passed, sem, value):
    eng.wait_ge(sem, value)
    eng.sem_inc(passed, 1)


def split3(a, b):
    return ((a[LO], b[HI]), (a[HI], b[LO]), (a[HI], b[HI]))


def stage_project(nc, x, wqk, bqk, wv, bv, cos, sin, ident_d, qk_d, v_d):
    NH = H + HKV
    with ExitStack() as ctx:
        def sb(name, shape, dt=F32):
            return ctx.enter_context(nc.sbuf_tensor("p1_" + name, shape, dt))

        def ps(name, shape):
            return ctx.enter_context(nc.psum_tensor("p1_" + name, shape, F32))

        def sem(name):
            return ctx.enter_context(nc.semaphore("p1_" + name))

        ident = sb("ident", [P, P])
        xraw = [sb(f"xraw{k}", [P, C]) for k in range(2)]
        xt = [[sb(f"xt{k}{s}", [P, NC, P], F32R) for s in "hl"] for k in range(2)]
        xT = [sb(f"xT{s}", [P, NC, T], F32R) for s in "hl"]
        wv_raw = sb("wv_raw", [P, NC * C])
        wv_s = [sb(f"wv{s}", [P, NC * C], F32R) for s in "hl"]
        bv_b = sb("bv_b", [P, C])
        vfull = [sb(f"vfull{k}", [P, C]) for k in range(2)]
        vout = [sb(f"vout{k}", [P, HKV, 2, HD], F32R) for k in range(2)]
        cosT, sinT = sb("cosT", [P, T]), sb("sinT", [P, T])
        bias = sb("bias", [P, NH])
        w_raw = [sb(f"w_raw{k}", [P, NC * P]) for k in range(2)]
        w_s = [[sb(f"w{k}{s}", [P, NC * P], F32R) for s in "hl"] for k in range(2)]
        rc = [sb(f"rc{k}", [P, 512]) for k in range(2)]
        rs = [sb(f"rs{k}", [P, 512]) for k in range(2)]
        qr = [sb(f"qr{k}", [P, 512]) for k in range(2)]
        qout = [sb(f"qout{k}", [P, NT, 2, 512], F32R) for k in range(2)]

        pt = [ps(f"pt{k}", [P, NC, P]) for k in range(2)]
        pv = [ps(f"pv{k}", [P, C]) for k in range(2)]
        pq = [ps(f"pq{k}", [P, 512]) for k in range(NT)]

        x_in = [sem(f"x_in{k}") for k in range(2)]
        const_in, wv_in = sem("const_in"), sem("wv_in")
        wv_hi, wv_lo = sem("wv_hi"), sem("wv_lo")
        xt_done, xt_hi, xt_lo, xt_kept = sem("xt_done"), sem("xt_hi"), sem("xt_lo"), sem("xt_kept")
        v_mm, v_full, v_hi, v_lo = sem("v_mm"), sem("v_full"), sem("v_hi"), sem("v_lo")
        v_out = [sem(f"v_out{k}") for k in range(2)]
        w_in = [sem(f"w_in{k}") for k in range(2)]
        w_hi, w_lo = sem("w_hi"), sem("w_lo")
        q_mm, q_prod, q_rot, q_hi, q_lo = sem("q_mm"), sem("q_prod"), sem("q_rot"), sem("q_hi"), sem("q_lo")
        q_out = [sem(f"q_out{k}") for k in range(2)]

        passed = sem("passed")
        block = ctx.enter_context(nc.Block())

        @block.sync
        def _(sp):
            sp.dma_start(ident[:], ident_d).then_inc(const_in, 16)
            for k in range(2):
                sp.dma_start(xraw[k][:], x[k * P:(k + 1) * P, :]).then_inc(x_in[k], 16)
            sp.dma_start(wv_raw[:], wv).then_inc(wv_in, 16)
            sp.dma_start(bv_b[:], bv.partition_broadcast(P)).then_inc(wv_in, 16)
            for k in range(2):
                sp.dma_start(w_raw[k][:], wqk[k]).then_inc(w_in[k], 16)
            sp.dma_start(cosT[:], cos).then_inc(const_in, 16)
            sp.dma_start(sinT[:], sin).then_inc(const_in, 16)
            sp.dma_start(bias[:], bqk).then_inc(const_in, 16)

            def v_step(i, first, last=False):
                for k in range(2):
                    tb = i * 2 + k
                    if not last:
                        sp.wait_ge(xt_done, tb + 1)
                        sp.dma_start(xraw[k][:], x[bass.ds((tb + 2) * P, P), :]).then_inc(x_in[k], 16)
                    sp.wait_ge(v_lo, tb + 1)
                    sp.dma_start(v_d[bass.ds(tb, 1)].rearrange("o j p h d -> p (o j) h d"),
                                 vout[k][:].bitcast(F32)).then_inc(v_out[k], 16)

            with sp.Fori(0, NB // 2 - 1) as i:
                v_step(i, False)
            v_step(NB // 2 - 1, False, last=True)

            def head_step(i, first, last=False):
                for k in range(2):
                    n = i * 2 + k
                    if not last:
                        sp.wait_ge(w_lo, n + 1)
                        sp.dma_start(w_raw[k][:], wqk[bass.ds(n + 2, 1)].rearrange("o p m -> (o p) m")
                                     ).then_inc(w_in[k], 16)
                    sp.wait_ge(q_lo, n * NT + NT)
                    sp.dma_start(qk_d[bass.ds(n, 1)].rearrange("o p c h t -> (o p) c h t"),
                                 qout[k][:].bitcast(F32)).then_inc(q_out[k], 16)

            with sp.Fori(0, NH // 2 - 1) as i:
                head_step(i, False)
            head_step(NH // 2 - 1, False, last=True)
            for k in range(2):
                sp.wait_ge(v_out[k], 16 * (NB // 2))
                sp.wait_ge(q_out[k], 16 * (NH // 2))

        @block.tensor
        def _(pe):
            def transposes(tb, k, i, early):
                pe.wait_ge(x_in[k], i * 16 + 16)
                if not early:
                    pe.wait_ge(xt_lo, tb - 1)
                for c in range(NC):
                    last = nc.tensor.transpose(pt[k][:, c, :], xraw[k][:, c * P:(c + 1) * P], ident[:])
                last.then_inc(xt_done, 1)

            def project_v(tb, k, early):
                pe.wait_ge(xt_lo, tb + 1)
                if not early:
                    pe.wait_ge(v_full, tb - 1)
                for n, (a, b) in enumerate(split3(xt[k], wv_s)):
                    for c in range(NC):
                        last = nc.tensor.matmul(pv[k][:], a[:, c, :], b[:, c * C:(c + 1) * C],
                                                start=(n == 0 and c == 0), stop=(n == 2 and c == NC - 1))
                last.then_inc(v_mm, 1)

            pe.wait_ge(const_in, 64)
            transposes(0, 0, 0, True)
            pe.wait_ge(wv_lo, 1)
            transposes(1, 1, 0, True)
            project_v(0, 0, True)
            transposes(2, 0, 1, False)
            project_v(1, 1, True)
            with pe.Fori(1, NB // 2 - 1) as i:
                transposes(i * 2 + 1, 1, i, False)
                project_v(i * 2, 0, False)
                transposes(i * 2 + 2, 0, i + 1, False)
                project_v(i * 2 + 1, 1, False)
            transposes(NB - 1, 1, NB // 2 - 1, False)
            project_v(NB - 2, 0, False)
            project_v(NB - 1, 1, False)
            pe.wait_ge(xt_kept, NB)

            def head_step(i, first):
                for k in range(2):
                    n = i * 2 + k
                    pe.wait_ge(w_lo, n + 1)
                    for t in range(NT):
                        if not (first and k == 0):
                            pe.wait_ge(q_prod, n * NT + t - NT + 1)
                        for m, (a, b) in enumerate(split3(w_s[k], xT)):
                            for c in range(NC):
                                last = nc.tensor.matmul(pq[t][:], a[:, c * P:(c + 1) * P],
                                                        b[:, c, t * 512:(t + 1) * 512],
                                                        start=(m == 0 and c == 0), stop=(m == 2 and c == NC - 1))
                        last.then_inc(q_mm, 1)

            loop(pe, NH // 2, head_step)

        @block.scalar
        def _(act):
            act.wait_ge(wv_in, 32)
            nc.scalar.copy(wv_s[HI][:], wv_raw[:]).then_inc(wv_hi, 1)

            def x_hi(tb, k, early):
                act.wait_ge(xt_done, tb + 1)
                if not early:
                    act.wait_ge(v_mm, tb - 1)
                    act.wait_ge(xt_kept, tb - 1)
                nc.scalar.copy(xt[k][HI][:], pt[k][:]).then_inc(xt_hi, 1)

            def v_hi_part(tb, k, i, early):
                act.wait_ge(v_full, tb + 1)
                if not early:
                    act.wait_ge(v_out[k], i * 16)
                nc.scalar.copy(vout[k][:, :, HI, :], vfull[k][:].rearrange("p (j d) -> p j d", j=HKV)
                               ).then_inc(v_hi, 1)

            x_hi(0, 0, True)
            x_hi(1, 1, True)
            v_hi_part(0, 0, 0, True)
            x_hi(2, 0, False)
            v_hi_part(1, 1, 0, True)
            with act.Fori(1, NB // 2 - 1) as i:
                x_hi(i * 2 + 1, 1, False)
                v_hi_part(i * 2, 0, i, False)
                x_hi(i * 2 + 2, 0, False)
                v_hi_part(i * 2 + 1, 1, i, False)
            x_hi(NB - 1, 1, False)
            v_hi_part(NB - 2, 0, NB // 2 - 1, False)
            v_hi_part(NB - 1, 1, NB // 2 - 1, False)

            def weights_hi(n, k, i, early):
                act.wait_ge(w_in[k], i * 16 + 16)
                if not early:
                    act.wait_ge(q_mm, n * NT - NT)
                nc.scalar.copy(w_s[k][HI][:], w_raw[k][:]).then_inc(w_hi, 1)

            def q_hi_part(q, k, t, i, early):
                act.wait_ge(q_rot, q + 1)
                if t == 0 and not early:
                    act.wait_ge(q_out[k], i * 16)
                nc.scalar.copy(qout[k][:, t, HI, :], qr[t % 2][:]).then_inc(q_hi, 1)

            weights_hi(0, 0, 0, True)

            def head_step(i, first, last=False):
                for k in range(2):
                    n = i * 2 + k
                    if not (last and k == 1):
                        weights_hi(n + 1, 1 - k, i + k, first and k == 0)
                    for t in range(NT):
                        q_hi_part(n * NT + t, k, t, i, first)

            head_step(0, True)
            with act.Fori(1, NH // 2 - 1) as i:
                head_step(i, False)
            head_step(NH // 2 - 1, False, last=True)

        @block.vector
        def _(dve):
            dve.wait_ge(wv_hi, 1)
            nc.vector.tensor_tensor(wv_s[LO][:], wv_raw[:], wv_s[HI][:].bitcast(F32), ALU.subtract
                                    ).then_inc(wv_lo, 1)

            def x_lo(tb, k):
                dve.wait_ge(xt_hi, tb + 1)
                nc.vector.tensor_tensor(xt[k][LO][:], pt[k][:], xt[k][HI][:].bitcast(F32), ALU.subtract
                                        ).then_inc(xt_lo, 1)
                nc.vector.tensor_copy(xT[HI][:, :, bass.ds(tb * P, P)], xt[k][HI][:].bitcast(F32))
                dve.wait_ge(xt_lo, tb + 1)
                nc.vector.tensor_copy(xT[LO][:, :, bass.ds(tb * P, P)], xt[k][LO][:].bitcast(F32)).then_inc(xt_kept, 1)

            def v_bias(tb, k, early):
                dve.wait_ge(v_mm, tb + 1)
                if not early:
                    dve.wait_ge(v_lo, tb - 1)
                nc.vector.tensor_tensor(vfull[k][:], pv[k][:], bv_b[:], ALU.add).then_inc(v_full, 1)

            def v_lo_part(tb, k):
                dve.wait_ge(v_hi, tb + 1)
                nc.vector.tensor_tensor(vout[k][:, :, LO, :], vfull[k][:].rearrange("p (j d) -> p j d", j=HKV),
                                        vout[k][:, :, HI, :].bitcast(F32), ALU.subtract).then_inc(v_lo, 1)

            x_lo(0, 0)
            x_lo(1, 1)
            v_bias(0, 0, True)
            x_lo(2, 0)
            v_lo_part(0, 0)
            v_bias(1, 1, True)
            with dve.Fori(1, NB // 2 - 1) as i:
                x_lo(i * 2 + 1, 1)
                v_lo_part(i * 2 - 1, 1)
                v_bias(i * 2, 0, False)
                x_lo(i * 2 + 2, 0)
                v_lo_part(i * 2, 0)
                v_bias(i * 2 + 1, 1, False)
            x_lo(NB - 1, 1)
            v_lo_part(NB - 3, 1)
            v_bias(NB - 2, 0, False)
            v_lo_part(NB - 2, 0)
            v_bias(NB - 1, 1, False)
            v_lo_part(NB - 1, 1)

            def weights_lo(n, k):
                dve.wait_ge(w_hi, n + 1)
                nc.vector.tensor_tensor(w_s[k][LO][:], w_raw[k][:], w_s[k][HI][:].bitcast(F32), ALU.subtract
                                        ).then_inc(w_lo, 1)

            def q_products(q, n, t, early):
                dve.wait_ge(q_mm, q + 1)
                if not early:
                    dve.wait_ge(q_rot, q - 1)
                k, half, cols = t % 2, HD // 2, slice(t * 512, (t + 1) * 512)
                nc.vector.scalar_tensor_tensor(rc[k][:], pq[t][:], bias[:, bass.ds(n, 1)], cosT[:, cols],
                                               ALU.add, ALU.mult)
                nc.vector.scalar_tensor_tensor(rs[k][0:half, :], pq[t][half:P, :], bias[half:P, bass.ds(n, 1)],
                                               sinT[half:P, cols], ALU.add, ALU.mult)
                nc.vector.scalar_tensor_tensor(rs[k][half:P, :], pq[t][0:half, :], bias[0:half, bass.ds(n, 1)],
                                               sinT[0:half, cols], ALU.add, ALU.mult).then_inc(q_prod, 1)

            def q_lo_part(q, k, t):
                dve.wait_ge(q_hi, q + 1)
                nc.vector.tensor_tensor(qout[k][:, t, LO, :], qr[t % 2][:], qout[k][:, t, HI, :].bitcast(F32),
                                        ALU.subtract).then_inc(q_lo, 1)

            dve.wait_ge(const_in, 64)
            weights_lo(0, 0)

            def head_step(i, first, last=False):
                for k in range(2):
                    n = i * 2 + k
                    if not (last and k == 1):
                        weights_lo(n + 1, 1 - k)
                    for t in range(NT):
                        q_products(n * NT + t, n, t, first and k == 0 and t < 2)
                        if t > 0:
                            q_lo_part(n * NT + t - 1, k, t - 1)
                        elif k > 0:
                            q_lo_part(n * NT - 1, 0, NT - 1)
                        elif not first:
                            q_lo_part(n * NT - 1, 1, NT - 1)

            head_step(0, True)
            with dve.Fori(1, NH // 2 - 1) as i:
                head_step(i, False)
            head_step(NH // 2 - 1, False, last=True)
            q_lo_part(NH * NT - 1, 1, NT - 1)

        @block.gpsimd
        def _(pool):
            def sum_products(i, first):
                for k in range(2):
                    for t in range(NT):
                        q = i * (2 * NT) + (k * NT + t)
                        pool.wait_ge(q_prod, q + 1)
                        if not (first and k == 0 and t < 2):
                            pool.wait_ge(q_lo, q - 1)
                        nc.gpsimd.tensor_tensor(qr[t % 2][:], rc[t % 2][:], rs[t % 2][:], ALU.add).then_inc(q_rot, 1)

            loop(pool, NH // 2, sum_products)


def stage_attend(nc, ident_d, mask_d, qk_d, v_d, o_d):
    U = NB * G
    blk = lambda u: u // G
    width = lambda u: (blk(u) + 1) * P
    ngrp = lambda u: 1 if width(u) <= 1024 else 2
    ntr = lambda u: -(-(blk(u) + 1) // 4)
    SG = [0]
    TG = [0]
    for u in range(U):
        SG.append(SG[-1] + ngrp(u))
        TG.append(TG[-1] + ntr(u))
    PAIRS = U // 2
    KEEP = 4
    LAG = 2

    def score_group(u, a):
        return (u % 2) if ngrp(u) == 1 else a

    last_use = {}
    before = {}
    for u in range(U):
        for a in range(ngrp(u)):
            s = score_group(u, a)
            before[(u, a)] = last_use.get(s)
            last_use[s] = SG[u] + a

    with ExitStack() as ctx:
        def sb(name, shape, dt=F32):
            return ctx.enter_context(nc.sbuf_tensor("p2_" + name, shape, dt))

        def ps(name, shape):
            return ctx.enter_context(nc.psum_tensor("p2_" + name, shape, F32))

        def sem(name):
            return ctx.enter_context(nc.semaphore("p2_" + name))

        ident = sb("ident", [P, P])
        identb = sb("identb", [P, P], BF16)
        maskb = sb("maskb", [P, P], BF16)
        maskf = sb("maskf", [P, P])
        kT = sb("kT", [P, NT, 2, 512], F32R)
        v = sb("v", [P, NB, 2, HD], F32R)
        q = [sb(f"q{k}", [P, G, 2, 512], F32R) for k in range(2)]
        prob = [sb(f"prob{k}", [P, T]) for k in range(KEEP)]
        pT = [[sb(f"pT{k}{s}", [P, NB, 2, P], F32R) for s in "hl"] for k in range(2)]
        oT = [sb(f"oT{k}", [P, 2, 2, P], F32R) for k in range(2)]
        nmax = sb("nmax", [P, KEEP, 2])
        nm = sb("nm", [P, KEEP])
        rsum = sb("rsum", [P, KEEP, 2])
        den = sb("den", [P, KEEP])
        inv = sb("inv", [P, KEEP])

        S = ps("S", [P, 2, 1024])
        TP = [ps(f"TP{k}", [P, 4, P]) for k in range(2)]
        O = [ps(f"O{k}", [P, 2, P]) for k in range(2)]

        const_in, const_ready = sem("const_in"), sem("const_ready")
        k_in = [sem(f"k_in{c}") for c in range(NT)]
        v_in = [sem(f"v_in{c}") for c in range(NT)]
        q_in = [sem(f"q_in{k}") for k in range(2)]
        scored, max_part, max_ready, exped = sem("scored"), sem("max_part"), sem("max_ready"), sem("exped")
        den_ready, inv_ready, normed = sem("den_ready"), sem("inv_ready"), sem("normed")
        turned, turn_hi, turn_lo = sem("turned"), sem("turn_hi"), sem("turn_lo")
        weighed, o_hi, o_lo = sem("weighed"), sem("o_hi"), sem("o_lo")
        o_out = [sem(f"o_out{k}") for k in range(2)]
        o_stored = sem("o_stored")
        FREE = 2

        passed = sem("passed")
        block = ctx.enter_context(nc.Block())

        def load_q(sp, j, tc):
            sp.dma_start(q[tc % 2][:].bitcast(F32), qk_d[bass.ds(j * G, G), :, tc]
                         .rearrange("g p h t -> p g h t")).then_inc(q_in[tc % 2], 16)

        def load_kv(sp, j):
            for c in range(NT):
                sp.dma_start(kT[:, c].bitcast(F32), qk_d[bass.ds(j + H, 1), :, c].rearrange("o p h t -> (o p) h t")
                             ).then_inc(k_in[c], 16)
                sp.dma_start(v[:, c * 4:(c + 1) * 4, :, :].bitcast(F32), v_d[c * 4:(c + 1) * 4, bass.ds(j, 1)]
                             .rearrange("b o p h d -> (o p) b h d")).then_inc(v_in[c], 16)

        @block.sync
        def _(sp):
            sp.dma_start(ident[:], ident_d).then_inc(const_in, 16)
            sp.dma_start(maskf[:], mask_d).then_inc(const_in, 16)
            load_q(sp, 0, 0)
            load_kv(sp, 0)
            load_q(sp, 0, 1)

            def head(j, last=False):
                for p in range(PAIRS):
                    b, g = blk(2 * p), 2 * p % G
                    sp.wait_ge(o_lo, j * PAIRS + (p + 1 + FREE))
                    sp.dma_start(o_d[b, :, bass.ds(j, 1), g:g + 2].rearrange("p o g h t -> p (o g) h t"),
                                 oT[p % 2][:].bitcast(F32)).then_inc(o_out[p % 2], 16)
                    if p % 8 == 6:
                        tc = p // 8
                        sp.wait_ge(scored, j * SG[U] + SG[16 * tc + 16])
                        if tc < 2:
                            load_q(sp, j, tc + 2)
                        elif not last:
                            load_q(sp, j + 1, tc - 2)
                if not last:
                    load_kv(sp, j + 1)
                for k in range(2):
                    sp.wait_ge(o_out[k], j * (8 * PAIRS) + 8 * PAIRS)
                sp.sem_inc(o_stored, 1)

            sp.sem_inc(o_stored, 1)
            with sp.Fori(0, HKV - 1) as j:
                head(j)
            head(HKV - 1, last=True)

        @block.tensor
        def _(pe):
            pe.wait_ge(const_ready, 2)
            with pe.Fori(0, HKV) as j:
                def scores(u, a):
                    b, g, tc = blk(u), u % G, u // 16
                    if u % 16 == 0 and a == 0:
                        pe.wait_ge(k_in[tc], j * 16 + 16)
                        pe.wait_ge(q_in[tc % 2], j * 32 + (16 + 16 * (tc // 2)))
                    qs = [q[tc % 2][:, g, s, (b % 4) * P:(b % 4 + 1) * P] for s in (HI, LO)]
                    if before[(u, a)] is not None:
                        pe.wait_ge(exped, j * SG[U] + (before[(u, a)] + 1))
                    s = score_group(u, a)
                    for c0 in range(a * 1024, min(width(u), a * 1024 + 1024), 512):
                        w = min(512, width(u) - c0)
                        out = S[:, s, c0 - a * 1024:c0 - a * 1024 + w]
                        for n, (x, y) in enumerate(split3(qs, [kT[:, c0 // 512, s2, 0:w] for s2 in (HI, LO)])):
                            mm = nc.tensor.matmul(out, x, y, start=(n == 0), stop=(n == 2))
                        if c0 + w == width(u):
                            mm = nc.tensor.matmul(S[:, s, width(u) - P - a * 1024:width(u) - a * 1024], identb[:],
                                                  maskb[:], start=False, stop=True, skip_group_check=True)
                    mm.then_inc(scored, 1)

                def turn(u, t):
                    if t == 0:
                        pe.wait_ge(normed, j * U + (u + 1))
                    n = TG[u] + t
                    pe.wait_ge(turn_lo, j * TG[U] + (n + 1))
                    for s in range(4 * t, min(4 * t + 4, blk(u) + 1)):
                        mm = nc.tensor.transpose(TP[n % 2][:, s % 4, :], prob[u % KEEP][:, s * P:(s + 1) * P], ident[:])
                    mm.then_inc(turned, 1)

                def weigh(p, part):
                    nb = blk(2 * p) + 1
                    cut = (nb + 1) // 2
                    if part == 0:
                        if p % 8 == 0:
                            pe.wait_ge(v_in[p // 8], j * 16 + 16)
                        pe.wait_ge(turn_lo, j * TG[U] + (TG[2 * p + 2] + FREE))
                        pe.wait_ge(o_lo, j * PAIRS + (p + 1))
                    for s in (range(cut), range(cut, nb))[part]:
                        for n, (x, y) in enumerate(split3([v[:, s, h, :] for h in (HI, LO)],
                                                          [pT[p % 2][h][:, s, :, :] for h in (HI, LO)])):
                            mm = nc.tensor.matmul(O[p % 2][:], x, y, start=(s == 0 and n == 0),
                                                  stop=(s == nb - 1 and n == 2))
                            if s == nb - 1 and n == 2:
                                mm.then_inc(weighed, 1)

                for i in range(U + LAG + 2):
                    u = i - LAG
                    turns = list(range(ntr(u))) if 0 <= u < U else []
                    for a in range(2):
                        if i < U and a < ngrp(i):
                            scores(i, a)
                        for t in turns[2 * a:2 * a + 2]:
                            turn(u, t)
                    if i >= 4:
                        weigh((i - 4) // 2, i % 2)

        @block.scalar
        def _(act):
            act.wait_ge(const_in, 32)
            nc.scalar.copy(identb[:], ident[:]).then_inc(const_ready, 1)
            nc.scalar.copy(maskb[:], maskf[:]).then_inc(const_ready, 1)
            act.sem_inc(weighed, FREE)
            with act.Fori(0, HKV) as j:
                def exp(u, a):
                    if a == 0:
                        act.wait_ge(max_ready, j * U + (u + 1))
                    w = min(1024, width(u) - a * 1024)
                    nc.scalar.activation(prob[u % KEEP][:, a * 1024:a * 1024 + w], S[:, score_group(u, a), 0:w], ACT.Exp,
                                         bias=nm[:, u % KEEP:u % KEEP + 1],
                                         accum_out=rsum[:, u % KEEP, a:a + 1]).then_inc(exped, 1)

                def p_hi(u, t):
                    n, p = TG[u] + t, u // 2
                    act.wait_ge(turned, j * TG[U] + (n + 1))
                    if u % 2 == 0 and t == 0:
                        act.wait_ge(weighed, j * PAIRS + (p + 1))
                    m = min(4, blk(u) + 1 - 4 * t)
                    nc.scalar.copy(pT[p % 2][HI][:, 4 * t:4 * t + m, u % 2, :], TP[n % 2][:, 0:m, :]).then_inc(turn_hi, 1)

                def out_hi(p):
                    act.wait_ge(weighed, j * PAIRS + (p + 1 + FREE))
                    if p < 2:
                        act.wait_ge(o_stored, j + 1)
                    else:
                        act.wait_ge(o_out[p % 2], j * (8 * PAIRS) + 16 * (p // 2))
                    nc.scalar.copy(oT[p % 2][:, :, HI, :], O[p % 2][:]).then_inc(o_hi, 1)

                for i in range(U + LAG + 3):
                    u = i - LAG
                    if i >= 6 and i % 2 == 0:
                        out_hi((i - 6) // 2)
                    if 0 <= u < U:
                        for t in range(ntr(u)):
                            p_hi(u, t)
                    if i < U:
                        for a in range(ngrp(i)):
                            exp(i, a)

        @block.vector
        def _(dve):
            dve.sem_inc(turn_lo, FREE)
            dve.sem_inc(o_lo, FREE)
            with dve.Fori(0, HKV) as j:
                def row_max(u, a):
                    k = u % KEEP
                    dve.wait_ge(scored, j * SG[U] + (SG[u] + a + 1))
                    w = min(1024, width(u) - a * 1024)
                    out = nm[:, k:k + 1] if ngrp(u) == 1 else nmax[:, k, a:a + 1]
                    r = nc.vector.reduce_max(out, S[:, score_group(u, a), 0:w], AX_X, negate=True)
                    r.then_inc(max_ready if ngrp(u) == 1 else max_part, 1)
                    if a == 1:
                        dve.wait_ge(max_part, j * (2 * (SG[U] - U)) + 2 * (SG[u + 1] - u - 1))
                        nc.vector.tensor_tensor(nm[:, k:k + 1], nmax[:, k, 0:1], nmax[:, k, 1:2], ALU.min
                                                ).then_inc(max_ready, 1)

                def recip(u):
                    k = u % KEEP
                    dve.wait_ge(exped, j * SG[U] + SG[u + 1])
                    if ngrp(u) == 1:
                        nc.vector.reciprocal(inv[:, k:k + 1], rsum[:, k, 0:1]).then_inc(inv_ready, 1)
                    else:
                        nc.vector.tensor_tensor(den[:, k:k + 1], rsum[:, k, 0:1], rsum[:, k, 1:2], ALU.add
                                                ).then_inc(den_ready, 1)
                        dve.wait_ge(den_ready, j * (SG[U] - U) + (SG[u + 1] - u - 1))
                        nc.vector.reciprocal(inv[:, k:k + 1], den[:, k:k + 1]).then_inc(inv_ready, 1)

                def p_lo(u, t):
                    n, p = TG[u] + t, u // 2
                    dve.wait_ge(turn_hi, j * TG[U] + (n + 1))
                    m = min(4, blk(u) + 1 - 4 * t)
                    nc.vector.tensor_tensor(pT[p % 2][LO][:, 4 * t:4 * t + m, u % 2, :], TP[n % 2][:, 0:m, :],
                                            pT[p % 2][HI][:, 4 * t:4 * t + m, u % 2, :].bitcast(F32), ALU.subtract
                                            ).then_inc(turn_lo, 1)

                def out_lo(p):
                    dve.wait_ge(o_hi, j * PAIRS + (p + 1))
                    nc.vector.tensor_tensor(oT[p % 2][:, :, LO, :], O[p % 2][:], oT[p % 2][:, :, HI, :].bitcast(F32),
                                            ALU.subtract).then_inc(o_lo, 1)

                for i in range(U + LAG + 3):
                    u = i - LAG
                    turns = list(range(ntr(u))) if 0 <= u < U else []
                    if i >= 6 and i % 2 == 0:
                        out_lo((i - 6) // 2)
                    if 1 <= i <= U:
                        recip(i - 1)
                    for a in range(2):
                        if i < U and a < ngrp(i):
                            row_max(i, a)
                        for t in turns[2 * a:2 * a + 2]:
                            p_lo(u, t)

        @block.gpsimd
        def _(pool):
            with pool.Fori(0, HKV) as j:
                for u in range(U):
                    k = u % KEEP
                    wait_alone(pool, passed, inv_ready, j * U + (u + 1))
                    nc.gpsimd.tensor_scalar(prob[k][:, 0:width(u)], prob[k][:, 0:width(u)], inv[:, k:k + 1], 1.0,
                                            ALU.mult, ALU.mult).then_inc(normed, 1)


def stage_route(nc, x, wo, bo, rw, ident_d, lower_d, o_d, x1_d, slot_d, comb, wcomb):
    with ExitStack() as ctx:
        def sb(name, shape, dt=F32):
            return ctx.enter_context(nc.sbuf_tensor("p3_" + name, shape, dt))

        def ps(name, shape):
            return ctx.enter_context(nc.psum_tensor("p3_" + name, shape, F32))

        def sem(name):
            return ctx.enter_context(nc.semaphore("p3_" + name))

        PARTS = 4
        wo_raw = [sb(f"wo_raw{k}", [P, H // PARTS, C]) for k in range(2)]
        wo_s = [sb(f"wo{s}", [P, H, C], F32R) for s in "hl"]
        ident, lower, ones = sb("ident", [P, P]), sb("lower", [P, P]), sb("ones", [P, P])
        bo_b = sb("bo_b", [P, C])
        rwT = sb("rwT", [P, NC, E])
        eps = sb("eps", [P, 1])
        iota_e = sb("iota_e", [P, E])
        tok = sb("tok", [P, 1], I32)
        zero = sb("zero", [P, SLOTS // P], I32)
        ot = [sb(f"ot{k}", [P, H, 2, P], F32R) for k in range(2)]
        xr = [sb(f"xr{k}", [P, C]) for k in range(2)]
        xb = [sb(f"xb{k}", [P, C]) for k in range(2)]
        h = [sb(f"h{k}", [P, C]) for k in range(2)]
        st = sb("st", [P, 6])
        mv = sb("mv", [P, 2])
        sd, rstd = sb("sd", [P, 1]), sb("rstd", [P, 1])
        x1 = [sb(f"x1{k}", [P, C]) for k in range(2)]
        x1T = sb("x1T", [P, NC, P])
        top, topi, topf = sb("top", [P, TOPK]), sb("topi", [P, TOPK], U32), sb("topf", [P, TOPK])
        ntop, et, esum, einv = sb("ntop", [P, 1]), sb("et", [P, TOPK]), sb("esum", [P, 1]), sb("einv", [P, 1])
        hot = sb("hot", [P, TOPK, E])
        mask = sb("mask", [P, E])
        count = sb("count", [P, E])
        posn = sb("posn", [P, E])
        pick = sb("pick", [P, TOPK, E])
        pos = sb("pos", [P, TOPK])
        slot, over, wk, keep = sb("slot", [P, TOPK]), sb("over", [P, TOPK]), sb("wk", [P, TOPK]), sb("keep", [P, TOPK])
        slot_out = sb("slot_out", [P, TOPK])
        slot_i = [sb(f"slot_i{k}", [P, TOPK], U32) for k in range(2)]

        acc = [ps(f"acc{k}", [P, C]) for k in range(2)]
        xtp = ps("xtp", [P, NC, P])
        lg = ps("lg", [P, E])
        cum = ps("cum", [P, E])
        tot = ps("tot", [P, E])

        const_in, zeroed, ones_ready = sem("const_in"), sem("zeroed"), sem("ones_ready")
        wo_in = [sem(f"wo_in{k}") for k in range(2)]
        wo_hi, wo_lo = sem("wo_hi"), sem("wo_lo")
        ot_in = [sem(f"ot_in{k}") for k in range(2)]
        xr_in = [sem(f"xr_in{k}") for k in range(2)]
        biased, projected, chain, normed = sem("biased"), sem("projected"), sem("chain"), sem("normed")
        var_ready, sd_ready = sem("var_ready"), sem("sd_ready")
        x1_out = [sem(f"x1_out{k}") for k in range(2)]
        turned, copied, routed, topped, exped = sem("turned"), sem("copied"), sem("routed"), sem("topped"), sem("exped")
        masked, summed, placed, scattered, counted = (sem("masked"), sem("summed"), sem("placed"), sem("scattered"),
                                                      sem("counted"))
        tok_ready = sem("tok_ready")

        passed = sem("passed")
        block = ctx.enter_context(nc.Block())

        def load_block(sp, b, k):
            sp.dma_start(ot[k][:].bitcast(F32), o_d[bass.ds(b, 1)].rearrange("o p j g h t -> (o p) (j g) h t")).then_inc(ot_in[k], 16)
            sp.dma_start(xr[k][:], x[bass.ds(b * P, P), :]).then_inc(xr_in[k], 16)

        @block.sync
        def _(sp):
            for n in range(2):
                sp.dma_start(wo_raw[n][:], wo[:, n * 4:(n + 1) * 4, :]).then_inc(wo_in[n], 16)
            sp.dma_start(ident[:], ident_d).then_inc(const_in, 16)
            sp.dma_start(lower[:], lower_d).then_inc(const_in, 16)
            sp.dma_start(bo_b[:], bo.partition_broadcast(P)).then_inc(const_in, 16)
            sp.dma_start(rwT[:], rw).then_inc(const_in, 16)
            for k in range(2):
                load_block(sp, k, k)
            for n in range(2, PARTS):
                sp.wait_ge(wo_lo, n - 1)
                sp.dma_start(wo_raw[n % 2][:], wo[:, n * 4:(n + 1) * 4, :]).then_inc(wo_in[n % 2], 16)
            sp.wait_ge(zeroed, 1)
            sp.dma_start(slot_d.rearrange("(p s) o -> p (s o)", p=P), zero[:]).then_inc(zeroed, 16)

            def step(i, last=False):
                for k in range(2):
                    b = i * 2 + k
                    if not last:
                        sp.wait_ge(projected, b + 1)
                        sp.wait_ge(biased, b + 1)
                        load_block(sp, b + 2, k)
                    sp.wait_ge(normed, b + 1)
                    sp.dma_start(x1_d[bass.ds(b * P, P), :], x1[k][:]).then_inc(x1_out[k], 16)

            with sp.Fori(0, NB // 2 - 1) as i:
                step(i)
            step(NB // 2 - 1, last=True)
            for k in range(2):
                sp.wait_ge(x1_out[k], 16 * (NB // 2))

        @block.tensor
        def _(pe):
            pe.wait_ge(wo_lo, PARTS)
            pe.wait_ge(const_in, 64)
            pe.wait_ge(ones_ready, 1)

            def project(b, k, i, early):
                pe.wait_ge(ot_in[k], i * 16 + 16)
                if not early:
                    pe.wait_ge(normed, b - 1)
                for n in range(H):
                    for m, (a, w) in enumerate(split3([ot[k][:, n, s, :] for s in (HI, LO)],
                                                      [wo_s[s][:, n, :] for s in (HI, LO)])):
                        mm = nc.tensor.matmul(acc[k][:], a, w, start=(n == 0 and m == 0), stop=(n == H - 1 and m == 2))
                mm.then_inc(projected, 1)

            def route(b, k, early):
                pe.wait_ge(normed, b + 1)
                if not early:
                    pe.wait_ge(copied, b)
                for c in range(NC):
                    mm = nc.tensor.transpose(xtp[:, c, :], x1[k][:, c * P:(c + 1) * P], ident[:])
                mm.then_inc(turned, 1)
                pe.wait_ge(copied, b + 1)
                if not early:
                    pe.wait_ge(topped, b)
                for c in range(NC):
                    mm = nc.tensor.matmul(lg[:], x1T[:, c, :], rwT[:, c, :], start=(c == 0), stop=(c == NC - 1))
                mm.then_inc(routed, 1)
                pe.wait_ge(masked, b + 1)
                if not early:
                    pe.wait_ge(counted, b)
                nc.tensor.matmul(cum[:], lower[:], mask[:], start=True, stop=True)
                nc.tensor.matmul(tot[:], ones[:], mask[:], start=True, stop=True).then_inc(summed, 1)

            project(0, 0, 0, True)
            project(1, 1, 0, True)
            route(0, 0, True)
            with pe.Fori(1, NB // 2) as i:
                project(i * 2, 0, i, False)
                route(i * 2 - 1, 1, False)
                project(i * 2 + 1, 1, i, False)
                route(i * 2, 0, False)
            route(NB - 1, 1, False)

        @block.scalar
        def _(act):
            for n in range(PARTS):
                act.wait_ge(wo_in[n % 2], 16 * (n // 2 + 1))
                nc.scalar.copy(wo_s[HI][:, n * 4:(n + 1) * 4, :], wo_raw[n % 2][:]).then_inc(wo_hi, 1)

            def step(i, first):
                for k in range(2):
                    b = i * 2 + k
                    act.wait_ge(var_ready, b + 1)
                    nc.scalar.activation(sd[:], mv[:, 1:2], ACT.Sqrt, bias=eps[:]).then_inc(sd_ready, 1)
                    act.wait_ge(turned, b + 1)
                    if not (first and k == 0):
                        act.wait_ge(routed, b)
                    nc.scalar.copy(x1T[:], xtp[:]).then_inc(copied, 1)
                    act.wait_ge(topped, b + 1)
                    nc.scalar.activation(et[:], top[:], ACT.Exp, bias=ntop[:], accum_out=esum[:]).then_inc(exped, 1)

            loop(act, NB // 2, step)

        @block.vector
        def _(dve):
            nc.vector.memset(zero[:], 0).then_inc(zeroed, 1)
            nc.vector.memset(ones[:], 1.0).then_inc(ones_ready, 1)
            nc.vector.memset(eps[:], EPS)
            nc.vector.memset(count[:], 0.0)
            for n in range(PARTS):
                dve.wait_ge(wo_hi, n + 1)
                nc.vector.tensor_tensor(wo_s[LO][:, n * 4:(n + 1) * 4, :], wo_raw[n % 2][:],
                                        wo_s[HI][:, n * 4:(n + 1) * 4, :].bitcast(F32), ALU.subtract).then_inc(wo_lo, 1)
            dve.wait_ge(tok_ready, 1)
            STEPS = 17

            def step(i, first):
                for k in range(2):
                    b = i * 2 + k
                    at = [0]

                    def link(ins):
                        at[0] += 1
                        ins.then_inc(chain, 1)
                        wait_alone(dve, passed, chain, b * STEPS + at[0])

                    dve.wait_ge(projected, b + 1)
                    dve.wait_ge(biased, b + 1)
                    link(nc.vector.tensor_tensor(h[k][:], acc[k][:], xb[k][:], ALU.add))
                    link(nc.vector.bn_stats(st[:], h[k][:]))
                    nc.vector.bn_aggr(mv[:], st[:]).then_inc(var_ready, 1)
                    dve.wait_ge(sd_ready, b + 1)
                    link(nc.vector.reciprocal(rstd[:], sd[:]))
                    if not first:
                        dve.wait_ge(x1_out[k], i * 16)
                    nc.vector.tensor_scalar(x1[k][:], h[k][:], mv[:, 0:1], rstd[:], ALU.subtract, ALU.mult
                                            ).then_inc(normed, 1)
                    wait_alone(dve, passed, routed, b + 1)
                    link(nc.vector.max(top[:], lg[:]))
                    nc.vector.max_index(topi[:], top[:], lg[:]).then_inc(chain, 1)
                    nc.vector.tensor_scalar(ntop[:], top[:, 0:1], -1.0, None, ALU.mult).then_inc(topped, 1)
                    at[0] += 1
                    dve.wait_ge(chain, b * STEPS + at[0])
                    link(nc.vector.tensor_copy(topf[:], topi[:]))
                    link(nc.vector.tensor_tensor(hot[:], iota_e[:].unsqueeze(1).to_broadcast([P, TOPK, E]),
                                                 topf[:].unsqueeze(2).to_broadcast([P, TOPK, E]), ALU.is_equal))
                    if not (first and k == 0):
                        dve.wait_ge(summed, b)
                    nc.vector.tensor_reduce(mask[:], hot[:].rearrange("p k e -> p e k"), AX_X, ALU.add).then_inc(masked, 1)
                    dve.wait_ge(exped, b + 1)
                    link(nc.vector.reciprocal(einv[:], esum[:]))
                    link(nc.vector.tensor_scalar(wk[:], et[:], einv[:], None, ALU.mult))
                    dve.wait_ge(summed, b + 1)
                    link(nc.vector.tensor_tensor(posn[:], cum[:], count[:], ALU.add))
                    nc.vector.tensor_tensor(count[:], tot[:], count[:], ALU.add).then_inc(counted, 1)
                    link(nc.vector.tensor_tensor(pick[:], hot[:], posn[:].unsqueeze(1).to_broadcast([P, TOPK, E]), ALU.mult))
                    link(nc.vector.tensor_reduce(pos[:], pick[:], AX_X, ALU.add))
                    link(nc.vector.tensor_scalar(over[:], pos[:], float(CAP), float(2 * SLOTS), ALU.is_ge, ALU.mult))
                    link(nc.vector.tensor_scalar(slot[:], topf[:], float(CAP), None, ALU.mult))
                    link(nc.vector.tensor_tensor(slot[:], slot[:], pos[:], ALU.add))
                    link(nc.vector.tensor_scalar(keep[:], pos[:], float(CAP), None, ALU.is_lt))
                    nc.vector.tensor_tensor(wcomb[:, bass.ds(b, 1), :].rearrange("p o k -> p (o k)"), wk[:], keep[:], ALU.mult)
                    link(nc.vector.tensor_tensor(slot_out[:], slot[:], over[:], ALU.add))
                    nc.vector.tensor_tensor(comb[:, bass.ds(b, 1), :].rearrange("p o k -> p (o k)"), slot[:], keep[:],
                                            ALU.mult)
                    if not first:
                        dve.wait_ge(scattered, i * (32 * TOPK) + (16 * TOPK * k))
                    elif k == 1:
                        pass
                    nc.vector.tensor_copy(slot_i[k][:], slot_out[:]).then_inc(placed, 1)
                    assert at[0] == STEPS

            loop(dve, NB // 2, step)

        @block.gpsimd
        def _(pool):
            nc.gpsimd.iota(iota_e[:], [[1, E]], base=0, channel_multiplier=0, allow_small_or_imprecise_dtypes=True)
            nc.gpsimd.iota(tok[:], [[0, 1]], base=0, channel_multiplier=1).then_inc(tok_ready, 1)
            pool.wait_ge(const_in, 64)
            pool.wait_ge(zeroed, 17)

            def step(i, first):
                for k in range(2):
                    b = i * 2 + k
                    pool.wait_ge(xr_in[k], i * 16 + 16)
                    if not first:
                        pool.wait_ge(normed, b - 1)
                    nc.gpsimd.tensor_tensor(xb[k][:], xr[k][:], bo_b[:], ALU.add).then_inc(biased, 1)
                    wait_alone(pool, passed, placed, b + 1)
                    for n in range(TOPK):
                        nc.gpsimd.indirect_dma_start(
                            out=slot_d, out_offset=bass.IndirectOffsetOnAxis(ap=slot_i[k][:, n:n + 1], axis=0),
                            in_=tok[:], in_offset=None, bounds_check=SLOTS - 1, oob_is_err=False
                        ).then_inc(scattered, 16)
                    wait_alone(pool, passed, scattered, b * (16 * TOPK) + 16 * TOPK)
                    nc.gpsimd.tensor_scalar(tok[:], tok[:], float(P), None, ALU.add).then_inc(tok_ready, 1)
                    pool.wait_ge(tok_ready, b + 2)

            loop(pool, NB // 2, step)


def stage_experts(nc, gu, dn, ident_d, slot_d, x1_d, y_d):
    PAIRS = E // 2
    GU = 3 * P
    with ExitStack() as ctx:
        def sb(name, shape, dt=F32):
            return ctx.enter_context(nc.sbuf_tensor("p4_" + name, shape, dt))

        def ps(name, shape):
            return ctx.enter_context(nc.psum_tensor("p4_" + name, shape, F32))

        def sem(name):
            return ctx.enter_context(nc.semaphore("p4_" + name))

        WCOLS = NC * GU + C
        ident = sb("ident", [P, P])
        table_i = sb("table_i", [P, P], I32)
        table_f = sb("table_f", [P, P])
        tableT = sb("tableT", [P, E, CH], U32)
        w_raw = [sb(f"w_raw{k}", [P, WCOLS]) for k in range(2)]
        t_raw = sb("t_raw", [P, C])
        w_s = [[sb(f"w{k}{s}", [P, WCOLS], F32R) for s in "hl"] for k in range(2)]
        t_s = [sb(f"t{s}", [P, C], F32R) for s in "hl"]
        idx = [sb(f"idx{k}", [P, CH], U32) for k in range(2)]
        xg = [[sb(f"xg{k}{c}", [P, C]) for c in range(CH)] for k in range(2)]
        xT = [sb(f"xT{s}", [P, NC, CAP], F32R) for s in "hl"]
        sg, sgt = sb("sg", [P, CAP]), sb("sgt", [P, CAP])
        h = sb("h", [P, 2, CAP])
        h_s = [sb(f"h{s}", [P, 2, CAP], F32R) for s in "hl"]
        y = [[sb(f"y{k}{c}", [P, C]) for c in range(CH)] for k in range(2)]

        tp = [ps(f"tp{c}", [P, NC, P]) for c in range(CH)]
        pgu = ps("pgu", [P, 2, CAP])
        prest = ps("prest", [P, CAP])
        py = [ps(f"py{c}", [P, C]) for c in range(CH)]

        const_in, table_ready, idx_ready = sem("const_in"), sem("table_ready"), sem("idx_ready")
        w_in = [sem(f"w_in{k}") for k in range(2)]
        t_in = sem("t_in")
        x_in = [[sem(f"x_in{k}{c}") for c in range(CH)] for k in range(2)]
        gu_hi, gu_lo, dn_hi, dn_lo = sem("gu_hi"), sem("gu_lo"), sem("dn_hi"), sem("dn_lo")
        t_hi, t_lo = sem("t_hi"), sem("t_lo")
        turned, x_hi, x_lo = sem("turned"), sem("x_hi"), sem("x_lo")
        gated, silued, rest_silued, h_main, h_rest = (sem("gated"), sem("silued"), sem("rest_silued"), sem("h_main"),
                                                      sem("h_rest"))
        h_part, h_split = sem("h_part"), sem("h_split")
        downed, y_a, y_b = sem("downed"), sem("y_a"), sem("y_b")
        y_out = [[sem(f"y_out{k}{c}") for c in range(CH)] for k in range(2)]
        passed = sem("passed")

        GUC, DNC = slice(0, NC * GU), slice(NC * GU, WCOLS)

        def rest(k):
            half = slice(k * IT, (k + 1) * IT)
            return half, slice((1 - k) * IT, (2 - k) * IT)

        def ahead(i, k, n):
            return i + (k + n) // 2, (k + n) % 2

        def first(i):
            return isinstance(i, int) and i == 0

        def exists(i):
            return not isinstance(i, int) or i < PAIRS

        def steps(eng, step):
            for k in range(2):
                step(0, k)
            with eng.Fori(1, PAIRS - 2) as i:
                for k in range(2):
                    step(i, k)
            for i in (PAIRS - 2, PAIRS - 1):
                for k in range(2):
                    step(i, k)

        block = ctx.enter_context(nc.Block())

        @block.sync
        def _(sp):
            def load_w(i, k):
                if not first(i):
                    sp.wait_ge(gu_lo, i * 2 + (k - 1))
                    sp.wait_ge(dn_lo, i * 2 + (k - 1))
                sp.dma_start(w_raw[k][:], gu[bass.ds(i * 2 + k, 1)].rearrange("o p n -> (o p) n")).then_inc(w_in[k], 16)

            def load_t(i):
                if not first(i):
                    sp.wait_ge(t_lo, i)
                sp.dma_start(t_raw[:], dn[bass.ds(i, 1)].rearrange("o p n -> (o p) n")).then_inc(t_in, 16)

            def step(i, k):
                e = i * 2 + k
                for c, done in ((0, y_a), (1, y_b)):
                    sp.wait_ge(done, e + 1)
                    sp.dma_start(y_d[bass.ds(e * CAP + c * P, P), :], y[k][c][:]).then_inc(y_out[k][c], 16)
                if exists(i + 2):
                    load_w(i + 2, k)
                if k == 0 and exists(i + 1):
                    load_t(i + 1)

            sp.dma_start(table_i[:], slot_d.rearrange("(p s) o -> p (s o)", p=P)).then_inc(const_in, 16)
            sp.dma_start(ident[:], ident_d).then_inc(const_in, 16)
            load_w(0, 0)
            load_w(0, 1)
            load_t(0)
            load_w(1, 0)
            load_w(1, 1)
            steps(sp, step)
            for k in range(2):
                for c in range(CH):
                    sp.wait_ge(y_out[k][c], 16 * PAIRS)

        @block.tensor
        def _(pe):
            def turn(i, k):
                for c in range(CH):
                    pe.wait_ge(x_in[k][c], i * 16 + 16)
                    if not (first(i) and k == 0):
                        pe.wait_ge(x_lo, (i * 2 + k) * CH + (c - CH + 1))
                    for d in range(NC):
                        mm = nc.tensor.transpose(tp[c][:, d, :], xg[k][c][:, d * P:(d + 1) * P], ident[:])
                    mm.then_inc(turned, 1)

            def gate_up(i, k):
                e = i * 2 + k
                pe.wait_ge(x_lo, e * CH + CH)
                pe.wait_ge(gu_lo, e + 1)
                if not (first(i) and k == 0):
                    pe.wait_ge(h_rest, e)
                for f, out in enumerate((pgu[:, 0, :], pgu[:, 1, :], prest[:])):
                    for m, (a, b) in enumerate(split3(w_s[k], xT)):
                        for d in range(NC):
                            col = d * GU + f * P
                            mm = nc.tensor.matmul(out, a[:, col:col + P], b[:, d, :], start=(m == 0 and d == 0),
                                                  stop=(m == 2 and d == NC - 1))
                mm.then_inc(gated, 1)

            def down(i, k):
                e = i * 2 + k
                half, _ = rest(k)
                pe.wait_ge(h_split, e + 1)
                pe.wait_ge(dn_lo, e + 1)
                if k == 0:
                    pe.wait_ge(t_lo, i + 1)
                if not (first(i) and k == 0):
                    pe.wait_ge(y_a, e)
                    pe.wait_ge(y_b, e)
                for c in range(CH):
                    cols = slice(c * P, (c + 1) * P)
                    for m, (a, b) in enumerate(split3(h_s, w_s[k])):
                        nc.tensor.matmul(py[c][:], a[:, 0, cols], b[:, DNC], start=(m == 0), stop=False)
                    for m, (a, b) in enumerate(split3(h_s, t_s)):
                        mm = nc.tensor.matmul(py[c][:], a[half, 1, cols], b[half, :], start=False, stop=(m == 2))
                mm.then_inc(downed, 1)

            def step(i, k):
                for f, n in ((gate_up, 1), (turn, 2), (down, 0)):
                    if exists(ahead(i, k, n)[0]):
                        f(*ahead(i, k, n))

            pe.wait_ge(const_in, 32)
            pe.wait_ge(table_ready, 1)
            nc.tensor.transpose(tp[0][:, 0, :], table_f[:], ident[:]).then_inc(table_ready, 1)
            pe.wait_ge(table_ready, 3)
            turn(0, 0)
            gate_up(0, 0)
            turn(0, 1)
            steps(pe, step)

        @block.scalar
        def _(act):
            def gate_up_hi(i, k):
                act.wait_ge(w_in[k], i * 16 + 16)
                if not first(i):
                    act.wait_ge(gated, i * 2 + (k - 1))
                nc.scalar.copy(w_s[k][HI][:, GUC], w_raw[k][:, GUC]).then_inc(gu_hi, 1)

            def down_hi(i, k):
                act.wait_ge(w_in[k], i * 16 + 16)
                if not first(i):
                    act.wait_ge(downed, i * 2 + (k - 1))
                nc.scalar.copy(w_s[k][HI][:, DNC], w_raw[k][:, DNC]).then_inc(dn_hi, 1)

            def rests_hi(i):
                act.wait_ge(t_in, i * 16 + 16)
                if not first(i):
                    act.wait_ge(downed, i * 2)
                nc.scalar.copy(t_s[HI][:], t_raw[:]).then_inc(t_hi, 1)

            def turn_hi(i, k):
                e = i * 2 + k
                for c in range(CH):
                    act.wait_ge(turned, e * CH + (c + 1))
                    if not (first(i) and k == 0):
                        act.wait_ge(gated, e)
                    nc.scalar.copy(xT[HI][:, :, c * P:(c + 1) * P], tp[c][:]).then_inc(x_hi, 1)

            def silu(i, k):
                e = i * 2 + k
                half, other = rest(k)
                act.wait_ge(gated, e + 1)
                if not (first(i) and k == 0):
                    act.wait_ge(h_rest, e)
                nc.scalar.activation(sg[:], pgu[:, 0, :], ACT.Silu).then_inc(silued, 1)
                nc.scalar.activation(sgt[half, :], prest[other, :], ACT.Silu).then_inc(rest_silued, 1)

            def rows(i, k):
                act.wait_ge(downed, i * 2 + (k + 1))
                if not first(i):
                    act.wait_ge(y_out[k][0], i * 16)
                nc.scalar.copy(y[k][0][:], py[0][:]).then_inc(y_a, 1)

            def step(i, k):
                for f, n in ((silu, 1), (turn_hi, 2), (gate_up_hi, 3), (rows, 0), (down_hi, 2)):
                    if exists(ahead(i, k, n)[0]):
                        f(*ahead(i, k, n))
                if k == 1 and exists(i + 1):
                    rests_hi(i + 1)

            turn_hi(0, 0)
            gate_up_hi(0, 0)
            turn_hi(0, 1)
            gate_up_hi(0, 1)
            down_hi(0, 0)
            down_hi(0, 1)
            rests_hi(0)
            silu(0, 0)
            gate_up_hi(1, 0)
            steps(act, step)

        @block.vector
        def _(dve):
            def gate_up_lo(i, k):
                dve.wait_ge(gu_hi, i * 2 + (k + 1))
                nc.vector.tensor_tensor(w_s[k][LO][:, GUC], w_raw[k][:, GUC], w_s[k][HI][:, GUC].bitcast(F32), ALU.subtract
                                        ).then_inc(gu_lo, 1)

            def down_lo(i, k):
                dve.wait_ge(dn_hi, i * 2 + (k + 1))
                nc.vector.tensor_tensor(w_s[k][LO][:, DNC], w_raw[k][:, DNC], w_s[k][HI][:, DNC].bitcast(F32), ALU.subtract
                                        ).then_inc(dn_lo, 1)

            def rests_lo(i):
                dve.wait_ge(t_hi, i + 1)
                nc.vector.tensor_tensor(t_s[LO][:], t_raw[:], t_s[HI][:].bitcast(F32), ALU.subtract).then_inc(t_lo, 1)

            def turn_lo(i, k):
                for c in range(CH):
                    dve.wait_ge(x_hi, (i * 2 + k) * CH + (c + 1))
                    cols = slice(c * P, (c + 1) * P)
                    nc.vector.tensor_tensor(xT[LO][:, :, cols], tp[c][:], xT[HI][:, :, cols].bitcast(F32), ALU.subtract
                                            ).then_inc(x_lo, 1)

            def gate(i, k):
                e = i * 2 + k
                half, _ = rest(k)
                dve.wait_ge(silued, e + 1)
                if not (first(i) and k == 0):
                    dve.wait_ge(h_split, e)
                nc.vector.tensor_tensor(h[:, 0, :], pgu[:, 1, :], sg[:], ALU.mult).then_inc(h_main, 1)
                dve.wait_ge(rest_silued, e + 1)
                nc.vector.tensor_tensor(h[half, 1, :], prest[half, :], sgt[half, :], ALU.mult).then_inc(h_rest, 1)

            def rows(i, k):
                dve.wait_ge(downed, i * 2 + (k + 1))
                if not first(i):
                    dve.wait_ge(y_out[k][1], i * 16)
                nc.vector.tensor_copy(y[k][1][:], py[1][:]).then_inc(y_b, 1)

            def step(i, k):
                for f, n in ((gate, 1), (turn_lo, 2), (gate_up_lo, 3), (rows, 0), (down_lo, 2)):
                    if exists(ahead(i, k, n)[0]):
                        f(*ahead(i, k, n))
                if k == 1 and exists(i + 1):
                    rests_lo(i + 1)

            nc.vector.memset(h[:], 0.0)
            dve.wait_ge(const_in, 32)
            nc.vector.tensor_copy(table_f[:], table_i[:]).then_inc(table_ready, 1)
            dve.wait_ge(table_ready, 2)
            nc.vector.tensor_copy(tableT[:].rearrange("p e c -> p (e c)"), tp[0][:, 0, :]).then_inc(table_ready, 1)
            turn_lo(0, 0)
            gate_up_lo(0, 0)
            turn_lo(0, 1)
            gate_up_lo(0, 1)
            down_lo(0, 0)
            down_lo(0, 1)
            rests_lo(0)
            gate(0, 0)
            gate_up_lo(1, 0)
            steps(dve, step)

        @block.gpsimd
        def _(pool):
            def gather(i, k):
                e = i * 2 + k
                if not first(i):
                    pool.wait_ge(turned, e * CH - CH)
                nc.gpsimd.tensor_copy(idx[k][:], tableT[:, bass.ds(e, 1), :].rearrange("p o c -> p (o c)")
                                      ).then_inc(idx_ready, 1)
                wait_alone(pool, passed, idx_ready, e + 1)
                for c in range(CH):
                    nc.gpsimd.indirect_dma_start(
                        out=xg[k][c][:], out_offset=None, in_=x1_d,
                        in_offset=bass.IndirectOffsetOnAxis(ap=idx[k][:, c:c + 1], axis=0)).then_inc(x_in[k][c], 16)

            def split_h(i, k):
                e = i * 2 + k
                if not (first(i) and k == 0):
                    pool.wait_ge(downed, e)
                pool.wait_ge(h_main, e + 1)
                wait_alone(pool, passed, h_rest, e + 1)
                nc.gpsimd.tensor_scalar(h_s[HI][:], h[:], 1.0, 1.0, ALU.mult, ALU.mult).then_inc(h_part, 1)
                wait_alone(pool, passed, h_part, e + 1)
                nc.gpsimd.tensor_tensor(h_s[LO][:], h[:], h_s[HI][:].bitcast(F32), ALU.subtract).then_inc(h_split, 1)

            def step(i, k):
                for f, n in ((split_h, 1), (gather, 4)):
                    if exists(ahead(i, k, n)[0]):
                        f(*ahead(i, k, n))

            pool.wait_ge(table_ready, 3)
            gather(0, 0)
            gather(0, 1)
            gather(1, 0)
            split_h(0, 0)
            gather(1, 1)
            steps(pool, step)


def stage_combine(nc, x1_d, y_d, comb, wcomb, out):
    with ExitStack() as ctx:
        def sb(name, shape, dt=F32):
            return ctx.enter_context(nc.sbuf_tensor("p5_" + name, shape, dt))

        def sem(name):
            return ctx.enter_context(nc.semaphore("p5_" + name))

        eps = sb("eps", [P, 1])
        x1 = [sb(f"x1{k}", [P, C]) for k in range(2)]
        idx = [sb(f"idx{k}", [P, TOPK], U32) for k in range(2)]
        rows = [[sb(f"rows{k}{n}", [P, C]) for n in range(TOPK)] for k in range(2)]
        acc = [[sb(f"acc{k}{n}", [P, C]) for n in range(2)] for k in range(2)]
        st, mv = sb("st", [P, 6]), sb("mv", [P, 2])
        sd, rstd = sb("sd", [P, 1]), sb("rstd", [P, 1])
        res = [sb(f"res{k}", [P, C]) for k in range(2)]

        x1_in = [sem(f"x1_in{k}") for k in range(2)]
        rows_in = [[sem(f"rows_in{k}{n}") for n in range(TOPK)] for k in range(2)]
        res_out = [sem(f"res_out{k}") for k in range(2)]
        indexed, chain, summed, var_ready, sd_ready, normed, eps_ready = (
            sem("indexed"), sem("chain"), sem("summed"), sem("var_ready"), sem("sd_ready"), sem("normed"), sem("eps_ready"))

        passed = sem("passed")
        block = ctx.enter_context(nc.Block())

        @block.sync
        def _(sp):
            for k in range(2):
                sp.dma_start(x1[k][:], x1_d[k * P:(k + 1) * P, :]).then_inc(x1_in[k], 16)

            def step(i, last=False):
                for k in range(2):
                    b = i * 2 + k
                    if not last:
                        sp.wait_ge(summed, b + 1)
                        sp.dma_start(x1[k][:], x1_d[bass.ds((b + 2) * P, P), :]).then_inc(x1_in[k], 16)
                    sp.wait_ge(normed, b + 1)
                    sp.dma_start(out[bass.ds(b * P, P), :], res[k][:]).then_inc(res_out[k], 16)

            with sp.Fori(0, NB // 2 - 1) as i:
                step(i)
            step(NB // 2 - 1, last=True)
            for k in range(2):
                sp.wait_ge(res_out[k], 16 * (NB // 2))

        @block.gpsimd
        def _(pool):
            def step(i, first):
                for k in range(2):
                    b = i * 2 + k
                    if not first:
                        pool.wait_ge(summed, b - 1)
                    nc.gpsimd.tensor_copy(idx[k][:], comb[:, bass.ds(b, 1), :].rearrange("p o k -> p (o k)")
                                          ).then_inc(indexed, 1)
                    wait_alone(pool, passed, indexed, b + 1)
                    for n in range(TOPK):
                        nc.gpsimd.indirect_dma_start(
                            out=rows[k][n][:], out_offset=None, in_=y_d,
                            in_offset=bass.IndirectOffsetOnAxis(ap=idx[k][:, n:n + 1], axis=0)).then_inc(rows_in[k][n], 16)

            loop(pool, NB // 2, step)

        @block.vector
        def _(dve):
            nc.vector.memset(eps[:], EPS).then_inc(eps_ready, 1)
            STEPS = TOPK + 1

            def step(i, first):
                for k in range(2):
                    b = i * 2 + k
                    dve.wait_ge(x1_in[k], i * 16 + 16)
                    for n in range(TOPK):
                        dve.wait_ge(rows_in[k][n], i * 16 + 16)
                        src = x1[k] if n == 0 else acc[k][(n - 1) % 2]
                        ins = nc.vector.scalar_tensor_tensor(
                            acc[k][n % 2][:], rows[k][n][:], wcomb[:, bass.ds(b, 1), n:n + 1].rearrange("p o k -> p (o k)"),
                            src[:], ALU.mult, ALU.add)
                        ins.then_inc(chain if n < TOPK - 1 else summed, 1)
                        if n < TOPK - 1:
                            dve.wait_ge(chain, b * STEPS + n + 1)
                        else:
                            dve.wait_ge(summed, b + 1)
                    total = acc[k][(TOPK - 1) % 2]
                    nc.vector.bn_stats(st[:], total[:]).then_inc(chain, 1)
                    wait_alone(dve, passed, chain, b * STEPS + TOPK)
                    nc.vector.bn_aggr(mv[:], st[:]).then_inc(var_ready, 1)
                    dve.wait_ge(sd_ready, b + 1)
                    nc.vector.reciprocal(rstd[:], sd[:]).then_inc(chain, 1)
                    dve.wait_ge(chain, b * STEPS + TOPK + 1)
                    if not first:
                        dve.wait_ge(res_out[k], i * 16)
                    nc.vector.tensor_scalar(res[k][:], total[:], mv[:, 0:1], rstd[:], ALU.subtract, ALU.mult
                                            ).then_inc(normed, 1)

            loop(dve, NB // 2, step)

        @block.scalar
        def _(act):
            act.wait_ge(eps_ready, 1)

            def step(i, first):
                for k in range(2):
                    act.wait_ge(var_ready, i * 2 + k + 1)
                    nc.scalar.activation(sd[:], mv[:, 1:2], ACT.Sqrt, bias=eps[:]).then_inc(sd_ready, 1)

            loop(act, NB // 2, step)


def build(nc, x, wqk, bqk, wv, bv, cos, sin, ident, mask, lower, wo, bo, rw, gu, dn, out):
    qk_d = nc.dram_tensor("qk_scratch", [H + HKV, HD, NT, 2, 512], F32, kind="Internal").ap()
    v_d = nc.dram_tensor("v_scratch", [NB, HKV, P, 2, HD], F32, kind="Internal").ap()
    o_d = nc.dram_tensor("o_scratch", [NB, HD, HKV, G, 2, P], F32, kind="Internal").ap()
    x1_d = nc.dram_tensor("x1_scratch", [T, C], F32, kind="Internal").ap()
    slot_d = nc.dram_tensor("slot_scratch", [SLOTS, 1], I32, kind="Internal").ap()
    y_d = nc.dram_tensor("y_scratch", [SLOTS, C], F32, kind="Internal").ap()
    with ExitStack() as ctx:
        comb = ctx.enter_context(nc.sbuf_tensor("comb", [P, NB, TOPK], F32))
        wcomb = ctx.enter_context(nc.sbuf_tensor("wcomb", [P, NB, TOPK], F32))
        stage_project(nc, x, wqk, bqk, wv, bv, cos, sin, ident, qk_d, v_d)
        stage_attend(nc, ident, mask, qk_d, v_d, o_d)
        stage_route(nc, x, wo, bo, rw, ident, lower, o_d, x1_d, slot_d, comb, wcomb)
        stage_experts(nc, gu, dn, ident, slot_d, x1_d, y_d)
        stage_combine(nc, x1_d, y_d, comb, wcomb, out)


def constants():
    theta = (1.0 / 10000.0 ** (np.arange(0, HD, 2, dtype=np.float32) / np.float32(HD))).astype(np.float32)
    freqs = (np.arange(T, dtype=np.float32)[:, None] * theta[None, :]).astype(np.float32)
    root = np.float32((1.0 / np.sqrt(H)) ** 0.5)
    cos, sin = (np.cos(freqs) * root).T, (np.sin(freqs) * root).T
    cos = np.concatenate([cos, cos]).astype(np.float32)
    sin = np.concatenate([sin, -sin]).astype(np.float32)
    row, col = np.arange(P)[:, None], np.arange(P)[None, :]
    mask = np.where(col <= row, 0.0, MASKED).astype(np.float32)
    lower = (row < col).astype(np.float32)
    return {"cos": cos, "sin": sin, "ident": np.eye(P, dtype=np.float32), "mask": mask, "lower": lower}


def layout(a):
    x, Wq, bq, Wk, bk, Wv, bv, Wo, bo, rw, gu, dn = a
    wq = Wq.reshape(NC, P, G, HKV, HD // 2, 2).transpose(3, 2, 1, 0, 5, 4).reshape(H, P, NC * HD)
    wk = Wk.reshape(NC, P, HKV, HD // 2, 2).transpose(2, 1, 0, 4, 3).reshape(HKV, P, NC * HD)
    bqh = bq.reshape(G, HKV, HD // 2, 2).transpose(1, 0, 3, 2).reshape(H, HD)
    bkh = bk.reshape(HKV, HD // 2, 2).transpose(0, 2, 1).reshape(HKV, HD)
    wo = Wo.reshape(G, HKV, HD, C).transpose(2, 1, 0, 3).reshape(HD, H, C)
    g, u = gu[:, :, :I], gu[:, :, I:]
    rest = np.concatenate([u[:, :, P:], g[:, :, P:]], 2)
    rest[1::2] = np.concatenate([g[1::2, :, P:], u[1::2, :, P:]], 2)
    cols = np.concatenate([g[:, :, :P], u[:, :, :P], rest], 2)
    cols = cols.reshape(E, NC, P, 3 * P).transpose(0, 2, 1, 3).reshape(E, P, NC * 3 * P)
    return {
        "x": x.reshape(T, C), "wqk": np.concatenate([wq, wk]), "bqk": np.concatenate([bqh, bkh]).T,
        "wv": Wv.reshape(NC, P, C).transpose(1, 0, 2).reshape(P, NC * C), "bv": bv, "wo": wo, "bo": bo,
        "rw": rw.T.reshape(NC, P, E).transpose(1, 0, 2), "gu": np.concatenate([cols, dn[:, :P, :]], 2),
        "dn": dn[:, P:, :].reshape(E // 2, 2 * IT, C),
    }


_ORDER = ["x", "wqk", "bqk", "wv", "bv", "cos", "sin", "ident", "mask", "lower", "wo", "bo", "rw", "gu", "dn"]
_INS = ["L0_attn_x", "L0_attn_Wq", "L0_attn_bq", "L0_attn_Wk", "L0_attn_bk", "L0_attn_Wv", "L0_attn_bv", "L0_attn_Wo",
        "L0_attn_bo", "L0_ffn_router_weight", "L0_ffn_gate_up_proj", "L0_ffn_down_proj"]


def kernel(**inputs):
    import concourse.bacc as bacc
    from concourse.bass_utils import run_bass_kernel_spmd

    arrays = layout([np.asarray(inputs[n]) for n in _INS]) | constants()
    nc = bacc.Bacc("TRN2", target_bir_lowering=False, num_devices=1)
    feed, args = {}, []
    for name in _ORDER:
        a = np.ascontiguousarray(arrays[name])
        feed[f"in_{name}"] = a
        args.append(nc.dram_tensor(f"in_{name}", a.shape, mybir.dt.from_np(a.dtype), kind="ExternalInput").ap())
    out = nc.dram_tensor("out", [T, C], F32, kind="ExternalOutput").ap()
    build(nc, *args, out)
    r = run_bass_kernel_spmd(nc, [feed], core_ids=[0])
    return r.results[0]["out"].reshape(1, T, C)
```

```python
from contextlib import ExitStack

import numpy as np

import concourse.bass as bass
from concourse import mybir

F32 = mybir.dt.float32
F32R = mybir.dt.float32r
BF16 = mybir.dt.bfloat16
I32 = mybir.dt.int32
U32 = mybir.dt.uint32
ALU = mybir.AluOpType
ACT = mybir.ActivationFunctionType
AX_X = mybir.AxisListType.X

P = 128
T = 2048
C = 512
H, HKV, HD = 16, 4, 128
G = H // HKV
E, TOPK, CAP = 64, 8, 256
I = 192
IT = I - P
NB = T // P
NC = C // P
NT = T // 512
EPS = 1e-5
MASKED = -1.0e30
HI, LO = 0, 1
SLOTS = E * CAP
CH = CAP // P
WO_EARLY = 12


def loop(eng, n, body):
    body(0, True)
    with eng.Fori(1, n) as i:
        body(i, False)


def wait_alone(eng, passed, sem, value):
    eng.wait_ge(sem, value)
    eng.sem_inc(passed, 1)


def split3(a, b):
    return ((a[LO], b[HI]), (a[HI], b[LO]), (a[HI], b[HI]))


def stage_project(nc, passed, x, wqk, wv, bv, cos, sin, ident_d, qk_d, v_d):
    NH = H + HKV
    with ExitStack() as ctx:
        def sb(name, shape, dt=F32):
            return ctx.enter_context(nc.sbuf_tensor("p1_" + name, shape, dt))

        def ps(name, shape):
            return ctx.enter_context(nc.psum_tensor("p1_" + name, shape, F32))

        def sem(name):
            return ctx.enter_context(nc.semaphore("p1_" + name))

        ident = sb("ident", [P, P])
        xraw = [sb(f"xraw{k}", [P, C]) for k in range(2)]
        xt = [[sb(f"xt{k}{s}", [P, NC, P], F32R) for s in "hl"] for k in range(2)]
        xT = [sb(f"xT{s}", [P, NC, T], F32R) for s in "hl"]
        wv_raw = sb("wv_raw", [P, NC * C])
        wv_s = [sb(f"wv{s}", [P, NC * C], F32R) for s in "hl"]
        bv_b = sb("bv_b", [P, C])
        vfull = [sb(f"vfull{k}", [P, C]) for k in range(2)]
        vout = [sb(f"vout{k}", [P, HKV, 2, HD], F32R) for k in range(2)]
        cosT, sinT = sb("cosT", [P, T]), sb("sinT", [P, T])
        w_raw = [sb(f"w_raw{k}", [P, NC * P + 1]) for k in range(2)]
        w_s = [[sb(f"w{k}{s}", [P, NC * P], F32R) for s in "hl"] for k in range(2)]
        qb = [sb(f"qb{k}", [P, 512]) for k in range(2)]
        sw = [sb(f"sw{k}", [P, 512]) for k in range(2)]
        rc = [sb(f"rc{k}", [P, 512]) for k in range(2)]
        rs = [sb(f"rs{k}", [P, 512]) for k in range(2)]
        qr = [sb(f"qr{k}", [P, 512]) for k in range(NT)]
        qout = [sb(f"qout{k}", [P, NT, 2, 512], F32R) for k in range(2)]

        pt = [ps(f"pt{k}", [P, NC, P]) for k in range(2)]
        pv = [ps(f"pv{k}", [P, C]) for k in range(2)]
        pq = [ps(f"pq{k}", [P, 512]) for k in range(NT)]

        x_in = [sem(f"x_in{k}") for k in range(2)]
        ident_in, const_in, wv_in = sem("ident_in"), sem("const_in"), sem("wv_in")
        wv_hi, wv_lo = sem("wv_hi"), sem("wv_lo")
        xt_done, xt_hi, xt_lo = sem("xt_done"), sem("xt_hi"), sem("xt_lo")
        hi_kept, lo_kept = sem("hi_kept"), sem("lo_kept")
        v_mm, v_full, v_hi, v_lo = sem("v_mm"), sem("v_full"), sem("v_hi"), sem("v_lo")
        v_out = [sem(f"v_out{k}") for k in range(2)]
        w_in = [sem(f"w_in{k}") for k in range(2)]
        w_hi, w_lo = sem("w_hi"), sem("w_lo")
        q_mm, q_swap, q_prod = sem("q_mm"), sem("q_swap"), sem("q_prod")
        q_rot, q_hi, q_lo = sem("q_rot"), sem("q_hi"), sem("q_lo")
        q_out = [sem(f"q_out{k}") for k in range(2)]

        block = ctx.enter_context(nc.Block())

        @block.sync
        def _(sp):
            sp.dma_start(ident[:], ident_d).then_inc(ident_in, 16)
            for k in range(2):
                sp.dma_start(xraw[k][:], x[k * P:(k + 1) * P, :]).then_inc(x_in[k], 16)
            sp.dma_start(wv_raw[:], wv).then_inc(wv_in, 16)
            sp.dma_start(bv_b[:], bv.partition_broadcast(P)).then_inc(wv_in, 16)

            def load_x(tb, k):
                sp.wait_ge(xt_done, tb - 1)
                sp.dma_start(xraw[k][:], x[bass.ds(tb * P, P), :]).then_inc(x_in[k], 16)

            def store_v(tb, k):
                sp.wait_ge(v_lo, tb + 1)
                sp.dma_start(v_d[bass.ds(tb, 1)].rearrange("o j p h d -> p (o j) h d"),
                             vout[k][:].bitcast(F32)).then_inc(v_out[k], 16)

            for k in range(2):
                load_x(2 + k, k)
            for k in range(2):
                sp.dma_start(w_raw[k][:], wqk[k]).then_inc(w_in[k], 16)
            sp.dma_start(cosT[:], cos).then_inc(const_in, 16)
            sp.dma_start(sinT[:], sin).then_inc(const_in, 16)
            with sp.Fori(2, NB // 2) as i:
                for k in range(2):
                    load_x(i * 2 + k, k)
                    store_v(i * 2 + (k - 4), k)
            for tb in range(NB - 4, NB):
                store_v(tb, tb % 2)

            def head_step(i, first, last=False):
                for k in range(2):
                    n = i * 2 + k
                    if not last:
                        sp.wait_ge(w_lo, n + 1)
                        sp.wait_ge(q_swap, n * NT + NT)
                        sp.dma_start(w_raw[k][:], wqk[bass.ds(n + 2, 1)].rearrange("o p m -> (o p) m")
                                     ).then_inc(w_in[k], 16)
                    sp.wait_ge(q_lo, n * NT + NT)
                    sp.dma_start(qk_d[bass.ds(n, 1)].rearrange("o p c h t -> (o p) c h t"),
                                 qout[k][:].bitcast(F32)).then_inc(q_out[k], 16)

            with sp.Fori(0, NH // 2 - 1) as i:
                head_step(i, False)
            head_step(NH // 2 - 1, False, last=True)
            for k in range(2):
                sp.wait_ge(v_out[k], 16 * (NB // 2))
                sp.wait_ge(q_out[k], 16 * (NH // 2))

        @block.tensor
        def _(pe):
            def transposes(tb, k, i, early):
                pe.wait_ge(x_in[k], i * 16 + 16)
                if not early:
                    pe.wait_ge(xt_lo, tb - 1)
                for c in range(NC):
                    last = nc.tensor.transpose(pt[k][:, c, :], xraw[k][:, c * P:(c + 1) * P], ident[:])
                last.then_inc(xt_done, 1)

            def project_v(tb, k, early):
                pe.wait_ge(xt_lo, tb + 1)
                if not early:
                    pe.wait_ge(v_full, tb - 1)
                for n, (a, b) in enumerate(split3(xt[k], wv_s)):
                    for c in range(NC):
                        last = nc.tensor.matmul(pv[k][:], a[:, c, :], b[:, c * C:(c + 1) * C],
                                                start=(n == 0 and c == 0), stop=(n == 2 and c == NC - 1))
                last.then_inc(v_mm, 1)

            pe.wait_ge(ident_in, 16)
            transposes(0, 0, 0, True)
            pe.wait_ge(wv_lo, 1)
            transposes(1, 1, 0, True)
            project_v(0, 0, True)
            transposes(2, 0, 1, False)
            project_v(1, 1, True)
            with pe.Fori(1, NB // 2 - 1) as i:
                transposes(i * 2 + 1, 1, i, False)
                project_v(i * 2, 0, False)
                transposes(i * 2 + 2, 0, i + 1, False)
                project_v(i * 2 + 1, 1, False)
            transposes(NB - 1, 1, NB // 2 - 1, False)
            project_v(NB - 2, 0, False)
            project_v(NB - 1, 1, False)
            pe.wait_ge(hi_kept, NB)
            pe.wait_ge(lo_kept, NB)

            def head_step(i, first):
                for k in range(2):
                    n = i * 2 + k
                    pe.wait_ge(w_lo, n + 1)
                    for t in range(NT):
                        if not (first and k == 0):
                            pe.wait_ge(q_swap, n * NT + t - NT + 1)
                        for m, (a, b) in enumerate(split3(w_s[k], xT)):
                            for c in range(NC):
                                last = nc.tensor.matmul(pq[t][:], a[:, c * P:(c + 1) * P],
                                                        b[:, c, t * 512:(t + 1) * 512],
                                                        start=(m == 0 and c == 0), stop=(m == 2 and c == NC - 1))
                        last.then_inc(q_mm, 1)

            loop(pe, NH // 2, head_step)

        @block.scalar
        def _(act):
            act.wait_ge(wv_in, 32)
            nc.scalar.copy(wv_s[HI][:], wv_raw[:]).then_inc(wv_hi, 1)

            def x_hi(tb, k, early):
                act.wait_ge(xt_done, tb + 1)
                if not early:
                    act.wait_ge(v_mm, tb - 1)
                    act.wait_ge(hi_kept, tb - 1)
                    act.wait_ge(lo_kept, tb - 1)
                nc.scalar.copy(xt[k][HI][:], pt[k][:]).then_inc(xt_hi, 1)

            def v_hi_part(tb, k, i, early):
                act.wait_ge(v_full, tb + 1)
                if not early:
                    act.wait_ge(v_out[k], i * 16)
                nc.scalar.copy(vout[k][:, :, HI, :], vfull[k][:].rearrange("p (j d) -> p j d", j=HKV)
                               ).then_inc(v_hi, 1)

            x_hi(0, 0, True)
            x_hi(1, 1, True)
            v_hi_part(0, 0, 0, True)
            x_hi(2, 0, False)
            v_hi_part(1, 1, 0, True)
            with act.Fori(1, NB // 2 - 1) as i:
                x_hi(i * 2 + 1, 1, False)
                v_hi_part(i * 2, 0, i, False)
                x_hi(i * 2 + 2, 0, False)
                v_hi_part(i * 2 + 1, 1, i, False)
            x_hi(NB - 1, 1, False)
            v_hi_part(NB - 2, 0, NB // 2 - 1, False)
            v_hi_part(NB - 1, 1, NB // 2 - 1, False)

            def weights_hi(n, k, i, early):
                act.wait_ge(w_in[k], i * 16 + 16)
                if not early:
                    act.wait_ge(q_mm, n * NT - NT)
                nc.scalar.copy(w_s[k][HI][:], w_raw[k][:, 0:NC * P]).then_inc(w_hi, 1)

            def swap(q, k, t, early):
                act.wait_ge(q_mm, q + 1)
                if not early:
                    act.wait_ge(q_prod, q - 1)
                half = HD // 2
                bias = w_raw[k][:, NC * P:]
                nc.scalar.activation(qb[t % 2][:], pq[t][:], ACT.Identity, bias=bias)
                nc.scalar.activation(sw[t % 2][0:half, :], pq[t][half:P, :], ACT.Identity, bias=bias[half:P])
                nc.scalar.activation(sw[t % 2][half:P, :], pq[t][0:half, :], ACT.Identity, bias=bias[0:half]
                                     ).then_inc(q_swap, 1)

            def q_hi_part(q, k, t, i, early):
                act.wait_ge(q_rot, q + 1)
                if t == 0 and not early:
                    act.wait_ge(q_out[k], i * 16)
                nc.scalar.copy(qout[k][:, t, HI, :], qr[t][:]).then_inc(q_hi, 1)

            weights_hi(0, 0, 0, True)

            def head_step(i, first, last=False):
                for k in range(2):
                    n = i * 2 + k
                    for t in range(NT):
                        q = i * (2 * NT) + (k * NT + t)
                        swap(q, k, t, first and k == 0 and t < 2)
                        if t > 0:
                            q_hi_part(q - 1, k, t - 1, i, first)
                        elif k > 0:
                            q_hi_part(q - 1, 0, NT - 1, i, first)
                        elif not first:
                            q_hi_part(q - 1, 1, NT - 1, i, False)
                        if t == 0 and not (last and k == 1):
                            weights_hi(n + 1, 1 - k, i + k, first and k == 0)

            head_step(0, True)
            with act.Fori(1, NH // 2 - 1) as i:
                head_step(i, False)
            head_step(NH // 2 - 1, False, last=True)
            q_hi_part(NH * NT - 1, 1, NT - 1, NH // 2 - 1, False)

        @block.vector
        def _(dve):
            dve.wait_ge(wv_hi, 1)
            nc.vector.tensor_tensor(wv_s[LO][:], wv_raw[:], wv_s[HI][:].bitcast(F32), ALU.subtract
                                    ).then_inc(wv_lo, 1)

            def x_lo(tb, k):
                dve.wait_ge(xt_hi, tb + 1)
                nc.vector.tensor_tensor(xt[k][LO][:], pt[k][:], xt[k][HI][:].bitcast(F32), ALU.subtract
                                        ).then_inc(xt_lo, 1)
                dve.wait_ge(xt_lo, tb + 1)
                nc.vector.tensor_copy(xT[LO][:, :, bass.ds(tb * P, P)], xt[k][LO][:].bitcast(F32)).then_inc(lo_kept, 1)

            def v_bias(tb, k, early):
                dve.wait_ge(v_mm, tb + 1)
                if not early:
                    dve.wait_ge(v_lo, tb - 1)
                nc.vector.tensor_tensor(vfull[k][:], pv[k][:], bv_b[:], ALU.add).then_inc(v_full, 1)

            def v_lo_part(tb, k):
                dve.wait_ge(v_hi, tb + 1)
                nc.vector.tensor_tensor(vout[k][:, :, LO, :], vfull[k][:].rearrange("p (j d) -> p j d", j=HKV),
                                        vout[k][:, :, HI, :].bitcast(F32), ALU.subtract).then_inc(v_lo, 1)

            x_lo(0, 0)
            x_lo(1, 1)
            v_bias(0, 0, True)
            x_lo(2, 0)
            v_lo_part(0, 0)
            v_bias(1, 1, True)
            with dve.Fori(1, NB // 2 - 1) as i:
                x_lo(i * 2 + 1, 1)
                v_lo_part(i * 2 - 1, 1)
                v_bias(i * 2, 0, False)
                x_lo(i * 2 + 2, 0)
                v_lo_part(i * 2, 0)
                v_bias(i * 2 + 1, 1, False)
            x_lo(NB - 1, 1)
            v_lo_part(NB - 3, 1)
            v_bias(NB - 2, 0, False)
            v_lo_part(NB - 2, 0)
            v_bias(NB - 1, 1, False)
            v_lo_part(NB - 1, 1)

            def weights_lo(n, k):
                dve.wait_ge(w_hi, n + 1)
                nc.vector.tensor_tensor(w_s[k][LO][:], w_raw[k][:, 0:NC * P], w_s[k][HI][:].bitcast(F32), ALU.subtract
                                        ).then_inc(w_lo, 1)

            def q_products(q, t, early):
                dve.wait_ge(q_swap, q + 1)
                if not early:
                    dve.wait_ge(q_rot, q - 1)
                k, cols = t % 2, slice(t * 512, (t + 1) * 512)
                nc.vector.tensor_tensor(rc[k][:], qb[k][:], cosT[:, cols], ALU.mult)
                nc.vector.tensor_tensor(rs[k][:], sw[k][:], sinT[:, cols], ALU.mult).then_inc(q_prod, 1)

            def q_lo_part(q, k, t):
                dve.wait_ge(q_hi, q + 1)
                nc.vector.tensor_tensor(qout[k][:, t, LO, :], qr[t][:], qout[k][:, t, HI, :].bitcast(F32),
                                        ALU.subtract).then_inc(q_lo, 1)

            dve.wait_ge(const_in, 32)
            weights_lo(0, 0)

            def head_step(i, first, last=False):
                for k in range(2):
                    n = i * 2 + k
                    if not (last and k == 1):
                        weights_lo(n + 1, 1 - k)
                    for t in range(NT):
                        q_products(n * NT + t, t, first and k == 0 and t < 2)
                        if t > 0:
                            q_lo_part(n * NT + t - 1, k, t - 1)
                        elif k > 0:
                            q_lo_part(n * NT - 1, 0, NT - 1)
                        elif not first:
                            q_lo_part(n * NT - 1, 1, NT - 1)

            head_step(0, True)
            with dve.Fori(1, NH // 2 - 1) as i:
                head_step(i, False)
            head_step(NH // 2 - 1, False, last=True)
            q_lo_part(NH * NT - 1, 1, NT - 1)

        @block.gpsimd
        def _(pool):
            def keep_hi(i, first):
                for k in range(2):
                    wait_alone(pool, passed, xt_hi, i * 2 + (k + 1))
                    nc.gpsimd.tensor_copy(xT[HI][:, :, bass.ds((i * 2 + k) * P, P)], xt[k][HI][:].bitcast(F32)
                                          ).then_inc(hi_kept, 1)

            loop(pool, NB // 2, keep_hi)

            def sum_products(i, first):
                for k in range(2):
                    for t in range(NT):
                        q = i * (2 * NT) + (k * NT + t)
                        pool.wait_ge(q_prod, q + 1)
                        if not (first and k == 0):
                            pool.wait_ge(q_lo, q - (NT - 1))
                        nc.gpsimd.tensor_tensor(qr[t][:], rc[t % 2][:], rs[t % 2][:], ALU.add).then_inc(q_rot, 1)

            loop(pool, NH // 2, sum_products)


def stage_attend(nc, passed, ident_d, mask_d, qk_d, v_d, o_d, wo, wo_raw, wo_in):
    U = NB * G
    blk = lambda u: u // G
    width = lambda u: (blk(u) + 1) * P
    ngrp = lambda u: 1 if width(u) <= 1024 else 2
    ntr = lambda u: -(-(blk(u) + 1) // 4)
    SG = [0]
    TG = [0]
    for u in range(U):
        SG.append(SG[-1] + ngrp(u))
        TG.append(TG[-1] + ntr(u))
    PAIRS = U // 2
    KEEP = 5
    LAG = 3
    WEIGH = LAG + 2
    OUT = WEIGH + 2

    def score_group(u, a):
        return (u % 2) if ngrp(u) == 1 else a

    before, last_use = {}, {}
    for u in [u - U for u in range(U)] + list(range(U)):
        for a in range(ngrp(u % U)):
            s = score_group(u % U, a)
            before[(u, a)] = last_use.get(s)
            last_use[s] = SG[u % U] + a - (SG[U] if u < 0 else 0)

    with ExitStack() as ctx:
        def sb(name, shape, dt=F32):
            return ctx.enter_context(nc.sbuf_tensor("p2_" + name, shape, dt))

        def ps(name, shape):
            return ctx.enter_context(nc.psum_tensor("p2_" + name, shape, F32))

        def sem(name):
            return ctx.enter_context(nc.semaphore("p2_" + name))

        ident = sb("ident", [P, P])
        identb = sb("identb", [P, P], BF16)
        maskb = sb("maskb", [P, P], BF16)
        maskf = sb("maskf", [P, P])
        kT = sb("kT", [P, NT, 2, 512], F32R)
        v = sb("v", [P, NB, 2, HD], F32R)
        k_next = sb("k_next", [P, 2, 512], F32R)
        v_next = sb("v_next", [P, 4, 2, HD], F32R)
        q = [sb(f"q{k}", [P, G, 2, 512], F32R) for k in range(2)]
        prob = [sb(f"prob{k}", [P, T]) for k in range(KEEP)]
        pT = [[sb(f"pT{k}{s}", [P, NB, 2, P], F32R) for s in "hl"] for k in range(2)]
        oT = [sb(f"oT{k}", [P, 2, 2, P], F32R) for k in range(2)]
        nmax, nmax1 = sb("nmax", [P, KEEP]), sb("nmax1", [P, KEEP])
        nm = sb("nm", [P, KEEP])
        rsum = sb("rsum", [P, KEEP, 2])
        part = sb("part", [P, KEEP])
        den = sb("den", [P, KEEP])
        inv = sb("inv", [P, KEEP])

        S = ps("S", [P, 2, 1024])
        TP = [ps(f"TP{k}", [P, 4, P]) for k in range(2)]
        O = [ps(f"O{k}", [P, 2, P]) for k in range(2)]

        const_in, const_ready = sem("const_in"), sem("const_ready")
        next_in, k_first, v_first, v_free = sem("next_in"), sem("k_first"), sem("v_first"), sem("v_free")
        k_in = [None] + [sem(f"k_in{c}") for c in range(1, NT)]
        v_in = [None] + [sem(f"v_in{c}") for c in range(1, NT)]
        q_in = [sem(f"q_in{k}") for k in range(2)]
        scored, max_part, max_ready, exped = sem("scored"), sem("max_part"), sem("max_ready"), sem("exped")
        den_ready, inv_ready, normed = sem("den_ready"), sem("inv_ready"), sem("normed")
        turned, turn_hi, turn_lo = sem("turned"), sem("turn_hi"), sem("turn_lo")
        weighed, o_hi, o_lo = sem("weighed"), sem("o_hi"), sem("o_lo")
        o_out = [sem(f"o_out{k}") for k in range(2)]
        FREE = 2

        block = ctx.enter_context(nc.Block())

        def load_q(sp, j, tc):
            sp.dma_start(q[tc % 2][:].bitcast(F32), qk_d[bass.ds(j * G, G), :, tc]
                         .rearrange("g p h t -> p g h t")).then_inc(q_in[tc % 2], 16)

        def load_next(sp, j):
            sp.dma_start(k_next[:].bitcast(F32), qk_d[bass.ds(j + H, 1), :, 0].rearrange("o p h t -> (o p) h t")
                         ).then_inc(next_in, 16)
            sp.dma_start(v_next[:].bitcast(F32), v_d[0:4, bass.ds(j, 1)].rearrange("b o p h d -> (o p) b h d")
                         ).then_inc(next_in, 16)

        def load_k(sp, j):
            for c in range(1, NT):
                sp.dma_start(kT[:, c].bitcast(F32), qk_d[bass.ds(j + H, 1), :, c].rearrange("o p h t -> (o p) h t")
                             ).then_inc(k_in[c], 16)

        def load_v(sp, j):
            for c in range(1, NT):
                sp.dma_start(v[:, c * 4:(c + 1) * 4, :, :].bitcast(F32), v_d[c * 4:(c + 1) * 4, bass.ds(j, 1)]
                             .rearrange("b o p h d -> (o p) b h d")).then_inc(v_in[c], 16)

        def lagged(i, lag, first):
            u = i - lag
            return (u, 0) if u >= 0 else None if first else (u + U, 1)

        def steps(eng, step, tail):
            def body(j, first):
                for i in range(U):
                    step(j, i, first)
            loop(eng, HKV, body)
            for i in range(U, U + tail + 1):
                step(HKV - 1, i, False)

        @block.sync
        def _(sp):
            sp.dma_start(ident[:], ident_d).then_inc(const_in, 16)
            sp.dma_start(maskf[:], mask_d).then_inc(const_in, 16)
            load_next(sp, 0)
            load_q(sp, 0, 0)

            def store(j, p):
                b, g = blk(2 * p), 2 * p % G
                sp.wait_ge(o_lo, j * PAIRS + (p + 1 + FREE))
                sp.dma_start(o_d[b, :, bass.ds(j, 1), g:g + 2].rearrange("p o g h t -> p (o g) h t"),
                             oT[p % 2][:].bitcast(F32)).then_inc(o_out[p % 2], 16)

            def head(j, first=False, last=False):
                if not first:
                    sp.wait_ge(scored, j * SG[U])
                load_k(sp, j)
                load_q(sp, j, 1)
                if not first:
                    store(j - 1, PAIRS - 2)
                    sp.wait_ge(weighed, j * PAIRS + FREE)
                load_v(sp, j)
                if not first:
                    store(j - 1, PAIRS - 1)
                for p in range(PAIRS - 2):
                    store(j, p)
                    if p == 5 and not last:
                        sp.wait_ge(k_first, j + 1)
                        sp.wait_ge(v_first, j + 1)
                        load_next(sp, j + 1)
                    if p in (6, 14, 22):
                        tc = p // 8
                        sp.wait_ge(scored, j * SG[U] + SG[16 * tc + 16])
                        if tc < 2:
                            load_q(sp, j, tc + 2)
                        elif not last:
                            load_q(sp, j + 1, 0)

            head(0, first=True)
            with sp.Fori(1, HKV - 1) as j:
                head(j)
            sp.dma_start(wo_raw[:], wo[:, 0:WO_EARLY, :]).then_inc(wo_in, 16)
            head(HKV - 1, last=True)
            for p in (PAIRS - 2, PAIRS - 1):
                store(HKV - 1, p)
            for k in range(2):
                sp.wait_ge(o_out[k], HKV * (8 * PAIRS))

        @block.tensor
        def _(pe):
            def scores(j, u, a, first):
                b, g, tc = blk(u), u % G, u // 16
                if u == 0:
                    pe.wait_ge(k_first, j + 1)
                elif u % 16 == 0 and a == 0:
                    pe.wait_ge(k_in[tc], j * 16 + 16)
                if u % 16 == 0 and a == 0:
                    pe.wait_ge(q_in[tc % 2], j * 32 + (16 + 16 * (tc // 2)))
                qs = [q[tc % 2][:, g, s, (b % 4) * P:(b % 4 + 1) * P] for s in (HI, LO)]
                if not (first and before[(u, a)] < 0):
                    pe.wait_ge(exped, j * SG[U] + (before[(u, a)] + 1))
                s = score_group(u, a)
                for c0 in range(a * 1024, min(width(u), a * 1024 + 1024), 512):
                    w = min(512, width(u) - c0)
                    out = S[:, s, c0 - a * 1024:c0 - a * 1024 + w]
                    for n, (x, y) in enumerate(split3(qs, [kT[:, c0 // 512, s2, 0:w] for s2 in (HI, LO)])):
                        mm = nc.tensor.matmul(out, x, y, start=(n == 0), stop=(n == 2))
                    if c0 + w == width(u):
                        mm = nc.tensor.matmul(S[:, s, width(u) - P - a * 1024:width(u) - a * 1024], identb[:],
                                              maskb[:], start=False, stop=True, skip_group_check=True)
                mm.then_inc(scored, 1)

            def turn(j, back, u, t):
                if t % 2 == 0:
                    pe.wait_ge(normed, j * SG[U] + (SG[u] + t // 2 + 1 - back * SG[U]))
                n = TG[u] + t
                pe.wait_ge(turn_lo, j * TG[U] + (n + 1 - back * TG[U]))
                for s in range(4 * t, min(4 * t + 4, blk(u) + 1)):
                    mm = nc.tensor.transpose(TP[n % 2][:, s % 4, :], prob[u % KEEP][:, s * P:(s + 1) * P], ident[:])
                mm.then_inc(turned, 1)

            def weigh(j, back, p, part):
                nb = blk(2 * p) + 1
                cut = (nb + 1) // 2
                if part == 0:
                    if p == 0:
                        pe.wait_ge(v_first, j + 1)
                    elif p % 8 == 0:
                        pe.wait_ge(v_in[p // 8], j * 16 + 16)
                    pe.wait_ge(turn_lo, j * TG[U] + (TG[2 * p + 2] + FREE - back * TG[U]))
                    pe.wait_ge(o_lo, j * PAIRS + (p + 1 - back * PAIRS))
                for s in (range(cut), range(cut, nb))[part]:
                    for n, (x, y) in enumerate(split3([v[:, s, h, :] for h in (HI, LO)],
                                                      [pT[p % 2][h][:, s, :, :] for h in (HI, LO)])):
                        mm = nc.tensor.matmul(O[p % 2][:], x, y, start=(s == 0 and n == 0),
                                              stop=(s == nb - 1 and n == 2))
                        if s == nb - 1 and n == 2:
                            mm.then_inc(weighed, 1)
                        elif p == PAIRS - 1 and s == cut - 1 and n == 2:
                            mm.then_inc(v_free, 1)

            def step(j, i, first):
                at = lagged(i, LAG, first)
                turns = [(j, at[1], at[0], t) for t in range(ntr(at[0]))] if at and i < U + LAG else []
                for a in range(2):
                    if i < U and a < ngrp(i):
                        scores(j, i, a, first)
                    for args in turns[0:2] if a == 0 else []:
                        turn(*args)
                at = lagged(i, WEIGH, first)
                if at and i < U + WEIGH:
                    weigh(j, at[1], at[0] // 2, at[0] % 2)
                for args in turns[2:]:
                    turn(*args)

            pe.wait_ge(const_ready, 2)
            steps(pe, step, WEIGH - 1)

        @block.scalar
        def _(act):
            act.wait_ge(const_in, 32)
            nc.scalar.copy(identb[:], ident[:]).then_inc(const_ready, 1)
            nc.scalar.copy(maskb[:], maskf[:]).then_inc(const_ready, 1)
            act.sem_inc(weighed, FREE)

            def exp(j, u, a):
                k = u % KEEP
                act.wait_ge(max_ready, j * SG[U] + (SG[u] + a + 1))
                if a == 1:
                    nc.scalar.activation(part[:, k:k + 1], nmax[:, k:k + 1], ACT.Exp, scale=-1.0, bias=nm[:, k:k + 1])
                w = min(1024, width(u) - a * 1024)
                top = nm if a == ngrp(u) - 1 else nmax
                nc.scalar.activation(prob[k][:, a * 1024:a * 1024 + w], S[:, score_group(u, a), 0:w], ACT.Exp,
                                     bias=top[:, k:k + 1], accum_out=rsum[:, k, a:a + 1]).then_inc(exped, 1)

            def p_hi(j, back, u, t):
                n, p = TG[u] + t, u // 2
                act.wait_ge(turned, j * TG[U] + (n + 1 - back * TG[U]))
                if u % 2 == 0 and t == 0:
                    act.wait_ge(weighed, j * PAIRS + (p + 1 - back * PAIRS))
                m = min(4, blk(u) + 1 - 4 * t)
                nc.scalar.copy(pT[p % 2][HI][:, 4 * t:4 * t + m, u % 2, :], TP[n % 2][:, 0:m, :]).then_inc(turn_hi, 1)

            def out_hi(j, back, p, first):
                act.wait_ge(weighed, j * PAIRS + (p + 1 + FREE - back * PAIRS))
                if not (first and p < 2):
                    act.wait_ge(o_out[p % 2], j * (8 * PAIRS) + (16 * (p // 2) - back * 8 * PAIRS))
                nc.scalar.copy(oT[p % 2][:, :, HI, :], O[p % 2][:]).then_inc(o_hi, 1)

            def step(j, i, first):
                at = lagged(i, OUT, first)
                if at and i % 2 == OUT % 2:
                    out_hi(j, at[1], at[0] // 2, first)
                at = lagged(i, LAG, first)
                turns = [(j, at[1], at[0], t) for t in range(ntr(at[0]))] if at and i < U + LAG else []
                for a in range(2):
                    for args in turns[2 * a:2 * a + 2]:
                        p_hi(*args)
                    if i < U and a < ngrp(i):
                        exp(j, i, a)

            steps(act, step, OUT - 2)

        @block.vector
        def _(dve):
            dve.sem_inc(turn_lo, FREE)
            dve.sem_inc(o_lo, FREE)

            def take_k(j):
                dve.wait_ge(next_in, j * 32 + 32)
                nc.vector.tensor_copy(kT[:, 0], k_next[:].bitcast(F32)).then_inc(k_first, 1)

            def take_v(j, first):
                if not first:
                    dve.wait_ge(v_free, j)
                nc.vector.tensor_copy(v[:, 0:4], v_next[:].bitcast(F32)).then_inc(v_first, 1)

            def row_max(j, u, a):
                k, wide = u % KEEP, ngrp(u) == 2
                dve.wait_ge(scored, j * SG[U] + (SG[u] + a + 1))
                w = min(1024, width(u) - a * 1024)
                out = (nmax if a == 0 else nmax1) if wide else nm
                r = nc.vector.reduce_max(out[:, k:k + 1], S[:, score_group(u, a), 0:w], AX_X, negate=True)
                r.then_inc(max_part if a == 1 else max_ready, 1)
                if a == 1:
                    dve.wait_ge(max_part, j * (SG[U] - U) + (SG[u + 1] - u - 1))
                    nc.vector.tensor_tensor(nm[:, k:k + 1], nmax[:, k:k + 1], nmax1[:, k:k + 1], ALU.min
                                            ).then_inc(max_ready, 1)

            def recip(j, back, u):
                k = u % KEEP
                dve.wait_ge(exped, j * SG[U] + (SG[u + 1] - back * SG[U]))
                if ngrp(u) == 1:
                    nc.vector.reciprocal(inv[:, k:k + 1], rsum[:, k, 0:1]).then_inc(inv_ready, 1)
                else:
                    nc.vector.scalar_tensor_tensor(den[:, k:k + 1], rsum[:, k, 0:1], part[:, k:k + 1], rsum[:, k, 1:2],
                                                   ALU.mult, ALU.add).then_inc(den_ready, 1)
                    dve.wait_ge(den_ready, j * (SG[U] - U) + (SG[u + 1] - u - 1 - back * (SG[U] - U)))
                    nc.vector.reciprocal(inv[:, k:k + 1], den[:, k:k + 1]).then_inc(inv_ready, 1)

            def p_lo(j, back, u, t):
                n, p = TG[u] + t, u // 2
                dve.wait_ge(turn_hi, j * TG[U] + (n + 1 - back * TG[U]))
                m = min(4, blk(u) + 1 - 4 * t)
                nc.vector.tensor_tensor(pT[p % 2][LO][:, 4 * t:4 * t + m, u % 2, :], TP[n % 2][:, 0:m, :],
                                        pT[p % 2][HI][:, 4 * t:4 * t + m, u % 2, :].bitcast(F32), ALU.subtract
                                        ).then_inc(turn_lo, 1)

            def out_lo(j, back, p):
                dve.wait_ge(o_hi, j * PAIRS + (p + 1 - back * PAIRS))
                nc.vector.tensor_tensor(oT[p % 2][:, :, LO, :], O[p % 2][:], oT[p % 2][:, :, HI, :].bitcast(F32),
                                        ALU.subtract).then_inc(o_lo, 1)

            def step(j, i, first):
                if i == 0:
                    take_k(j)
                if i == (0 if first else WEIGH - 1):
                    take_v(j, first)
                at = lagged(i, OUT, first)
                if at and i % 2 == OUT % 2:
                    out_lo(j, at[1], at[0] // 2)
                at = lagged(i, 1, first)
                if at and i < U + 1:
                    recip(j, at[1], at[0])
                at = lagged(i, LAG, first)
                turns = [(j, at[1], at[0], t) for t in range(ntr(at[0]))] if at and i < U + LAG else []
                for a in range(2):
                    if i < U and a < ngrp(i):
                        row_max(j, i, a)
                    for args in turns[2 * a:2 * a + 2]:
                        p_lo(*args)

            steps(dve, step, OUT - 2)

        @block.gpsimd
        def _(pool):
            def step(j, first):
                for u in range(U):
                    k = u % KEEP
                    wait_alone(pool, passed, inv_ready, j * U + (u + 1))
                    for a in range(ngrp(u)):
                        cols = slice(a * 1024, min(width(u), a * 1024 + 1024))
                        scale = part[:, k:k + 1] if a < ngrp(u) - 1 else 1.0
                        nc.gpsimd.tensor_scalar(prob[k][:, cols], prob[k][:, cols], inv[:, k:k + 1], scale,
                                                ALU.mult, ALU.mult).then_inc(normed, 1)

            loop(pool, HKV, step)


def stage_route(nc, passed, x, wo, bo, rw, ident_d, lower_d, o_d, x1_d, slot_d, comb, wcomb, wo_raw, wo_in):
    with ExitStack() as ctx:
        def sb(name, shape, dt=F32):
            return ctx.enter_context(nc.sbuf_tensor("p3_" + name, shape, dt))

        def ps(name, shape):
            return ctx.enter_context(nc.psum_tensor("p3_" + name, shape, F32))

        def sem(name):
            return ctx.enter_context(nc.semaphore("p3_" + name))

        PARTS = 4
        wo_last = sb("wo_last", [P, H - WO_EARLY, C])
        wo_s = [sb(f"wo{s}", [P, H, C], F32R) for s in "hl"]
        ident, lower, ones = sb("ident", [P, P]), sb("lower", [P, P]), sb("ones", [P, P])
        bo_b = sb("bo_b", [P, C])
        rwT = sb("rwT", [P, NC, E])
        eps = sb("eps", [P, 1])
        iota_e = sb("iota_e", [P, E])
        tok = [sb(f"tok{k}", [P, 1], I32) for k in range(2)]
        zero = sb("zero", [P, SLOTS // P], I32)
        ot = [sb(f"ot{k}", [P, H, 2, P], F32R) for k in range(2)]
        xr = [sb(f"xr{k}", [P, C]) for k in range(2)]
        xb = [sb(f"xb{k}", [P, C]) for k in range(2)]
        h = [sb(f"h{k}", [P, C]) for k in range(2)]
        st = sb("st", [P, 6])
        mv = sb("mv", [P, 2])
        sd, rstd = sb("sd", [P, 1]), sb("rstd", [P, 1])
        x1 = [sb(f"x1{k}", [P, C]) for k in range(2)]
        x1T = sb("x1T", [P, NC, P])
        top, topi, topf = sb("top", [P, TOPK]), sb("topi", [P, TOPK], U32), sb("topf", [P, TOPK])
        ntop, et, esum, einv = sb("ntop", [P, 1]), sb("et", [P, TOPK]), sb("esum", [P, 1]), sb("einv", [P, 1])
        hot = sb("hot", [P, TOPK, E])
        mask = sb("mask", [P, E])
        count = sb("count", [P, E])
        posn = sb("posn", [P, E])
        pick = sb("pick", [P, TOPK, E])
        pos = sb("pos", [P, TOPK])
        slot, over, wk, keep = sb("slot", [P, TOPK]), sb("over", [P, TOPK]), sb("wk", [P, TOPK]), sb("keep", [P, TOPK])
        slot_out = sb("slot_out", [P, TOPK])
        slot_i = [sb(f"slot_i{k}", [P, TOPK], U32) for k in range(2)]

        acc = [ps(f"acc{k}", [P, C]) for k in range(2)]
        xtp = ps("xtp", [P, NC, P])
        lg = ps("lg", [P, E])
        cum = ps("cum", [P, E])
        tot = ps("tot", [P, E])

        const_in, zeroed, ones_ready = sem("const_in"), sem("zeroed"), sem("ones_ready")
        wo_last_in, wo_hi, wo_lo = sem("wo_last_in"), sem("wo_hi"), sem("wo_lo")
        ot_in = [sem(f"ot_in{k}") for k in range(2)]
        xr_in = [sem(f"xr_in{k}") for k in range(2)]
        biased, projected, normed = sem("biased"), sem("projected"), sem("normed")
        norm_step, choose_step, place_step = sem("norm_step"), sem("choose_step"), sem("place_step")
        var_ready, sd_ready = sem("var_ready"), sem("sd_ready")
        x1_out = [sem(f"x1_out{k}") for k in range(2)]
        turned, copied, routed, topped, exped = sem("turned"), sem("copied"), sem("routed"), sem("topped"), sem("exped")
        masked, summed, placed = sem("masked"), sem("summed"), sem("placed")
        scattered = [sem(f"scattered{k}") for k in range(2)]
        iota_ready, tok_next = sem("iota_ready"), sem("tok_next")

        block = ctx.enter_context(nc.Block())

        def wo_part(n):
            return wo_raw[:, n * H // PARTS:(n + 1) * H // PARTS, :] if n < PARTS - 1 else wo_last[:]

        def load_block(sp, b, k):
            sp.dma_start(ot[k][:].bitcast(F32), o_d[bass.ds(b, 1)].rearrange("o p j g h t -> (o p) (j g) h t")).then_inc(ot_in[k], 16)
            sp.dma_start(xr[k][:], x[bass.ds(b * P, P), :]).then_inc(xr_in[k], 16)

        @block.sync
        def _(sp):
            for k in range(2):
                load_block(sp, k, k)
            sp.dma_start(ident[:], ident_d).then_inc(const_in, 16)
            sp.dma_start(wo_last[:], wo[:, WO_EARLY:, :]).then_inc(wo_last_in, 16)
            sp.dma_start(lower[:], lower_d).then_inc(const_in, 16)
            sp.dma_start(bo_b[:], bo.partition_broadcast(P)).then_inc(const_in, 16)
            sp.dma_start(rwT[:], rw).then_inc(const_in, 16)
            sp.wait_ge(zeroed, 1)
            sp.dma_start(slot_d.rearrange("(p s) o -> p (s o)", p=P), zero[:]).then_inc(zeroed, 16)

            def step(i, last=False):
                for k in range(2):
                    b = i * 2 + k
                    if not last:
                        sp.wait_ge(projected, b + 1)
                        sp.wait_ge(biased, b + 1)
                        load_block(sp, b + 2, k)
                    sp.wait_ge(normed, b + 1)
                    sp.dma_start(x1_d[bass.ds(b * P, P), :], x1[k][:]).then_inc(x1_out[k], 16)

            with sp.Fori(0, NB // 2 - 1) as i:
                step(i)
            step(NB // 2 - 1, last=True)
            for k in range(2):
                sp.wait_ge(x1_out[k], 16 * (NB // 2))

        @block.tensor
        def _(pe):
            PART = H // PARTS

            def project(b, k, heads, first):
                for n in heads:
                    if first and n % PART == 0:
                        pe.wait_ge(wo_lo, n // PART + 1)
                    for m, (a, w) in enumerate(split3([ot[k][:, n, s, :] for s in (HI, LO)],
                                                      [wo_s[s][:, n, :] for s in (HI, LO)])):
                        mm = nc.tensor.matmul(acc[k][:], a, w, start=(n == 0 and m == 0), stop=(n == H - 1 and m == 2))
                if n == H - 1:
                    mm.then_inc(projected, 1)

            def turn(b, k, early):
                pe.wait_ge(normed, b + 1)
                if not early:
                    pe.wait_ge(copied, b)
                for c in range(NC):
                    mm = nc.tensor.transpose(xtp[:, c, :], x1[k][:, c * P:(c + 1) * P], ident[:])
                mm.then_inc(turned, 1)

            def logits(b, early):
                pe.wait_ge(copied, b + 1)
                if not early:
                    pe.wait_ge(topped, b)
                for c in range(NC):
                    mm = nc.tensor.matmul(lg[:], x1T[:, c, :], rwT[:, c, :], start=(c == 0), stop=(c == NC - 1))
                mm.then_inc(routed, 1)

            def sums(b):
                pe.wait_ge(masked, b + 1)
                nc.tensor.matmul(cum[:], lower[:], mask[:], start=True, stop=True)
                nc.tensor.matmul(tot[:], ones[:], mask[:], start=True, stop=True).then_inc(summed, 1)

            def step(i, first):
                for k in range(2):
                    b = i * 2 + k
                    pe.wait_ge(ot_in[k], i * 16 + 16)
                    if not first:
                        pe.wait_ge(normed, b - 1)
                    project(b, k, range(H // 2), first and k == 0)
                    if not first:
                        sums(b - 2)
                    if not (first and k == 0):
                        turn(b - 1, 1 - k, first)
                    project(b, k, range(H // 2, 3 * H // 4), first and k == 0)
                    if not (first and k == 0):
                        logits(b - 1, first)
                    project(b, k, range(3 * H // 4, H), first and k == 0)

            pe.wait_ge(const_in, 64)
            pe.wait_ge(ones_ready, 1)
            loop(pe, NB // 2, step)
            sums(NB - 2)
            turn(NB - 1, 1, False)
            logits(NB - 1, False)
            sums(NB - 1)

        @block.scalar
        def _(act):
            act.wait_ge(wo_in, 16)
            for n in range(PARTS):
                part = slice(n * H // PARTS, (n + 1) * H // PARTS)
                if n == PARTS - 1:
                    act.wait_ge(wo_last_in, 16)
                nc.scalar.copy(wo_s[HI][:, part, :], wo_part(n)).then_inc(wo_hi, 1)

            def step(i, first):
                for k in range(2):
                    b = i * 2 + k
                    act.wait_ge(var_ready, b + 1)
                    nc.scalar.activation(sd[:], mv[:, 1:2], ACT.Sqrt, bias=eps[:]).then_inc(sd_ready, 1)
                    act.wait_ge(turned, b + 1)
                    if not (first and k == 0):
                        act.wait_ge(routed, b)
                    nc.scalar.copy(x1T[:], xtp[:]).then_inc(copied, 1)
                    act.wait_ge(topped, b + 1)
                    nc.scalar.activation(et[:], top[:], ACT.Exp, bias=ntop[:], accum_out=esum[:]).then_inc(exped, 1)

            loop(act, NB // 2, step)

        @block.vector
        def _(dve):
            nc.vector.memset(zero[:], 0).then_inc(zeroed, 1)
            nc.vector.memset(ones[:], 1.0).then_inc(ones_ready, 1)
            nc.vector.memset(eps[:], EPS)
            nc.vector.memset(count[:], 0.0)
            for n in range(PARTS):
                part = slice(n * H // PARTS, (n + 1) * H // PARTS)
                dve.wait_ge(wo_hi, n + 1)
                nc.vector.tensor_tensor(wo_s[LO][:, part, :], wo_part(n), wo_s[HI][:, part, :].bitcast(F32),
                                        ALU.subtract).then_inc(wo_lo, 1)
            dve.wait_ge(iota_ready, 1)

            def chain(done, links, b):
                at = [0]

                def link(ins):
                    at[0] += 1
                    assert at[0] <= links
                    ins.then_inc(done, 1)
                    wait_alone(dve, passed, done, b * links + at[0])
                return link

            def normalise(b, k, i, early):
                link = chain(norm_step, 3, b)
                dve.wait_ge(projected, b + 1)
                dve.wait_ge(biased, b + 1)
                link(nc.vector.tensor_tensor(h[k][:], acc[k][:], xb[k][:], ALU.add))
                link(nc.vector.bn_stats(st[:], h[k][:]))
                nc.vector.bn_aggr(mv[:], st[:]).then_inc(var_ready, 1)
                dve.wait_ge(sd_ready, b + 1)
                link(nc.vector.reciprocal(rstd[:], sd[:]))
                if not early:
                    dve.wait_ge(x1_out[k], i * 16)
                nc.vector.tensor_scalar(x1[k][:], h[k][:], mv[:, 0:1], rstd[:], ALU.subtract, ALU.mult
                                        ).then_inc(normed, 1)

            def choose(b):
                link = chain(choose_step, 6, b)
                wait_alone(dve, passed, routed, b + 1)
                link(nc.vector.max(top[:], lg[:]))
                link(nc.vector.max_index(topi[:], top[:], lg[:]))
                nc.vector.tensor_scalar(ntop[:], top[:, 0:1], -1.0, None, ALU.mult).then_inc(topped, 1)
                link(nc.vector.tensor_copy(topf[:], topi[:]))
                link(nc.vector.tensor_tensor(hot[:], iota_e[:].unsqueeze(1).to_broadcast([P, TOPK, E]),
                                             topf[:].unsqueeze(2).to_broadcast([P, TOPK, E]), ALU.is_equal))
                nc.vector.tensor_reduce(mask[:], hot[:].rearrange("p k e -> p e k"), AX_X, ALU.add).then_inc(masked, 1)
                dve.wait_ge(exped, b + 1)
                link(nc.vector.reciprocal(einv[:], esum[:]))
                link(nc.vector.tensor_scalar(wk[:], et[:], einv[:], None, ALU.mult))

            def place(b, k, i, early):
                link = chain(place_step, 6, b)
                dve.wait_ge(summed, b + 1)
                link(nc.vector.tensor_tensor(posn[:], cum[:], count[:], ALU.add))
                nc.vector.tensor_tensor(count[:], tot[:], count[:], ALU.add)
                link(nc.vector.tensor_tensor(pick[:], hot[:], posn[:].unsqueeze(1).to_broadcast([P, TOPK, E]), ALU.mult))
                link(nc.vector.tensor_reduce(pos[:], pick[:], AX_X, ALU.add))
                nc.vector.tensor_scalar(over[:], pos[:], float(CAP), float(2 * SLOTS), ALU.is_ge, ALU.mult)
                nc.vector.tensor_scalar(keep[:], pos[:], float(CAP), None, ALU.is_lt)
                link(nc.vector.scalar_tensor_tensor(slot[:], topf[:], float(CAP), pos[:], ALU.mult, ALU.add))
                nc.vector.tensor_tensor(wcomb[:, bass.ds(b, 1), :].rearrange("p o k -> p (o k)"), wk[:], keep[:], ALU.mult)
                link(nc.vector.tensor_tensor(slot_out[:], slot[:], over[:], ALU.add))
                link(nc.vector.tensor_tensor(comb[:, bass.ds(b, 1), :].rearrange("p o k -> p (o k)"), slot[:], keep[:],
                                             ALU.mult))
                if not early:
                    dve.wait_ge(scattered[k], i * (16 * TOPK))
                nc.vector.tensor_copy(slot_i[k][:], slot_out[:]).then_inc(placed, 1)

            def step(i, first, second=False):
                for k in range(2):
                    b = i * 2 + k
                    normalise(b, k, i, first)
                    if k == 1:
                        place(b - 1, 0, i, first)
                    elif not first:
                        place(b - 1, 1, i - 1, second)
                    choose(b)

            step(0, True)
            step(1, False, second=True)
            with dve.Fori(2, NB // 2) as i:
                step(i, False)
            place(NB - 1, 1, NB // 2 - 1, False)

        @block.gpsimd
        def _(pool):
            nc.gpsimd.iota(iota_e[:], [[1, E]], base=0, channel_multiplier=0, allow_small_or_imprecise_dtypes=True)
            for k in range(2):
                nc.gpsimd.iota(tok[k][:], [[0, 1]], base=k * P, channel_multiplier=1).then_inc(iota_ready, 1)
            pool.wait_ge(const_in, 64)

            def residual(b, k, i, early):
                pool.wait_ge(xr_in[k], i * 16 + 16)
                if not early:
                    pool.wait_ge(normed, b - 1)
                nc.gpsimd.tensor_tensor(xb[k][:], xr[k][:], bo_b[:], ALU.add).then_inc(biased, 1)

            def scatter(b, k, i, early):
                if not early:
                    wait_alone(pool, passed, scattered[k], i * (16 * TOPK))
                    nc.gpsimd.tensor_scalar(tok[k][:], tok[k][:], float(2 * P), None, ALU.add).then_inc(tok_next, 1)
                    pool.wait_ge(tok_next, b - 1)
                wait_alone(pool, passed, placed, b + 1)
                for n in range(TOPK):
                    nc.gpsimd.indirect_dma_start(
                        out=slot_d, out_offset=bass.IndirectOffsetOnAxis(ap=slot_i[k][:, n:n + 1], axis=0),
                        in_=tok[k][:], in_offset=None, bounds_check=SLOTS - 1, oob_is_err=False
                    ).then_inc(scattered[k], 16)

            for k in range(2):
                residual(k, k, 0, True)
            pool.wait_ge(iota_ready, 2)
            pool.wait_ge(zeroed, 17)

            def step(i, first, last=False):
                for k in range(2):
                    b = i * 2 + k
                    if not last:
                        residual(b + 2, k, i + 1, False)
                    scatter(b, k, i, first)

            step(0, True)
            with pool.Fori(1, NB // 2 - 1) as i:
                step(i, False)
            step(NB // 2 - 1, False, last=True)
            for k in range(2):
                pool.wait_ge(scattered[k], NB // 2 * (16 * TOPK))


def stage_experts(nc, passed, gu, dn, ident_d, slot_d, x1_d, y_d):
    PAIRS = E // 2
    GU = 3 * P
    with ExitStack() as ctx:
        def sb(name, shape, dt=F32):
            return ctx.enter_context(nc.sbuf_tensor("p4_" + name, shape, dt))

        def ps(name, shape):
            return ctx.enter_context(nc.psum_tensor("p4_" + name, shape, F32))

        def sem(name):
            return ctx.enter_context(nc.semaphore("p4_" + name))

        WCOLS = NC * GU + C
        ident = sb("ident", [P, P])
        table_i = sb("table_i", [P, P], I32)
        table_f = sb("table_f", [P, P])
        tableT = sb("tableT", [P, E, CH], U32)
        w_raw = [sb(f"w_raw{k}", [P, WCOLS]) for k in range(2)]
        t_raw = sb("t_raw", [P, C])
        w_s = [[sb(f"w{k}{s}", [P, WCOLS], F32R) for s in "hl"] for k in range(2)]
        t_s = [sb(f"t{s}", [P, C], F32R) for s in "hl"]
        idx = [sb(f"idx{k}", [P, CH], U32) for k in range(2)]
        xg = [[sb(f"xg{k}{c}", [P, C]) for c in range(CH)] for k in range(2)]
        xT = [sb(f"xT{s}", [P, NC, CAP], F32R) for s in "hl"]
        sg, sgt = sb("sg", [P, CAP]), sb("sgt", [P, CAP])
        h = sb("h", [P, 2, CAP])
        h_s = [sb(f"h{s}", [P, 2, CAP], F32R) for s in "hl"]
        y = [[sb(f"y{k}{c}", [P, C]) for c in range(CH)] for k in range(2)]

        tp = [ps(f"tp{c}", [P, NC, P]) for c in range(CH)]
        pgu = ps("pgu", [P, 2, CAP])
        prest = ps("prest", [P, CAP])
        py = [ps(f"py{c}", [P, C]) for c in range(CH)]

        const_in, table_ready, idx_ready = sem("const_in"), sem("table_ready"), sem("idx_ready")
        gu_in = [sem(f"gu_in{k}") for k in range(2)]
        dn_in = [sem(f"dn_in{k}") for k in range(2)]
        t_in = sem("t_in")
        x_in = [[sem(f"x_in{k}{c}") for c in range(CH)] for k in range(2)]
        gu_hi, gu_lo, dn_hi, dn_lo = sem("gu_hi"), sem("gu_lo"), sem("dn_hi"), sem("dn_lo")
        t_hi, t_lo = sem("t_hi"), sem("t_lo")
        turned, x_hi, x_lo = sem("turned"), sem("x_hi"), sem("x_lo")
        gated, silued, rest_silued, h_main, h_rest = (sem("gated"), sem("silued"), sem("rest_silued"), sem("h_main"),
                                                      sem("h_rest"))
        h_part, h_split = sem("h_part"), sem("h_split")
        downed, y_a, y_b = sem("downed"), sem("y_a"), sem("y_b")
        y_out = [[sem(f"y_out{k}{c}") for c in range(CH)] for k in range(2)]

        GUC, DNC = slice(0, NC * GU), slice(NC * GU, WCOLS)

        def rest(k):
            half = slice(k * IT, (k + 1) * IT)
            return half, slice((1 - k) * IT, (2 - k) * IT)

        def ahead(i, k, n):
            return i + (k + n) // 2, (k + n) % 2

        def first(i):
            return isinstance(i, int) and i == 0

        def exists(i):
            return not isinstance(i, int) or i < PAIRS

        def steps(eng, step, behind=2):
            for k in range(2):
                step(0, k)
            with eng.Fori(1, PAIRS - behind) as i:
                for k in range(2):
                    step(i, k)
            for i in range(PAIRS - behind, PAIRS):
                for k in range(2):
                    step(i, k)

        block = ctx.enter_context(nc.Block())

        @block.sync
        def _(sp):
            def load(i, k, cols, split, done):
                if not first(i):
                    sp.wait_ge(split, i * 2 + (k - 1))
                sp.dma_start(w_raw[k][:, cols], gu[bass.ds(i * 2 + k, 1), :, cols].rearrange("o p n -> (o p) n")
                             ).then_inc(done[k], 16)

            def load_gu(i, k):
                load(i, k, GUC, gu_lo, gu_in)

            def load_dn(i, k):
                load(i, k, DNC, dn_lo, dn_in)

            def load_t(i):
                if not first(i):
                    sp.wait_ge(t_lo, i)
                sp.dma_start(t_raw[:], dn[bass.ds(i, 1)].rearrange("o p n -> (o p) n")).then_inc(t_in, 16)

            def step(i, k):
                e = i * 2 + k
                if exists(ahead(i, k, 5)[0]):
                    load_gu(*ahead(i, k, 5))
                for c, done in ((0, y_a), (1, y_b)):
                    sp.wait_ge(done, e + 1)
                    sp.dma_start(y_d[bass.ds(e * CAP + c * P, P), :], y[k][c][:]).then_inc(y_out[k][c], 16)
                if exists(i + 2):
                    load_dn(i + 2, k)
                if k == 0 and exists(i + 1):
                    load_t(i + 1)

            sp.dma_start(table_i[:], slot_d.rearrange("(p s) o -> p (s o)", p=P)).then_inc(const_in, 16)
            sp.dma_start(ident[:], ident_d).then_inc(const_in, 16)
            load_gu(0, 0)
            load_gu(0, 1)
            for k in range(2):
                load_dn(0, k)
            load_t(0)
            for i, k in ((1, 0), (1, 1), (2, 0)):
                load_gu(i, k)
            for k in range(2):
                load_dn(1, k)
            steps(sp, step, behind=3)
            for k in range(2):
                for c in range(CH):
                    sp.wait_ge(y_out[k][c], 16 * PAIRS)

        @block.tensor
        def _(pe):
            def turn(i, k):
                for c in range(CH):
                    pe.wait_ge(x_in[k][c], i * 16 + 16)
                    if not (first(i) and k == 0):
                        pe.wait_ge(x_lo, (i * 2 + k) * CH + (c - CH + 1))
                    for d in range(NC):
                        mm = nc.tensor.transpose(tp[c][:, d, :], xg[k][c][:, d * P:(d + 1) * P], ident[:])
                    mm.then_inc(turned, 1)

            def gate_up(i, k):
                e = i * 2 + k
                pe.wait_ge(x_lo, e * CH + CH)
                pe.wait_ge(gu_lo, e + 1)
                if not (first(i) and k == 0):
                    pe.wait_ge(h_rest, e)
                for f, out in enumerate((pgu[:, 0, :], pgu[:, 1, :], prest[:])):
                    for m, (a, b) in enumerate(split3(w_s[k], xT)):
                        for d in range(NC):
                            col = d * GU + f * P
                            mm = nc.tensor.matmul(out, a[:, col:col + P], b[:, d, :], start=(m == 0 and d == 0),
                                                  stop=(m == 2 and d == NC - 1))
                mm.then_inc(gated, 1)

            def down(i, k):
                e = i * 2 + k
                half, _ = rest(k)
                pe.wait_ge(h_split, e + 1)
                pe.wait_ge(dn_lo, e + 1)
                if k == 0:
                    pe.wait_ge(t_lo, i + 1)
                if not (first(i) and k == 0):
                    pe.wait_ge(y_a, e)
                    pe.wait_ge(y_b, e)
                for c in range(CH):
                    cols = slice(c * P, (c + 1) * P)
                    for m, (a, b) in enumerate(split3(h_s, w_s[k])):
                        nc.tensor.matmul(py[c][:], a[:, 0, cols], b[:, DNC], start=(m == 0), stop=False)
                    for m, (a, b) in enumerate(split3(h_s, t_s)):
                        mm = nc.tensor.matmul(py[c][:], a[half, 1, cols], b[half, :], start=False, stop=(m == 2))
                mm.then_inc(downed, 1)

            def step(i, k):
                for f, n in ((gate_up, 1), (turn, 2), (down, 0)):
                    if exists(ahead(i, k, n)[0]):
                        f(*ahead(i, k, n))

            pe.wait_ge(const_in, 32)
            pe.wait_ge(table_ready, 1)
            nc.tensor.transpose(tp[0][:, 0, :], table_f[:], ident[:]).then_inc(table_ready, 1)
            pe.wait_ge(table_ready, 3)
            turn(0, 0)
            gate_up(0, 0)
            turn(0, 1)
            steps(pe, step)

        @block.scalar
        def _(act):
            def gate_up_hi(i, k):
                act.wait_ge(gu_in[k], i * 16 + 16)
                if not first(i):
                    act.wait_ge(gated, i * 2 + (k - 1))
                nc.scalar.copy(w_s[k][HI][:, GUC], w_raw[k][:, GUC]).then_inc(gu_hi, 1)

            def down_hi(i, k):
                act.wait_ge(dn_in[k], i * 16 + 16)
                if not first(i):
                    act.wait_ge(downed, i * 2 + (k - 1))
                nc.scalar.copy(w_s[k][HI][:, DNC], w_raw[k][:, DNC]).then_inc(dn_hi, 1)

            def rests_hi(i):
                act.wait_ge(t_in, i * 16 + 16)
                if not first(i):
                    act.wait_ge(downed, i * 2)
                nc.scalar.copy(t_s[HI][:], t_raw[:]).then_inc(t_hi, 1)

            def turn_hi(i, k):
                e = i * 2 + k
                for c in range(CH):
                    act.wait_ge(turned, e * CH + (c + 1))
                    if not (first(i) and k == 0):
                        act.wait_ge(gated, e)
                    nc.scalar.copy(xT[HI][:, :, c * P:(c + 1) * P], tp[c][:]).then_inc(x_hi, 1)

            def silu(i, k):
                e = i * 2 + k
                half, other = rest(k)
                act.wait_ge(gated, e + 1)
                if not (first(i) and k == 0):
                    act.wait_ge(h_rest, e)
                nc.scalar.activation(sg[:], pgu[:, 0, :], ACT.Silu).then_inc(silued, 1)
                nc.scalar.activation(sgt[half, :], prest[other, :], ACT.Silu).then_inc(rest_silued, 1)

            def rows(i, k):
                act.wait_ge(downed, i * 2 + (k + 1))
                if not first(i):
                    act.wait_ge(y_out[k][0], i * 16)
                nc.scalar.copy(y[k][0][:], py[0][:]).then_inc(y_a, 1)

            def step(i, k):
                for f, n in ((silu, 1), (turn_hi, 2), (gate_up_hi, 3), (rows, 0), (down_hi, 2)):
                    if exists(ahead(i, k, n)[0]):
                        f(*ahead(i, k, n))
                if k == 1 and exists(i + 1):
                    rests_hi(i + 1)

            turn_hi(0, 0)
            gate_up_hi(0, 0)
            turn_hi(0, 1)
            gate_up_hi(0, 1)
            down_hi(0, 0)
            down_hi(0, 1)
            rests_hi(0)
            silu(0, 0)
            gate_up_hi(1, 0)
            steps(act, step)

        @block.vector
        def _(dve):
            def gate_up_lo(i, k):
                dve.wait_ge(gu_hi, i * 2 + (k + 1))
                nc.vector.tensor_tensor(w_s[k][LO][:, GUC], w_raw[k][:, GUC], w_s[k][HI][:, GUC].bitcast(F32), ALU.subtract
                                        ).then_inc(gu_lo, 1)

            def down_lo(i, k):
                dve.wait_ge(dn_hi, i * 2 + (k + 1))
                nc.vector.tensor_tensor(w_s[k][LO][:, DNC], w_raw[k][:, DNC], w_s[k][HI][:, DNC].bitcast(F32), ALU.subtract
                                        ).then_inc(dn_lo, 1)

            def rests_lo(i):
                dve.wait_ge(t_hi, i + 1)
                nc.vector.tensor_tensor(t_s[LO][:], t_raw[:], t_s[HI][:].bitcast(F32), ALU.subtract).then_inc(t_lo, 1)

            def turn_lo(i, k):
                for c in range(CH):
                    dve.wait_ge(x_hi, (i * 2 + k) * CH + (c + 1))
                    cols = slice(c * P, (c + 1) * P)
                    nc.vector.tensor_tensor(xT[LO][:, :, cols], tp[c][:], xT[HI][:, :, cols].bitcast(F32), ALU.subtract
                                            ).then_inc(x_lo, 1)

            def gate(i, k):
                e = i * 2 + k
                half, _ = rest(k)
                dve.wait_ge(silued, e + 1)
                if not (first(i) and k == 0):
                    dve.wait_ge(h_split, e)
                nc.vector.tensor_tensor(h[:, 0, :], pgu[:, 1, :], sg[:], ALU.mult).then_inc(h_main, 1)
                dve.wait_ge(rest_silued, e + 1)
                nc.vector.tensor_tensor(h[half, 1, :], prest[half, :], sgt[half, :], ALU.mult).then_inc(h_rest, 1)

            def rows(i, k):
                dve.wait_ge(downed, i * 2 + (k + 1))
                if not first(i):
                    dve.wait_ge(y_out[k][1], i * 16)
                nc.vector.tensor_copy(y[k][1][:], py[1][:]).then_inc(y_b, 1)

            def step(i, k):
                for f, n in ((gate, 1), (turn_lo, 2), (gate_up_lo, 3), (rows, 0), (down_lo, 2)):
                    if exists(ahead(i, k, n)[0]):
                        f(*ahead(i, k, n))
                if k == 1 and exists(i + 1):
                    rests_lo(i + 1)

            nc.vector.memset(h[:], 0.0)
            dve.wait_ge(const_in, 32)
            nc.vector.tensor_copy(table_f[:], table_i[:]).then_inc(table_ready, 1)
            dve.wait_ge(table_ready, 2)
            nc.vector.tensor_copy(tableT[:].rearrange("p e c -> p (e c)"), tp[0][:, 0, :]).then_inc(table_ready, 1)
            turn_lo(0, 0)
            gate_up_lo(0, 0)
            turn_lo(0, 1)
            gate_up_lo(0, 1)
            down_lo(0, 0)
            down_lo(0, 1)
            rests_lo(0)
            gate(0, 0)
            gate_up_lo(1, 0)
            steps(dve, step)

        @block.gpsimd
        def _(pool):
            def gather(i, k):
                e = i * 2 + k
                if not first(i):
                    pool.wait_ge(turned, e * CH - CH)
                nc.gpsimd.tensor_copy(idx[k][:], tableT[:, bass.ds(e, 1), :].rearrange("p o c -> p (o c)")
                                      ).then_inc(idx_ready, 1)
                wait_alone(pool, passed, idx_ready, e + 1)
                for c in range(CH):
                    nc.gpsimd.indirect_dma_start(
                        out=xg[k][c][:], out_offset=None, in_=x1_d,
                        in_offset=bass.IndirectOffsetOnAxis(ap=idx[k][:, c:c + 1], axis=0)).then_inc(x_in[k][c], 16)

            def split_h(i, k):
                e = i * 2 + k
                if not (first(i) and k == 0):
                    pool.wait_ge(downed, e)
                pool.wait_ge(h_main, e + 1)
                wait_alone(pool, passed, h_rest, e + 1)
                nc.gpsimd.tensor_scalar(h_s[HI][:], h[:], 1.0, 1.0, ALU.mult, ALU.mult).then_inc(h_part, 1)
                wait_alone(pool, passed, h_part, e + 1)
                nc.gpsimd.tensor_tensor(h_s[LO][:], h[:], h_s[HI][:].bitcast(F32), ALU.subtract).then_inc(h_split, 1)

            def step(i, k):
                for f, n in ((split_h, 1), (gather, 4)):
                    if exists(ahead(i, k, n)[0]):
                        f(*ahead(i, k, n))

            pool.wait_ge(table_ready, 3)
            gather(0, 0)
            gather(0, 1)
            gather(1, 0)
            split_h(0, 0)
            gather(1, 1)
            steps(pool, step)


def stage_combine(nc, passed, x1_d, y_d, comb, wcomb, out):
    with ExitStack() as ctx:
        def sb(name, shape, dt=F32):
            return ctx.enter_context(nc.sbuf_tensor("p5_" + name, shape, dt))

        def sem(name):
            return ctx.enter_context(nc.semaphore("p5_" + name))

        eps = sb("eps", [P, 1])
        x1 = [sb(f"x1{k}", [P, C]) for k in range(2)]
        idx = [sb(f"idx{k}", [P, TOPK], U32) for k in range(2)]
        rows = [[sb(f"rows{k}{n}", [P, C]) for n in range(TOPK)] for k in range(2)]
        acc = [[sb(f"acc{k}{n}", [P, C]) for n in range(2)] for k in range(2)]
        st, mv = sb("st", [P, 6]), sb("mv", [P, 2])
        sd, rstd = sb("sd", [P, 1]), sb("rstd", [P, 1])
        res = [sb(f"res{k}", [P, C]) for k in range(2)]

        x1_in = [sem(f"x1_in{k}") for k in range(2)]
        rows_in = [[sem(f"rows_in{k}{n}") for n in range(TOPK)] for k in range(2)]
        res_out = [sem(f"res_out{k}") for k in range(2)]
        indexed, chain, summed, var_ready, sd_ready, normed, eps_ready = (
            sem("indexed"), sem("chain"), sem("summed"), sem("var_ready"), sem("sd_ready"), sem("normed"), sem("eps_ready"))

        block = ctx.enter_context(nc.Block())

        @block.sync
        def _(sp):
            for k in range(2):
                sp.dma_start(x1[k][:], x1_d[k * P:(k + 1) * P, :]).then_inc(x1_in[k], 16)

            def step(i, last=False):
                for k in range(2):
                    b = i * 2 + k
                    if not last:
                        sp.wait_ge(summed, b + 1)
                        sp.dma_start(x1[k][:], x1_d[bass.ds((b + 2) * P, P), :]).then_inc(x1_in[k], 16)
                    sp.wait_ge(normed, b + 1)
                    sp.dma_start(out[bass.ds(b * P, P), :], res[k][:]).then_inc(res_out[k], 16)

            with sp.Fori(0, NB // 2 - 1) as i:
                step(i)
            step(NB // 2 - 1, last=True)
            for k in range(2):
                sp.wait_ge(res_out[k], 16 * (NB // 2))

        @block.gpsimd
        def _(pool):
            def step(i, first):
                for k in range(2):
                    b = i * 2 + k
                    if not first:
                        pool.wait_ge(summed, b - 1)
                    nc.gpsimd.tensor_copy(idx[k][:], comb[:, bass.ds(b, 1), :].rearrange("p o k -> p (o k)")
                                          ).then_inc(indexed, 1)
                    wait_alone(pool, passed, indexed, b + 1)
                    for n in range(TOPK):
                        nc.gpsimd.indirect_dma_start(
                            out=rows[k][n][:], out_offset=None, in_=y_d,
                            in_offset=bass.IndirectOffsetOnAxis(ap=idx[k][:, n:n + 1], axis=0)).then_inc(rows_in[k][n], 16)

            loop(pool, NB // 2, step)

        @block.vector
        def _(dve):
            nc.vector.memset(eps[:], EPS).then_inc(eps_ready, 1)
            STEPS = TOPK + 1

            def step(i, first):
                for k in range(2):
                    b = i * 2 + k
                    dve.wait_ge(x1_in[k], i * 16 + 16)
                    for n in range(TOPK):
                        dve.wait_ge(rows_in[k][n], i * 16 + 16)
                        src = x1[k] if n == 0 else acc[k][(n - 1) % 2]
                        ins = nc.vector.scalar_tensor_tensor(
                            acc[k][n % 2][:], rows[k][n][:], wcomb[:, bass.ds(b, 1), n:n + 1].rearrange("p o k -> p (o k)"),
                            src[:], ALU.mult, ALU.add)
                        ins.then_inc(chain if n < TOPK - 1 else summed, 1)
                        if n < TOPK - 1:
                            dve.wait_ge(chain, b * STEPS + n + 1)
                        else:
                            dve.wait_ge(summed, b + 1)
                    total = acc[k][(TOPK - 1) % 2]
                    nc.vector.bn_stats(st[:], total[:]).then_inc(chain, 1)
                    wait_alone(dve, passed, chain, b * STEPS + TOPK)
                    nc.vector.bn_aggr(mv[:], st[:]).then_inc(var_ready, 1)
                    dve.wait_ge(sd_ready, b + 1)
                    nc.vector.reciprocal(rstd[:], sd[:]).then_inc(chain, 1)
                    dve.wait_ge(chain, b * STEPS + TOPK + 1)
                    if not first:
                        dve.wait_ge(res_out[k], i * 16)
                    nc.vector.tensor_scalar(res[k][:], total[:], mv[:, 0:1], rstd[:], ALU.subtract, ALU.mult
                                            ).then_inc(normed, 1)

            loop(dve, NB // 2, step)

        @block.scalar
        def _(act):
            act.wait_ge(eps_ready, 1)

            def step(i, first):
                for k in range(2):
                    act.wait_ge(var_ready, i * 2 + k + 1)
                    nc.scalar.activation(sd[:], mv[:, 1:2], ACT.Sqrt, bias=eps[:]).then_inc(sd_ready, 1)

            loop(act, NB // 2, step)


def build(nc, x, wqk, wv, bv, cos, sin, ident, mask, lower, wo, bo, rw, gu, dn, out):
    qk_d = nc.dram_tensor("qk_scratch", [H + HKV, HD, NT, 2, 512], F32, kind="Internal").ap()
    v_d = nc.dram_tensor("v_scratch", [NB, HKV, P, 2, HD], F32, kind="Internal").ap()
    o_d = nc.dram_tensor("o_scratch", [NB, HD, HKV, G, 2, P], F32, kind="Internal").ap()
    x1_d = nc.dram_tensor("x1_scratch", [T, C], F32, kind="Internal").ap()
    slot_d = nc.dram_tensor("slot_scratch", [SLOTS, 1], I32, kind="Internal").ap()
    y_d = nc.dram_tensor("y_scratch", [SLOTS, C], F32, kind="Internal").ap()
    with ExitStack() as ctx:
        comb = ctx.enter_context(nc.sbuf_tensor("comb", [P, NB, TOPK], F32))
        wcomb = ctx.enter_context(nc.sbuf_tensor("wcomb", [P, NB, TOPK], F32))
        passed = ctx.enter_context(nc.semaphore("passed"))
        stage_project(nc, passed, x, wqk, wv, bv, cos, sin, ident, qk_d, v_d)
        with nc.sbuf_tensor("wo_raw", [P, WO_EARLY, C], F32) as wo_raw, nc.semaphore("wo_in") as wo_in:
            stage_attend(nc, passed, ident, mask, qk_d, v_d, o_d, wo, wo_raw, wo_in)
            stage_route(nc, passed, x, wo, bo, rw, ident, lower, o_d, x1_d, slot_d, comb, wcomb, wo_raw, wo_in)
        stage_experts(nc, passed, gu, dn, ident, slot_d, x1_d, y_d)
        stage_combine(nc, passed, x1_d, y_d, comb, wcomb, out)


def constants():
    theta = (1.0 / 10000.0 ** (np.arange(0, HD, 2, dtype=np.float32) / np.float32(HD))).astype(np.float32)
    freqs = (np.arange(T, dtype=np.float32)[:, None] * theta[None, :]).astype(np.float32)
    root = np.float32((1.0 / np.sqrt(H)) ** 0.5)
    cos, sin = (np.cos(freqs) * root).T, (np.sin(freqs) * root).T
    cos = np.concatenate([cos, cos]).astype(np.float32)
    sin = np.concatenate([-sin, sin]).astype(np.float32)
    row, col = np.arange(P)[:, None], np.arange(P)[None, :]
    mask = np.where(col <= row, 0.0, MASKED).astype(np.float32)
    lower = (row < col).astype(np.float32)
    return {"cos": cos, "sin": sin, "ident": np.eye(P, dtype=np.float32), "mask": mask, "lower": lower}


def layout(a):
    x, Wq, bq, Wk, bk, Wv, bv, Wo, bo, rw, gu, dn = a
    wq = Wq.reshape(NC, P, G, HKV, HD // 2, 2).transpose(3, 2, 1, 0, 5, 4).reshape(H, P, NC * HD)
    wk = Wk.reshape(NC, P, HKV, HD // 2, 2).transpose(2, 1, 0, 4, 3).reshape(HKV, P, NC * HD)
    bqh = bq.reshape(G, HKV, HD // 2, 2).transpose(1, 0, 3, 2).reshape(H, HD)
    bkh = bk.reshape(HKV, HD // 2, 2).transpose(0, 2, 1).reshape(HKV, HD)
    wo = Wo.reshape(G, HKV, HD, C).transpose(2, 1, 0, 3).reshape(HD, H, C)
    g, u = gu[:, :, :I], gu[:, :, I:]
    rest = np.concatenate([u[:, :, P:], g[:, :, P:]], 2)
    rest[1::2] = np.concatenate([g[1::2, :, P:], u[1::2, :, P:]], 2)
    cols = np.concatenate([g[:, :, :P], u[:, :, :P], rest], 2)
    cols = cols.reshape(E, NC, P, 3 * P).transpose(0, 2, 1, 3).reshape(E, P, NC * 3 * P)
    return {
        "x": x.reshape(T, C), "wqk": np.concatenate([np.concatenate([wq, wk]), np.concatenate([bqh, bkh])[:, :, None]], 2),
        "wv": Wv.reshape(NC, P, C).transpose(1, 0, 2).reshape(P, NC * C), "bv": bv, "wo": wo, "bo": bo,
        "rw": rw.T.reshape(NC, P, E).transpose(1, 0, 2), "gu": np.concatenate([cols, dn[:, :P, :]], 2),
        "dn": dn[:, P:, :].reshape(E // 2, 2 * IT, C),
    }


_ORDER = ["x", "wqk", "wv", "bv", "cos", "sin", "ident", "mask", "lower", "wo", "bo", "rw", "gu", "dn"]
_INS = ["L0_attn_x", "L0_attn_Wq", "L0_attn_bq", "L0_attn_Wk", "L0_attn_bk", "L0_attn_Wv", "L0_attn_bv", "L0_attn_Wo",
        "L0_attn_bo", "L0_ffn_router_weight", "L0_ffn_gate_up_proj", "L0_ffn_down_proj"]


def kernel(**inputs):
    import concourse.bacc as bacc
    from concourse.bass_utils import run_bass_kernel_spmd

    arrays = layout([np.asarray(inputs[n]) for n in _INS]) | constants()
    nc = bacc.Bacc("TRN2", target_bir_lowering=False, num_devices=1)
    feed, args = {}, []
    for name in _ORDER:
        a = np.ascontiguousarray(arrays[name])
        feed[f"in_{name}"] = a
        args.append(nc.dram_tensor(f"in_{name}", a.shape, mybir.dt.from_np(a.dtype), kind="ExternalInput").ap())
    out = nc.dram_tensor("out", [T, C], F32, kind="ExternalOutput").ap()
    build(nc, *args, out)
    r = run_bass_kernel_spmd(nc, [feed], core_ids=[0])
    return r.results[0]["out"].reshape(1, T, C)
```

```python
from contextlib import ExitStack

import numpy as np

import concourse.bass as bass
from concourse import mybir

F32 = mybir.dt.float32
F32R = mybir.dt.float32r
BF16 = mybir.dt.bfloat16
I32 = mybir.dt.int32
U32 = mybir.dt.uint32
ALU = mybir.AluOpType
ACT = mybir.ActivationFunctionType
AX_X = mybir.AxisListType.X

P = 128
T = 2048
C = 512
H, HKV, HD = 16, 4, 128
G = H // HKV
E, TOPK, CAP = 64, 8, 256
I = 192
IT = I - P
NB = T // P
NC = C // P
NT = T // 512
EPS = 1e-5
MASKED = -1.0e30
HI, LO = 0, 1
SLOTS = E * CAP
CH = CAP // P
WO_EARLY = 12


def loop(eng, n, body):
    body(0, True)
    with eng.Fori(1, n) as i:
        body(i, False)


def wait_alone(eng, passed, sem, value):
    eng.wait_ge(sem, value)
    eng.sem_inc(passed, 1)


def split3(a, b):
    return ((a[LO], b[HI]), (a[HI], b[LO]), (a[HI], b[HI]))


def stage_project(nc, passed, x, wqk, wv, bv, cos, sin, ident_d, qk_d, v_d):
    NH = H + HKV
    with ExitStack() as ctx:
        def sb(name, shape, dt=F32):
            return ctx.enter_context(nc.sbuf_tensor("p1_" + name, shape, dt))

        def ps(name, shape):
            return ctx.enter_context(nc.psum_tensor("p1_" + name, shape, F32))

        def sem(name):
            return ctx.enter_context(nc.semaphore("p1_" + name))

        ident = sb("ident", [P, P])
        xraw = [sb(f"xraw{k}", [P, C]) for k in range(2)]
        xt = [[sb(f"xt{k}{s}", [P, NC, P], F32R) for s in "hl"] for k in range(2)]
        xT = [sb(f"xT{s}", [P, NC, T], F32R) for s in "hl"]
        wv_raw = sb("wv_raw", [P, NC * C])
        wv_s = [sb(f"wv{s}", [P, NC * C], F32R) for s in "hl"]
        WV = [slice(s * NC * C // 2, (s + 1) * NC * C // 2) for s in range(2)]
        bv_b = sb("bv_b", [P, C])
        vfull = [sb(f"vfull{k}", [P, C]) for k in range(2)]
        vout = [sb(f"vout{k}", [P, HKV, 2, HD], F32R) for k in range(2)]
        cosT, sinT = sb("cosT", [P, T]), sb("sinT", [P, T])
        w_raw = [sb(f"w_raw{k}", [P, NC * P + 1]) for k in range(2)]
        bias = [sb(f"bias{k}", [P, 1]) for k in range(2)]
        w_s = [[sb(f"w{k}{s}", [P, NC * P], F32R) for s in "hl"] for k in range(2)]
        qb = [sb(f"qb{k}", [P, 512]) for k in range(2)]
        sw = [sb(f"sw{k}", [P, 512]) for k in range(2)]
        rc = [sb(f"rc{k}", [P, 512]) for k in range(2)]
        rs = [sb(f"rs{k}", [P, 512]) for k in range(2)]
        qr = [sb(f"qr{k}", [P, 512]) for k in range(NT)]
        qout = [sb(f"qout{k}", [P, NT, 2, 512], F32R) for k in range(2)]

        pt = [ps(f"pt{k}", [P, NC, P]) for k in range(2)]
        pv = [ps(f"pv{k}", [P, C]) for k in range(2)]
        pq = [ps(f"pq{k}", [P, 512]) for k in range(NT)]

        x_in = [sem(f"x_in{k}") for k in range(2)]
        ident_in, const_in, bv_in = sem("ident_in"), sem("const_in"), sem("bv_in")
        wv_in = [sem(f"wv_in{s}") for s in range(2)]
        wv_hi, wv_lo = sem("wv_hi"), sem("wv_lo")
        xt_done, xt_hi, xt_lo = sem("xt_done"), sem("xt_hi"), sem("xt_lo")
        hi_kept, lo_kept = sem("hi_kept"), sem("lo_kept")
        v_mm, v_full, v_hi, v_lo = sem("v_mm"), sem("v_full"), sem("v_hi"), sem("v_lo")
        v_out = [sem(f"v_out{k}") for k in range(2)]
        w_in = [sem(f"w_in{k}") for k in range(2)]
        w_hi, w_lo = sem("w_hi"), sem("w_lo")
        q_mm, q_swap, q_prod = sem("q_mm"), sem("q_swap"), sem("q_prod")
        q_rot, q_hi, q_lo = sem("q_rot"), sem("q_hi"), sem("q_lo")
        q_out = [sem(f"q_out{k}") for k in range(2)]

        block = ctx.enter_context(nc.Block())

        @block.sync
        def _(sp):
            sp.dma_start(ident[:], ident_d).then_inc(ident_in, 16)
            for k in range(2):
                sp.dma_start(xraw[k][:], x[k * P:(k + 1) * P, :]).then_inc(x_in[k], 16)
            for s in range(2):
                sp.dma_start(wv_raw[:, WV[s]], wv[:, WV[s]]).then_inc(wv_in[s], 16)
            sp.dma_start(bv_b[:], bv.partition_broadcast(P)).then_inc(bv_in, 16)

            def load_x(tb, k):
                sp.wait_ge(xt_done, tb - 1)
                sp.dma_start(xraw[k][:], x[bass.ds(tb * P, P), :]).then_inc(x_in[k], 16)

            def store_v(tb, k):
                sp.wait_ge(v_lo, tb + 1)
                sp.dma_start(v_d[bass.ds(tb, 1)].rearrange("o j p h d -> p (o j) h d"),
                             vout[k][:].bitcast(F32)).then_inc(v_out[k], 16)

            for k in range(2):
                load_x(2 + k, k)
            for k in range(2):
                sp.dma_start(w_raw[k][:], wqk[k]).then_inc(w_in[k], 16)
            sp.dma_start(cosT[:], cos).then_inc(const_in, 16)
            sp.dma_start(sinT[:], sin).then_inc(const_in, 16)
            with sp.Fori(2, NB // 2) as i:
                for k in range(2):
                    load_x(i * 2 + k, k)
                    store_v(i * 2 + (k - 4), k)
            for tb in range(NB - 4, NB):
                store_v(tb, tb % 2)

            def head_step(i, first, last=False):
                for k in range(2):
                    n = i * 2 + k
                    if not last:
                        sp.wait_ge(w_lo, n + 1)
                        sp.dma_start(w_raw[k][:], wqk[bass.ds(n + 2, 1)].rearrange("o p m -> (o p) m")
                                     ).then_inc(w_in[k], 16)
                    for t in range(NT):
                        sp.wait_ge(q_lo, n * NT + (t + 1))
                        sp.dma_start(qk_d[bass.ds(n, 1), :, t].rearrange("o p h t -> (o p) h t"),
                                     qout[k][:, t].bitcast(F32)).then_inc(q_out[k], 16)

            with sp.Fori(0, NH // 2 - 1) as i:
                head_step(i, False)
            head_step(NH // 2 - 1, False, last=True)
            for k in range(2):
                sp.wait_ge(v_out[k], 16 * (NB // 2))
                sp.wait_ge(q_out[k], 16 * NT * (NH // 2))

        @block.tensor
        def _(pe):
            def transposes(tb, k, i, early):
                pe.wait_ge(x_in[k], i * 16 + 16)
                if not early:
                    pe.wait_ge(xt_lo, tb - 1)
                for c in range(NC):
                    last = nc.tensor.transpose(pt[k][:, c, :], xraw[k][:, c * P:(c + 1) * P], ident[:])
                last.then_inc(xt_done, 1)

            def project_v(tb, k, early):
                pe.wait_ge(xt_lo, tb + 1)
                if not early:
                    pe.wait_ge(v_full, tb - 1)
                for n, (a, b) in enumerate(split3(xt[k], wv_s)):
                    for c in range(NC):
                        last = nc.tensor.matmul(pv[k][:], a[:, c, :], b[:, c * C:(c + 1) * C],
                                                start=(n == 0 and c == 0), stop=(n == 2 and c == NC - 1))
                last.then_inc(v_mm, 1)

            pe.wait_ge(ident_in, 16)
            transposes(0, 0, 0, True)
            transposes(1, 1, 0, True)
            pe.wait_ge(wv_lo, 2)
            project_v(0, 0, True)
            transposes(2, 0, 1, False)
            project_v(1, 1, True)
            with pe.Fori(1, NB // 2 - 1) as i:
                transposes(i * 2 + 1, 1, i, False)
                project_v(i * 2, 0, False)
                transposes(i * 2 + 2, 0, i + 1, False)
                project_v(i * 2 + 1, 1, False)
            transposes(NB - 1, 1, NB // 2 - 1, False)
            project_v(NB - 2, 0, False)
            project_v(NB - 1, 1, False)

            def head_step(i, first):
                for k in range(2):
                    n = i * 2 + k
                    pe.wait_ge(w_lo, n + 1)
                    for t in range(NT):
                        if first and k == 0:
                            pe.wait_ge(hi_kept, (t + 1) * NB // NT)
                            pe.wait_ge(lo_kept, (t + 1) * NB // NT)
                        else:
                            pe.wait_ge(q_swap, n * NT + t - NT + 1)
                        for m, (a, b) in enumerate(split3(w_s[k], xT)):
                            for c in range(NC):
                                last = nc.tensor.matmul(pq[t][:], a[:, c * P:(c + 1) * P],
                                                        b[:, c, t * 512:(t + 1) * 512],
                                                        start=(m == 0 and c == 0), stop=(m == 2 and c == NC - 1))
                        last.then_inc(q_mm, 1)

            loop(pe, NH // 2, head_step)

        @block.scalar
        def _(act):
            for s in range(2):
                act.wait_ge(wv_in[s], 16)
                nc.scalar.copy(wv_s[HI][:, WV[s]], wv_raw[:, WV[s]]).then_inc(wv_hi, 1)

            def x_hi(tb, k, early):
                act.wait_ge(xt_done, tb + 1)
                if not early:
                    act.wait_ge(v_mm, tb - 1)
                    act.wait_ge(hi_kept, tb - 1)
                    act.wait_ge(lo_kept, tb - 1)
                nc.scalar.copy(xt[k][HI][:], pt[k][:]).then_inc(xt_hi, 1)

            def v_hi_part(tb, k, i, early):
                act.wait_ge(v_full, tb + 1)
                if not early:
                    act.wait_ge(v_out[k], i * 16)
                nc.scalar.copy(vout[k][:, :, HI, :], vfull[k][:].rearrange("p (j d) -> p j d", j=HKV)
                               ).then_inc(v_hi, 1)

            for k in range(2):
                x_hi(k, k, True)
            for k in range(2):
                x_hi(2 + k, k, False)
                v_hi_part(k, k, 0, True)
            with act.Fori(1, NB // 2 - 1) as i:
                for k in range(2):
                    x_hi(i * 2 + (2 + k), k, False)
                    v_hi_part(i * 2 + k, k, i, False)
            def weights_hi(n, k, i, early):
                act.wait_ge(w_in[k], i * 16 + 16)
                if not early:
                    act.wait_ge(q_mm, n * NT - NT)
                    act.wait_ge(q_swap, n * NT - NT)
                nc.scalar.copy(bias[k][:], w_raw[k][:, NC * P:])
                nc.scalar.copy(w_s[k][HI][:], w_raw[k][:, 0:NC * P]).then_inc(w_hi, 1)

            def swap(q, n, k, t, early):
                act.wait_ge(q_mm, q + 1)
                if not early:
                    act.wait_ge(q_prod, q - 1)
                half = HD // 2
                if t == 0:
                    act.wait_ge(w_hi, n + 1)
                nc.scalar.activation(qb[t % 2][:], pq[t][:], ACT.Identity, bias=bias[k][:])
                nc.scalar.activation(sw[t % 2][0:half, :], pq[t][half:P, :], ACT.Identity, bias=bias[k][half:P])
                nc.scalar.activation(sw[t % 2][half:P, :], pq[t][0:half, :], ACT.Identity, bias=bias[k][0:half]
                                     ).then_inc(q_swap, 1)

            def q_hi_part(q, k, t, i, early):
                act.wait_ge(q_rot, q + 1)
                if t == 0 and not early:
                    act.wait_ge(q_out[k], i * (16 * NT))
                nc.scalar.copy(qout[k][:, t, HI, :], qr[t][:]).then_inc(q_hi, 1)

            weights_hi(0, 0, 0, True)
            for k in range(2):
                v_hi_part(NB - 2 + k, k, NB // 2 - 1, False)

            def head_step(i, first, last=False):
                for k in range(2):
                    n = i * 2 + k
                    for t in range(NT):
                        q = i * (2 * NT) + (k * NT + t)
                        swap(q, n, k, t, first and k == 0 and t < 2)
                        if t >= 2:
                            q_hi_part(q - 2, k, t - 2, i, first)
                        elif k > 0:
                            q_hi_part(q - 2, 0, t + NT - 2, i, first)
                        elif not first:
                            q_hi_part(q - 2, 1, t + NT - 2, i, False)
                        if t == 0 and not (last and k == 1):
                            weights_hi(n + 1, 1 - k, i + k, first and k == 0)

            head_step(0, True)
            with act.Fori(1, NH // 2 - 1) as i:
                head_step(i, False)
            head_step(NH // 2 - 1, False, last=True)
            for t in (NT - 2, NT - 1):
                q_hi_part(NH * NT - NT + t, 1, t, NH // 2 - 1, False)

        @block.vector
        def _(dve):
            for s in range(2):
                dve.wait_ge(wv_hi, s + 1)
                nc.vector.tensor_tensor(wv_s[LO][:, WV[s]], wv_raw[:, WV[s]], wv_s[HI][:, WV[s]].bitcast(F32), ALU.subtract
                                        ).then_inc(wv_lo, 1)
            dve.wait_ge(bv_in, 16)

            def x_lo(tb, k):
                dve.wait_ge(xt_hi, tb + 1)
                nc.vector.tensor_tensor(xt[k][LO][:], pt[k][:], xt[k][HI][:].bitcast(F32), ALU.subtract
                                        ).then_inc(xt_lo, 1)

            def keep_lo(tb, k):
                dve.wait_ge(xt_lo, tb + 1)
                nc.vector.tensor_copy(xT[LO][:, :, bass.ds(tb * P, P)], xt[k][LO][:].bitcast(F32)).then_inc(lo_kept, 1)

            def v_bias(tb, k, early):
                dve.wait_ge(v_mm, tb + 1)
                if not early:
                    dve.wait_ge(v_lo, tb - 1)
                nc.vector.tensor_tensor(vfull[k][:], pv[k][:], bv_b[:], ALU.add).then_inc(v_full, 1)

            def v_lo_part(tb, k):
                dve.wait_ge(v_hi, tb + 1)
                nc.vector.tensor_tensor(vout[k][:, :, LO, :], vfull[k][:].rearrange("p (j d) -> p j d", j=HKV),
                                        vout[k][:, :, HI, :].bitcast(F32), ALU.subtract).then_inc(v_lo, 1)

            for k in range(2):
                x_lo(k, k)
                keep_lo(k, k)

            def step(i, first):
                for k in range(2):
                    tb = i * 2 + k
                    x_lo(tb + 2, k)
                    v_bias(tb, k, first)
                    keep_lo(tb + 2, k)
                    v_lo_part(tb, k)

            step(0, True)
            with dve.Fori(1, NB // 2 - 1) as i:
                step(i, False)
            def weights_lo(n, k):
                dve.wait_ge(w_hi, n + 1)
                nc.vector.tensor_tensor(w_s[k][LO][:], w_raw[k][:, 0:NC * P], w_s[k][HI][:].bitcast(F32), ALU.subtract
                                        ).then_inc(w_lo, 1)

            def q_products(q, t, early):
                dve.wait_ge(q_swap, q + 1)
                if not early:
                    dve.wait_ge(q_rot, q - 1)
                k, cols = t % 2, slice(t * 512, (t + 1) * 512)
                nc.vector.tensor_tensor(rc[k][:], qb[k][:], cosT[:, cols], ALU.mult)
                nc.vector.tensor_tensor(rs[k][:], sw[k][:], sinT[:, cols], ALU.mult).then_inc(q_prod, 1)

            def q_lo_part(q, k, t):
                dve.wait_ge(q_hi, q + 1)
                nc.vector.tensor_tensor(qout[k][:, t, LO, :], qr[t][:], qout[k][:, t, HI, :].bitcast(F32),
                                        ALU.subtract).then_inc(q_lo, 1)

            weights_lo(0, 0)
            for k in range(2):
                v_bias(NB - 2 + k, k, False)
                v_lo_part(NB - 2 + k, k)
            dve.wait_ge(const_in, 32)

            def head_step(i, first, last=False):
                for k in range(2):
                    n = i * 2 + k
                    for t in range(NT):
                        q_products(n * NT + t, t, first and k == 0 and t < 2)
                        if t >= 2:
                            q_lo_part(n * NT + (t - 2), k, t - 2)
                        elif k > 0:
                            q_lo_part(n * NT + (t - 2), 0, t + NT - 2)
                        elif not first:
                            q_lo_part(n * NT + (t - 2), 1, t + NT - 2)
                        if t == 0 and not (last and k == 1):
                            weights_lo(n + 1, 1 - k)

            head_step(0, True)
            with dve.Fori(1, NH // 2 - 1) as i:
                head_step(i, False)
            head_step(NH // 2 - 1, False, last=True)
            for t in (NT - 2, NT - 1):
                q_lo_part(NH * NT - NT + t, 1, t)

        @block.gpsimd
        def _(pool):
            def keep_hi(i, first):
                for k in range(2):
                    wait_alone(pool, passed, xt_hi, i * 2 + (k + 1))
                    nc.gpsimd.tensor_copy(xT[HI][:, :, bass.ds((i * 2 + k) * P, P)], xt[k][HI][:].bitcast(F32)
                                          ).then_inc(hi_kept, 1)

            loop(pool, NB // 2, keep_hi)

            def sum_products(i, first):
                for k in range(2):
                    for t in range(NT):
                        q = i * (2 * NT) + (k * NT + t)
                        pool.wait_ge(q_prod, q + 1)
                        if not (first and k == 0):
                            pool.wait_ge(q_lo, q - (NT - 1))
                        nc.gpsimd.tensor_tensor(qr[t][:], rc[t % 2][:], rs[t % 2][:], ALU.add).then_inc(q_rot, 1)

            loop(pool, NH // 2, sum_products)


def stage_attend(nc, passed, ident_d, mask_d, qk_d, v_d, o_d, wo, wo_raw, wo_in):
    U = NB * G
    blk = lambda u: u // G
    width = lambda u: (blk(u) + 1) * P
    ngrp = lambda u: 1 if width(u) <= 1024 else 2
    ntr = lambda u: -(-(blk(u) + 1) // 4)
    SG = [0]
    TG = [0]
    for u in range(U):
        SG.append(SG[-1] + ngrp(u))
        TG.append(TG[-1] + ntr(u))
    PAIRS = U // 2
    KEEP = 5
    LAG = 3
    WEIGH = LAG + 2
    OUT = WEIGH + 2

    def score_group(u, a):
        return (u % 2) if ngrp(u) == 1 else a

    before, last_use = {}, {}
    for u in [u - U for u in range(U)] + list(range(U)):
        for a in range(ngrp(u % U)):
            s = score_group(u % U, a)
            before[(u, a)] = last_use.get(s)
            last_use[s] = SG[u % U] + a - (SG[U] if u < 0 else 0)

    with ExitStack() as ctx:
        def sb(name, shape, dt=F32):
            return ctx.enter_context(nc.sbuf_tensor("p2_" + name, shape, dt))

        def ps(name, shape):
            return ctx.enter_context(nc.psum_tensor("p2_" + name, shape, F32))

        def sem(name):
            return ctx.enter_context(nc.semaphore("p2_" + name))

        ident = sb("ident", [P, P])
        identb = sb("identb", [P, P], BF16)
        maskb = sb("maskb", [P, P], BF16)
        maskf = sb("maskf", [P, P])
        kT = sb("kT", [P, NT, 2, 512], F32R)
        v = sb("v", [P, NB, 2, HD], F32R)
        k_next = sb("k_next", [P, 2, 512], F32R)
        v_next = sb("v_next", [P, 4, 2, HD], F32R)
        q = [sb(f"q{k}", [P, G, 2, 512], F32R) for k in range(2)]
        prob = [sb(f"prob{k}", [P, T]) for k in range(KEEP)]
        pT = [[sb(f"pT{k}{s}", [P, NB, 2, P], F32R) for s in "hl"] for k in range(2)]
        oT = [sb(f"oT{k}", [P, 2, 2, P], F32R) for k in range(2)]
        nmax, nmax1 = sb("nmax", [P, KEEP]), sb("nmax1", [P, KEEP])
        nm = sb("nm", [P, KEEP])
        rsum = sb("rsum", [P, KEEP, 2])
        part = sb("part", [P, KEEP])
        den = sb("den", [P, KEEP])
        inv = sb("inv", [P, KEEP])

        S = ps("S", [P, 2, 1024])
        TP = [ps(f"TP{k}", [P, 4, P]) for k in range(2)]
        O = [ps(f"O{k}", [P, 2, P]) for k in range(2)]

        const_in, const_ready = sem("const_in"), sem("const_ready")
        next_in, k_first, v_first, v_free = sem("next_in"), sem("k_first"), sem("v_first"), sem("v_free")
        k_in = [None] + [sem(f"k_in{c}") for c in range(1, NT)]
        v_in = [None] + [sem(f"v_in{c}") for c in range(1, NT)]
        q_in = [sem(f"q_in{k}") for k in range(2)]
        q_first = [sem(f"q_first{g}") for g in range(G - 1)]
        scored, max_part, max_ready, exped = sem("scored"), sem("max_part"), sem("max_ready"), sem("exped")
        den_ready, inv_ready, normed = sem("den_ready"), sem("inv_ready"), sem("normed")
        turned, turn_hi, turn_lo = sem("turned"), sem("turn_hi"), sem("turn_lo")
        weighed, o_hi, o_lo = sem("weighed"), sem("o_hi"), sem("o_lo")
        o_out = [sem(f"o_out{k}") for k in range(2)]
        FREE = 2

        block = ctx.enter_context(nc.Block())

        def load_q(sp, j, tc):
            sp.dma_start(q[tc % 2][:].bitcast(F32), qk_d[bass.ds(j * G, G), :, tc]
                         .rearrange("g p h t -> p g h t")).then_inc(q_in[tc % 2], 16)

        def load_next(sp, j):
            sp.dma_start(k_next[:].bitcast(F32), qk_d[bass.ds(j + H, 1), :, 0].rearrange("o p h t -> (o p) h t")
                         ).then_inc(next_in, 16)
            sp.dma_start(v_next[:].bitcast(F32), v_d[0:4, bass.ds(j, 1)].rearrange("b o p h d -> (o p) b h d")
                         ).then_inc(next_in, 16)

        def load_k(sp, j, c):
            sp.dma_start(kT[:, c].bitcast(F32), qk_d[bass.ds(j + H, 1), :, c].rearrange("o p h t -> (o p) h t")
                         ).then_inc(k_in[c], 16)

        def load_v(sp, j, c):
            sp.dma_start(v[:, c * 4:(c + 1) * 4, :, :].bitcast(F32), v_d[c * 4:(c + 1) * 4, bass.ds(j, 1)]
                         .rearrange("b o p h d -> (o p) b h d")).then_inc(v_in[c], 16)

        def lagged(i, lag, first):
            u = i - lag
            return (u, 0) if u >= 0 else None if first else (u + U, 1)

        def steps(eng, step, tail):
            def body(j, first):
                for i in range(U):
                    step(j, i, first)
            loop(eng, HKV, body)
            for i in range(U, U + tail + 1):
                step(HKV - 1, i, False)

        @block.sync
        def _(sp):
            sp.dma_start(ident[:], ident_d).then_inc(const_in, 16)
            sp.dma_start(maskf[:], mask_d).then_inc(const_in, 16)
            load_next(sp, 0)
            for g in range(G):
                sp.dma_start(q[0][:, g].bitcast(F32), qk_d[g, :, 0]).then_inc(q_first[g] if g < G - 1 else q_in[0], 16)

            def store(j, p):
                b, g = blk(2 * p), 2 * p % G
                sp.wait_ge(o_lo, j * PAIRS + (p + 1 + FREE))
                sp.dma_start(o_d[b, :, bass.ds(j, 1), g:g + 2].rearrange("p o g h t -> p (o g) h t"),
                             oT[p % 2][:].bitcast(F32)).then_inc(o_out[p % 2], 16)

            def head(j, first=False, last=False):
                if not first:
                    sp.wait_ge(scored, j * SG[U])
                load_k(sp, j, 1)
                load_q(sp, j, 1)
                if not first:
                    store(j - 1, PAIRS - 2)
                    store(j - 1, PAIRS - 1)
                    sp.wait_ge(weighed, j * PAIRS + FREE)
                load_v(sp, j, 1)
                for p in range(PAIRS - 2):
                    store(j, p)
                    if p in (1, 8):
                        load_k(sp, j, 2 + p // 8)
                    if p in (3, 9):
                        load_v(sp, j, 2 + p // 8)
                    if p == 5 and not last:
                        sp.wait_ge(k_first, j + 1)
                        sp.wait_ge(v_first, j + 1)
                        load_next(sp, j + 1)
                    if p in (6, 14, 22):
                        tc = p // 8
                        sp.wait_ge(scored, j * SG[U] + SG[16 * tc + 16])
                        if tc < 2:
                            load_q(sp, j, tc + 2)
                        elif not last:
                            load_q(sp, j + 1, 0)

            head(0, first=True)
            with sp.Fori(1, HKV - 1) as j:
                head(j)
            sp.dma_start(wo_raw[:], wo[:, 0:WO_EARLY, :]).then_inc(wo_in, 16)
            head(HKV - 1, last=True)
            for p in (PAIRS - 2, PAIRS - 1):
                store(HKV - 1, p)
            for k in range(2):
                sp.wait_ge(o_out[k], HKV * (8 * PAIRS))

        @block.tensor
        def _(pe):
            def scores(j, u, a, first):
                b, g, tc = blk(u), u % G, u // 16
                if u == 0:
                    pe.wait_ge(k_first, j + 1)
                elif u % 16 == 0 and a == 0:
                    pe.wait_ge(k_in[tc], j * 16 + 16)
                if first and u < G - 1:
                    pe.wait_ge(q_first[u], 16)
                if a == 0 and u % 16 == (G - 1 if first and tc == 0 else 0):
                    pe.wait_ge(q_in[tc % 2], j * 32 + (16 + 16 * (tc // 2)))
                qs = [q[tc % 2][:, g, s, (b % 4) * P:(b % 4 + 1) * P] for s in (HI, LO)]
                if not (first and before[(u, a)] < 0):
                    pe.wait_ge(exped, j * SG[U] + (before[(u, a)] + 1))
                s = score_group(u, a)
                for c0 in range(a * 1024, min(width(u), a * 1024 + 1024), 512):
                    w = min(512, width(u) - c0)
                    out = S[:, s, c0 - a * 1024:c0 - a * 1024 + w]
                    for n, (x, y) in enumerate(split3(qs, [kT[:, c0 // 512, s2, 0:w] for s2 in (HI, LO)])):
                        mm = nc.tensor.matmul(out, x, y, start=(n == 0), stop=(n == 2))
                    if c0 + w == width(u):
                        mm = nc.tensor.matmul(S[:, s, width(u) - P - a * 1024:width(u) - a * 1024], identb[:],
                                              maskb[:], start=False, stop=True, skip_group_check=True)
                mm.then_inc(scored, 1)

            def turn(j, back, u, t):
                if t % 2 == 0:
                    pe.wait_ge(normed, j * SG[U] + (SG[u] + t // 2 + 1 - back * SG[U]))
                n = TG[u] + t
                pe.wait_ge(turn_lo, j * TG[U] + (n + 1 - back * TG[U]))
                for s in range(4 * t, min(4 * t + 4, blk(u) + 1)):
                    mm = nc.tensor.transpose(TP[n % 2][:, s % 4, :], prob[u % KEEP][:, s * P:(s + 1) * P], ident[:])
                mm.then_inc(turned, 1)

            def weigh(j, back, p, part, half=None):
                nb = blk(2 * p) + 1
                cut = (nb + 1) // 2
                lo, hi = ((0, cut), (cut, nb))[part]
                mid = {None: hi, 0: (lo + hi) // 2, 1: (lo + hi) // 2}[half]
                if part == 0 and half != 1:
                    if p == 0:
                        pe.wait_ge(v_first, j + 1)
                    elif p % 8 == 0:
                        pe.wait_ge(v_in[p // 8], j * 16 + 16)
                    pe.wait_ge(turn_lo, j * TG[U] + (TG[2 * p + 2] + FREE - back * TG[U]))
                    pe.wait_ge(o_lo, j * PAIRS + (p + 1 - back * PAIRS))
                for s in range(mid, hi) if half == 1 else range(lo, mid):
                    for n, (x, y) in enumerate(split3([v[:, s, h, :] for h in (HI, LO)],
                                                      [pT[p % 2][h][:, s, :, :] for h in (HI, LO)])):
                        mm = nc.tensor.matmul(O[p % 2][:], x, y, start=(s == 0 and n == 0),
                                              stop=(s == nb - 1 and n == 2))
                        if s == nb - 1 and n == 2:
                            mm.then_inc(weighed, 1)
                        elif p == PAIRS - 1 and s == cut - 1 and n == 2:
                            mm.then_inc(v_free, 1)

            def step(j, i, first):
                at = lagged(i, LAG, first)
                turns = [(j, at[1], at[0], t) for t in range(ntr(at[0]))] if at and i < U + LAG else []
                at = lagged(i, WEIGH, first)
                halves = [None]
                if len(turns) > 2 and (i >= U or ngrp(i) == 1):
                    halves = [0, 1]
                if i < U and len(halves) == 1:
                    scores(j, i, 0, first)
                if len(halves) == 2:
                    weigh(j, at[1], at[0] // 2, at[0] % 2, 0)
                for args in turns[0:2]:
                    turn(*args)
                if i < U and len(halves) == 2:
                    scores(j, i, 0, first)
                if i < U and ngrp(i) == 2:
                    scores(j, i, 1, first)
                if at and i < U + WEIGH:
                    weigh(j, at[1], at[0] // 2, at[0] % 2, halves[-1])
                for args in turns[2:]:
                    turn(*args)

            pe.wait_ge(const_ready, 2)
            steps(pe, step, WEIGH - 1)

        @block.scalar
        def _(act):
            act.wait_ge(const_in, 32)
            nc.scalar.copy(identb[:], ident[:]).then_inc(const_ready, 1)
            nc.scalar.copy(maskb[:], maskf[:]).then_inc(const_ready, 1)
            act.sem_inc(weighed, FREE)

            def exp(j, u, a):
                k = u % KEEP
                act.wait_ge(max_ready, j * SG[U] + (SG[u] + a + 1))
                if a == 1:
                    nc.scalar.activation(part[:, k:k + 1], nmax[:, k:k + 1], ACT.Exp, scale=-1.0, bias=nm[:, k:k + 1])
                w = min(1024, width(u) - a * 1024)
                top = nm if a == ngrp(u) - 1 else nmax
                nc.scalar.activation(prob[k][:, a * 1024:a * 1024 + w], S[:, score_group(u, a), 0:w], ACT.Exp,
                                     bias=top[:, k:k + 1], accum_out=rsum[:, k, a:a + 1]).then_inc(exped, 1)

            def p_hi(j, back, u, t):
                n, p = TG[u] + t, u // 2
                act.wait_ge(turned, j * TG[U] + (n + 1 - back * TG[U]))
                if u % 2 == 0 and t == 0:
                    act.wait_ge(weighed, j * PAIRS + (p + 1 - back * PAIRS))
                m = min(4, blk(u) + 1 - 4 * t)
                nc.scalar.copy(pT[p % 2][HI][:, 4 * t:4 * t + m, u % 2, :], TP[n % 2][:, 0:m, :]).then_inc(turn_hi, 1)

            def out_hi(j, back, p, first):
                act.wait_ge(weighed, j * PAIRS + (p + 1 + FREE - back * PAIRS))
                if not (first and p < 2):
                    act.wait_ge(o_out[p % 2], j * (8 * PAIRS) + (16 * (p // 2) - back * 8 * PAIRS))
                nc.scalar.copy(oT[p % 2][:, :, HI, :], O[p % 2][:]).then_inc(o_hi, 1)

            def step(j, i, first):
                at = lagged(i, OUT, first)
                if at and i % 2 == OUT % 2:
                    out_hi(j, at[1], at[0] // 2, first)
                at = lagged(i, LAG, first)
                turns = [(j, at[1], at[0], t) for t in range(ntr(at[0]))] if at and i < U + LAG else []
                for a in range(2):
                    for args in turns[2 * a:2 * a + 2]:
                        p_hi(*args)
                    if i < U and a < ngrp(i):
                        exp(j, i, a)

            steps(act, step, OUT - 2)

        @block.vector
        def _(dve):
            dve.sem_inc(turn_lo, FREE)
            dve.sem_inc(o_lo, FREE)

            def take_k(j):
                dve.wait_ge(next_in, j * 32 + 32)
                nc.vector.tensor_copy(kT[:, 0], k_next[:].bitcast(F32)).then_inc(k_first, 1)

            def take_v(j, first):
                if not first:
                    dve.wait_ge(v_free, j)
                nc.vector.tensor_copy(v[:, 0:4], v_next[:].bitcast(F32)).then_inc(v_first, 1)

            def row_max(j, u, a):
                k, wide = u % KEEP, ngrp(u) == 2
                dve.wait_ge(scored, j * SG[U] + (SG[u] + a + 1))
                w = min(1024, width(u) - a * 1024)
                out = (nmax if a == 0 else nmax1) if wide else nm
                r = nc.vector.reduce_max(out[:, k:k + 1], S[:, score_group(u, a), 0:w], AX_X, negate=True)
                r.then_inc(max_part if a == 1 else max_ready, 1)
                if a == 1:
                    dve.wait_ge(max_part, j * (SG[U] - U) + (SG[u + 1] - u - 1))
                    nc.vector.tensor_tensor(nm[:, k:k + 1], nmax[:, k:k + 1], nmax1[:, k:k + 1], ALU.min
                                            ).then_inc(max_ready, 1)

            def recip(j, back, u):
                k = u % KEEP
                dve.wait_ge(exped, j * SG[U] + (SG[u + 1] - back * SG[U]))
                if ngrp(u) == 1:
                    nc.vector.reciprocal(inv[:, k:k + 1], rsum[:, k, 0:1]).then_inc(inv_ready, 1)
                else:
                    nc.vector.scalar_tensor_tensor(den[:, k:k + 1], rsum[:, k, 0:1], part[:, k:k + 1], rsum[:, k, 1:2],
                                                   ALU.mult, ALU.add).then_inc(den_ready, 1)
                    dve.wait_ge(den_ready, j * (SG[U] - U) + (SG[u + 1] - u - 1 - back * (SG[U] - U)))
                    nc.vector.reciprocal(inv[:, k:k + 1], den[:, k:k + 1]).then_inc(inv_ready, 1)

            def p_lo(j, back, u, t):
                n, p = TG[u] + t, u // 2
                dve.wait_ge(turn_hi, j * TG[U] + (n + 1 - back * TG[U]))
                m = min(4, blk(u) + 1 - 4 * t)
                nc.vector.tensor_tensor(pT[p % 2][LO][:, 4 * t:4 * t + m, u % 2, :], TP[n % 2][:, 0:m, :],
                                        pT[p % 2][HI][:, 4 * t:4 * t + m, u % 2, :].bitcast(F32), ALU.subtract
                                        ).then_inc(turn_lo, 1)

            def out_lo(j, back, p):
                dve.wait_ge(o_hi, j * PAIRS + (p + 1 - back * PAIRS))
                nc.vector.tensor_tensor(oT[p % 2][:, :, LO, :], O[p % 2][:], oT[p % 2][:, :, HI, :].bitcast(F32),
                                        ALU.subtract).then_inc(o_lo, 1)

            def step(j, i, first):
                if i == 0:
                    take_k(j)
                if i == (0 if first else WEIGH - 1):
                    take_v(j, first)
                at = lagged(i, OUT, first)
                if at and i % 2 == OUT % 2:
                    out_lo(j, at[1], at[0] // 2)
                former, at = lagged(i, 1, first), lagged(i, LAG, first)
                turns = [(j, at[1], at[0], t) for t in range(ntr(at[0]))] if at and i < U + LAG else []
                if i < U:
                    row_max(j, i, 0)
                if former and i < U + 1:
                    recip(j, former[1], former[0])
                for args in turns[0:2]:
                    p_lo(*args)
                if i < U and ngrp(i) == 2:
                    row_max(j, i, 1)
                for args in turns[2:]:
                    p_lo(*args)

            steps(dve, step, OUT - 2)

        @block.gpsimd
        def _(pool):
            def step(j, first):
                for u in range(U):
                    k = u % KEEP
                    wait_alone(pool, passed, inv_ready, j * U + (u + 1))
                    for a in range(ngrp(u)):
                        cols = slice(a * 1024, min(width(u), a * 1024 + 1024))
                        scale = part[:, k:k + 1] if a < ngrp(u) - 1 else 1.0
                        nc.gpsimd.tensor_scalar(prob[k][:, cols], prob[k][:, cols], inv[:, k:k + 1], scale,
                                                ALU.mult, ALU.mult).then_inc(normed, 1)

            loop(pool, HKV, step)


def stage_route(nc, passed, x, wo, bo, rw, ident_d, lower_d, o_d, x1_d, slot_d, comb, wcomb, wo_raw, wo_in):
    with ExitStack() as ctx:
        def sb(name, shape, dt=F32):
            return ctx.enter_context(nc.sbuf_tensor("p3_" + name, shape, dt))

        def ps(name, shape):
            return ctx.enter_context(nc.psum_tensor("p3_" + name, shape, F32))

        def sem(name):
            return ctx.enter_context(nc.semaphore("p3_" + name))

        PARTS = 4
        wo_last = sb("wo_last", [P, H - WO_EARLY, C])
        wo_s = [sb(f"wo{s}", [P, H, C], F32R) for s in "hl"]
        ident, lower, ones = sb("ident", [P, P]), sb("lower", [P, P]), sb("ones", [P, P])
        bo_b = sb("bo_b", [P, C])
        rwT = sb("rwT", [P, NC, E])
        eps = sb("eps", [P, 1])
        iota_e = sb("iota_e", [P, E])
        tok = [sb(f"tok{k}", [P, 1], I32) for k in range(2)]
        zero = sb("zero", [P, SLOTS // P], I32)
        ot = [sb(f"ot{k}", [P, H, 2, P], F32R) for k in range(2)]
        xr = [sb(f"xr{k}", [P, C]) for k in range(2)]
        xb = [sb(f"xb{k}", [P, C]) for k in range(2)]
        h = [sb(f"h{k}", [P, C]) for k in range(2)]
        st = sb("st", [P, 6])
        mv = sb("mv", [P, 2])
        sd, rstd = sb("sd", [P, 1]), sb("rstd", [P, 1])
        x1 = [sb(f"x1{k}", [P, C]) for k in range(2)]
        x1T = sb("x1T", [P, NC, P])
        top, topi, topf = sb("top", [P, TOPK]), sb("topi", [P, TOPK], U32), sb("topf", [P, TOPK])
        ntop, et, esum, einv = sb("ntop", [P, 1]), sb("et", [P, TOPK]), sb("esum", [P, 1]), sb("einv", [P, 1])
        hot = sb("hot", [P, TOPK, E])
        mask = sb("mask", [P, E])
        count = sb("count", [P, E])
        posn = sb("posn", [P, E])
        pick = sb("pick", [P, TOPK, E])
        pos = sb("pos", [P, TOPK])
        slot, over, wk, keep = sb("slot", [P, TOPK]), sb("over", [P, TOPK]), sb("wk", [P, TOPK]), sb("keep", [P, TOPK])
        slot_out = sb("slot_out", [P, TOPK])
        slot_i = [sb(f"slot_i{k}", [P, TOPK], U32) for k in range(2)]

        acc = [ps(f"acc{k}", [P, C]) for k in range(2)]
        xtp = ps("xtp", [P, NC, P])
        lg = ps("lg", [P, E])
        cum = ps("cum", [P, E])
        tot = ps("tot", [P, E])

        const_in, zeroed, ones_ready = sem("const_in"), sem("zeroed"), sem("ones_ready")
        wo_last_in, wo_hi, wo_lo = sem("wo_last_in"), sem("wo_hi"), sem("wo_lo")
        ot_in = [[sem(f"ot_in{k}{s}") for s in range(2)] for k in range(2)]
        xr_in = [sem(f"xr_in{k}") for k in range(2)]
        biased, projected, normed = sem("biased"), sem("projected"), sem("normed")
        norm_step, choose_step, place_step = sem("norm_step"), sem("choose_step"), sem("place_step")
        var_ready, sd_ready = sem("var_ready"), sem("sd_ready")
        x1_out = [sem(f"x1_out{k}") for k in range(2)]
        turned, copied, routed, topped, exped = sem("turned"), sem("copied"), sem("routed"), sem("topped"), sem("exped")
        masked, summed, placed = sem("masked"), sem("summed"), sem("placed")
        scattered = [sem(f"scattered{k}") for k in range(2)]
        iota_ready, tok_next = sem("iota_ready"), sem("tok_next")

        block = ctx.enter_context(nc.Block())

        def wo_part(n):
            return wo_raw[:, n * H // PARTS:(n + 1) * H // PARTS, :] if n < PARTS - 1 else wo_last[:]

        def load_block(sp, b, k):
            for s in range(2):
                sp.dma_start(ot[k][:, s * H // 2:(s + 1) * H // 2].bitcast(F32),
                             o_d[bass.ds(b, 1), :, s * HKV // 2:(s + 1) * HKV // 2]
                             .rearrange("o p j g h t -> (o p) (j g) h t")).then_inc(ot_in[k][s], 16)
            sp.dma_start(xr[k][:], x[bass.ds(b * P, P), :]).then_inc(xr_in[k], 16)

        @block.sync
        def _(sp):
            load_block(sp, 0, 0)
            sp.dma_start(wo_last[:], wo[:, WO_EARLY:, :]).then_inc(wo_last_in, 16)
            sp.dma_start(bo_b[:], bo.partition_broadcast(P)).then_inc(const_in, 16)
            sp.dma_start(ident[:], ident_d).then_inc(const_in, 16)
            sp.dma_start(rwT[:], rw).then_inc(const_in, 16)
            sp.dma_start(lower[:], lower_d).then_inc(const_in, 16)
            load_block(sp, 1, 1)
            sp.wait_ge(zeroed, 1)
            sp.dma_start(slot_d.rearrange("(p s) o -> p (s o)", p=P), zero[:]).then_inc(zeroed, 16)

            def step(i, last=False):
                for k in range(2):
                    b = i * 2 + k
                    if not last:
                        sp.wait_ge(projected, b + 1)
                        sp.wait_ge(biased, b + 1)
                        load_block(sp, b + 2, k)
                    sp.wait_ge(normed, b + 1)
                    sp.dma_start(x1_d[bass.ds(b * P, P), :], x1[k][:]).then_inc(x1_out[k], 16)

            with sp.Fori(0, NB // 2 - 1) as i:
                step(i)
            step(NB // 2 - 1, last=True)
            for k in range(2):
                sp.wait_ge(x1_out[k], 16 * (NB // 2))

        @block.tensor
        def _(pe):
            PART = H // PARTS

            def project(b, k, heads, first):
                for n in heads:
                    if first and n % PART == 0:
                        pe.wait_ge(wo_lo, n // PART + 1)
                    for m, (a, w) in enumerate(split3([ot[k][:, n, s, :] for s in (HI, LO)],
                                                      [wo_s[s][:, n, :] for s in (HI, LO)])):
                        mm = nc.tensor.matmul(acc[k][:], a, w, start=(n == 0 and m == 0), stop=(n == H - 1 and m == 2))
                if n == H - 1:
                    mm.then_inc(projected, 1)

            def turn(b, k, early):
                pe.wait_ge(normed, b + 1)
                if early:
                    pe.wait_ge(const_in, 64)
                    pe.wait_ge(ones_ready, 1)
                if not early:
                    pe.wait_ge(copied, b)
                for c in range(NC):
                    mm = nc.tensor.transpose(xtp[:, c, :], x1[k][:, c * P:(c + 1) * P], ident[:])
                mm.then_inc(turned, 1)

            def logits(b, early):
                pe.wait_ge(copied, b + 1)
                if not early:
                    pe.wait_ge(topped, b)
                for c in range(NC):
                    mm = nc.tensor.matmul(lg[:], x1T[:, c, :], rwT[:, c, :], start=(c == 0), stop=(c == NC - 1))
                mm.then_inc(routed, 1)

            def sums(b):
                pe.wait_ge(masked, b + 1)
                nc.tensor.matmul(cum[:], lower[:], mask[:], start=True, stop=True)
                nc.tensor.matmul(tot[:], ones[:], mask[:], start=True, stop=True).then_inc(summed, 1)

            def step(i, first):
                for k in range(2):
                    b = i * 2 + k
                    pe.wait_ge(ot_in[k][0], i * 16 + 16)
                    if not first:
                        pe.wait_ge(normed, b - 1)
                    project(b, k, range(H // 2), first and k == 0)
                    if not first:
                        sums(b - 2)
                    if not (first and k == 0):
                        turn(b - 1, 1 - k, first)
                    pe.wait_ge(ot_in[k][1], i * 16 + 16)
                    project(b, k, range(H // 2, 3 * H // 4), first and k == 0)
                    if not (first and k == 0):
                        logits(b - 1, first)
                    project(b, k, range(3 * H // 4, H), first and k == 0)

            loop(pe, NB // 2, step)
            sums(NB - 2)
            turn(NB - 1, 1, False)
            logits(NB - 1, False)
            sums(NB - 1)

        @block.scalar
        def _(act):
            act.wait_ge(wo_in, 16)
            for n in range(PARTS):
                part = slice(n * H // PARTS, (n + 1) * H // PARTS)
                if n == PARTS - 1:
                    act.wait_ge(wo_last_in, 16)
                nc.scalar.copy(wo_s[HI][:, part, :], wo_part(n)).then_inc(wo_hi, 1)

            def step(i, first):
                for k in range(2):
                    b = i * 2 + k
                    act.wait_ge(var_ready, b + 1)
                    nc.scalar.activation(sd[:], mv[:, 1:2], ACT.Sqrt, bias=eps[:]).then_inc(sd_ready, 1)
                    act.wait_ge(turned, b + 1)
                    if not (first and k == 0):
                        act.wait_ge(routed, b)
                    nc.scalar.copy(x1T[:], xtp[:]).then_inc(copied, 1)
                    act.wait_ge(topped, b + 1)
                    nc.scalar.activation(et[:], top[:], ACT.Exp, bias=ntop[:], accum_out=esum[:]).then_inc(exped, 1)

            loop(act, NB // 2, step)

        @block.vector
        def _(dve):
            nc.vector.memset(zero[:], 0).then_inc(zeroed, 1)
            nc.vector.memset(ones[:], 1.0).then_inc(ones_ready, 1)
            nc.vector.memset(eps[:], EPS)
            nc.vector.memset(count[:], 0.0)
            for n in range(PARTS):
                part = slice(n * H // PARTS, (n + 1) * H // PARTS)
                dve.wait_ge(wo_hi, n + 1)
                nc.vector.tensor_tensor(wo_s[LO][:, part, :], wo_part(n), wo_s[HI][:, part, :].bitcast(F32),
                                        ALU.subtract).then_inc(wo_lo, 1)
            dve.wait_ge(iota_ready, 1)

            def chain(done, links, b):
                at = [0]

                def link(ins):
                    at[0] += 1
                    assert at[0] <= links
                    ins.then_inc(done, 1)
                    wait_alone(dve, passed, done, b * links + at[0])
                return link

            def normalise(b, k, i, early):
                link = chain(norm_step, 3, b)
                dve.wait_ge(projected, b + 1)
                dve.wait_ge(biased, b + 1)
                link(nc.vector.tensor_tensor(h[k][:], acc[k][:], xb[k][:], ALU.add))
                link(nc.vector.bn_stats(st[:], h[k][:]))
                nc.vector.bn_aggr(mv[:], st[:]).then_inc(var_ready, 1)
                dve.wait_ge(sd_ready, b + 1)
                link(nc.vector.reciprocal(rstd[:], sd[:]))
                if not early:
                    dve.wait_ge(x1_out[k], i * 16)
                nc.vector.tensor_scalar(x1[k][:], h[k][:], mv[:, 0:1], rstd[:], ALU.subtract, ALU.mult
                                        ).then_inc(normed, 1)

            def choose(b):
                link = chain(choose_step, 6, b)
                wait_alone(dve, passed, routed, b + 1)
                link(nc.vector.max(top[:], lg[:]))
                link(nc.vector.max_index(topi[:], top[:], lg[:]))
                nc.vector.tensor_scalar(ntop[:], top[:, 0:1], -1.0, None, ALU.mult).then_inc(topped, 1)
                link(nc.vector.tensor_copy(topf[:], topi[:]))
                link(nc.vector.tensor_tensor(hot[:], iota_e[:].unsqueeze(1).to_broadcast([P, TOPK, E]),
                                             topf[:].unsqueeze(2).to_broadcast([P, TOPK, E]), ALU.is_equal))
                nc.vector.tensor_reduce(mask[:], hot[:].rearrange("p k e -> p e k"), AX_X, ALU.add).then_inc(masked, 1)
                dve.wait_ge(exped, b + 1)
                link(nc.vector.reciprocal(einv[:], esum[:]))
                link(nc.vector.tensor_scalar(wk[:], et[:], einv[:], None, ALU.mult))

            def place(b, k, i, early):
                link = chain(place_step, 6, b)
                dve.wait_ge(summed, b + 1)
                link(nc.vector.tensor_tensor(posn[:], cum[:], count[:], ALU.add))
                nc.vector.tensor_tensor(count[:], tot[:], count[:], ALU.add)
                link(nc.vector.tensor_tensor(pick[:], hot[:], posn[:].unsqueeze(1).to_broadcast([P, TOPK, E]), ALU.mult))
                link(nc.vector.tensor_reduce(pos[:], pick[:], AX_X, ALU.add))
                nc.vector.tensor_scalar(over[:], pos[:], float(CAP), float(2 * SLOTS), ALU.is_ge, ALU.mult)
                nc.vector.tensor_scalar(keep[:], pos[:], float(CAP), None, ALU.is_lt)
                link(nc.vector.scalar_tensor_tensor(slot[:], topf[:], float(CAP), pos[:], ALU.mult, ALU.add))
                nc.vector.tensor_tensor(wcomb[:, bass.ds(b, 1), :].rearrange("p o k -> p (o k)"), wk[:], keep[:], ALU.mult)
                link(nc.vector.tensor_tensor(slot_out[:], slot[:], over[:], ALU.add))
                link(nc.vector.tensor_tensor(comb[:, bass.ds(b, 1), :].rearrange("p o k -> p (o k)"), slot[:], keep[:],
                                             ALU.mult))
                if not early:
                    dve.wait_ge(scattered[k], i * (16 * TOPK))
                nc.vector.tensor_copy(slot_i[k][:], slot_out[:]).then_inc(placed, 1)

            def step(i, first, second=False):
                for k in range(2):
                    b = i * 2 + k
                    normalise(b, k, i, first)
                    if k == 1:
                        place(b - 1, 0, i, first)
                    elif not first:
                        place(b - 1, 1, i - 1, second)
                    choose(b)

            step(0, True)
            step(1, False, second=True)
            with dve.Fori(2, NB // 2) as i:
                step(i, False)
            place(NB - 1, 1, NB // 2 - 1, False)

        @block.gpsimd
        def _(pool):
            nc.gpsimd.iota(iota_e[:], [[1, E]], base=0, channel_multiplier=0, allow_small_or_imprecise_dtypes=True)
            for k in range(2):
                nc.gpsimd.iota(tok[k][:], [[0, 1]], base=k * P, channel_multiplier=1).then_inc(iota_ready, 1)
            pool.wait_ge(const_in, 64)

            def residual(b, k, i, early):
                pool.wait_ge(xr_in[k], i * 16 + 16)
                if not early:
                    pool.wait_ge(normed, b - 1)
                nc.gpsimd.tensor_tensor(xb[k][:], xr[k][:], bo_b[:], ALU.add).then_inc(biased, 1)

            def scatter(b, k, i, early):
                if not early:
                    wait_alone(pool, passed, scattered[k], i * (16 * TOPK))
                    nc.gpsimd.tensor_scalar(tok[k][:], tok[k][:], float(2 * P), None, ALU.add).then_inc(tok_next, 1)
                    pool.wait_ge(tok_next, b - 1)
                wait_alone(pool, passed, placed, b + 1)
                for n in range(TOPK):
                    nc.gpsimd.indirect_dma_start(
                        out=slot_d, out_offset=bass.IndirectOffsetOnAxis(ap=slot_i[k][:, n:n + 1], axis=0),
                        in_=tok[k][:], in_offset=None, bounds_check=SLOTS - 1, oob_is_err=False
                    ).then_inc(scattered[k], 16)

            for k in range(2):
                residual(k, k, 0, True)
            pool.wait_ge(iota_ready, 2)
            pool.wait_ge(zeroed, 17)

            def step(i, first, last=False):
                for k in range(2):
                    b = i * 2 + k
                    if not last:
                        residual(b + 2, k, i + 1, False)
                    scatter(b, k, i, first)

            step(0, True)
            with pool.Fori(1, NB // 2 - 1) as i:
                step(i, False)
            step(NB // 2 - 1, False, last=True)
            for k in range(2):
                pool.wait_ge(scattered[k], NB // 2 * (16 * TOPK))


def stage_experts(nc, passed, gu, dn, ident_d, slot_d, x1_d, y_d):
    PAIRS = E // 2
    GU = 3 * P
    with ExitStack() as ctx:
        def sb(name, shape, dt=F32):
            return ctx.enter_context(nc.sbuf_tensor("p4_" + name, shape, dt))

        def ps(name, shape):
            return ctx.enter_context(nc.psum_tensor("p4_" + name, shape, F32))

        def sem(name):
            return ctx.enter_context(nc.semaphore("p4_" + name))

        WCOLS = NC * GU + C
        ident = sb("ident", [P, P])
        table_i = sb("table_i", [P, P], I32)
        table_f = sb("table_f", [P, P])
        tableT = sb("tableT", [P, E, CH], U32)
        w_raw = [sb(f"w_raw{k}", [P, WCOLS]) for k in range(2)]
        t_raw = sb("t_raw", [P, C])
        w_s = [[sb(f"w{k}{s}", [P, WCOLS], F32R) for s in "hl"] for k in range(2)]
        t_x = [sb(f"t_x{k}", [P, C], F32R) for k in range(2)]
        idx = [sb(f"idx{k}", [P, CH], U32) for k in range(2)]
        xg = [[sb(f"xg{k}{c}", [P, C]) for c in range(CH)] for k in range(2)]
        xT = [sb(f"xT{s}", [P, NC, CAP], F32R) for s in "hl"]
        sg, sgt = sb("sg", [P, CAP]), sb("sgt", [P, CAP])
        h = sb("h", [P, 2, CAP])
        h_s = [sb(f"h{s}", [P, 2, CAP], F32R) for s in "hl"]
        y = [[sb(f"y{k}{c}", [P, C]) for c in range(CH)] for k in range(2)]

        tp = [ps(f"tp{c}", [P, NC, P]) for c in range(CH)]
        pgu = ps("pgu", [P, 2, CAP])
        prest = ps("prest", [P, CAP])
        py = [ps(f"py{c}", [P, C]) for c in range(CH)]

        const_in, table_ready, idx_ready = sem("const_in"), sem("table_ready"), sem("idx_ready")
        gu_in = [sem(f"gu_in{k}") for k in range(2)]
        dn_in = [sem(f"dn_in{k}") for k in range(2)]
        t_in = sem("t_in")
        x_in = [[sem(f"x_in{k}{c}") for c in range(CH)] for k in range(2)]
        gu_hi, gu_lo, dn_hi, dn_lo = sem("gu_hi"), sem("gu_lo"), sem("dn_hi"), sem("dn_lo")
        t_hi, t_lo = sem("t_hi"), sem("t_lo")
        turned, x_hi, x_lo = sem("turned"), sem("x_hi"), sem("x_lo")
        gated, silued, rest_silued, h_main, h_rest = (sem("gated"), sem("silued"), sem("rest_silued"), sem("h_main"),
                                                      sem("h_rest"))
        h_part, h_split, h_cross = sem("h_part"), sem("h_split"), sem("h_cross")
        downed, y_a, y_b = sem("downed"), sem("y_a"), sem("y_b")
        y_out = [[sem(f"y_out{k}{c}") for c in range(CH)] for k in range(2)]

        GUC, DNC = slice(0, NC * GU), slice(NC * GU, WCOLS)

        def rest(k):
            half = slice(k * IT, (k + 1) * IT)
            return half, slice((1 - k) * IT, (2 - k) * IT)

        def ahead(i, k, n):
            return i + (k + n) // 2, (k + n) % 2

        def first(i):
            return isinstance(i, int) and i == 0

        def exists(i):
            return not isinstance(i, int) or i < PAIRS

        def steps(eng, step, behind=2):
            for k in range(2):
                step(0, k)
            with eng.Fori(1, PAIRS - behind) as i:
                for k in range(2):
                    step(i, k)
            for i in range(PAIRS - behind, PAIRS):
                for k in range(2):
                    step(i, k)

        block = ctx.enter_context(nc.Block())

        @block.sync
        def _(sp):
            def load(i, k, cols, split, done):
                if not first(i):
                    sp.wait_ge(split, i * 2 + (k - 1))
                sp.dma_start(w_raw[k][:, cols], gu[bass.ds(i * 2 + k, 1), :, cols].rearrange("o p n -> (o p) n")
                             ).then_inc(done[k], 16)

            def load_gu(i, k):
                load(i, k, GUC, gu_lo, gu_in)

            def load_dn(i, k):
                load(i, k, DNC, dn_lo, dn_in)

            def load_t(i):
                if not first(i):
                    sp.wait_ge(t_lo, i)
                sp.dma_start(t_raw[:], dn[bass.ds(i, 1)].rearrange("o p n -> (o p) n")).then_inc(t_in, 16)

            def step(i, k):
                e = i * 2 + k
                if k == 0 and exists(i + 1):
                    load_t(i + 1)
                if exists(ahead(i, k, 5)[0]):
                    load_gu(*ahead(i, k, 5))
                for c, done in ((0, y_a), (1, y_b)):
                    sp.wait_ge(done, e + 1)
                    sp.dma_start(y_d[bass.ds(e * CAP + c * P, P), :], y[k][c][:]).then_inc(y_out[k][c], 16)
                if exists(i + 2):
                    load_dn(i + 2, k)

            sp.dma_start(table_i[:], slot_d.rearrange("(p s) o -> p (s o)", p=P)).then_inc(const_in, 16)
            sp.dma_start(ident[:], ident_d).then_inc(const_in, 16)
            load_gu(0, 0)
            for c in range(CH):
                sp.wait_ge(x_in[0][c], 16)
            load_gu(0, 1)
            for k in range(2):
                load_dn(0, k)
            load_t(0)
            for i, k in ((1, 0), (1, 1), (2, 0)):
                load_gu(i, k)
            for k in range(2):
                load_dn(1, k)
            steps(sp, step, behind=3)
            for k in range(2):
                for c in range(CH):
                    sp.wait_ge(y_out[k][c], 16 * PAIRS)

        @block.tensor
        def _(pe):
            def turn(i, k):
                for c in range(CH):
                    pe.wait_ge(x_in[k][c], i * 16 + 16)
                    if not (first(i) and k == 0):
                        pe.wait_ge(x_lo, (i * 2 + k) * CH + (c - CH + 1))
                    for d in range(NC):
                        mm = nc.tensor.transpose(tp[c][:, d, :], xg[k][c][:, d * P:(d + 1) * P], ident[:])
                    mm.then_inc(turned, 1)

            def gate_up(i, k):
                e = i * 2 + k
                pe.wait_ge(x_lo, e * CH + CH)
                pe.wait_ge(gu_lo, e + 1)
                if not (first(i) and k == 0):
                    pe.wait_ge(h_rest, e)
                for f, out in enumerate((pgu[:, 0, :], pgu[:, 1, :], prest[:])):
                    for m, (a, b) in enumerate(split3(w_s[k], xT)):
                        for d in range(NC):
                            col = d * GU + f * P
                            mm = nc.tensor.matmul(out, a[:, col:col + P], b[:, d, :], start=(m == 0 and d == 0),
                                                  stop=(m == 2 and d == NC - 1))
                mm.then_inc(gated, 1)

            def down(i, k):
                e = i * 2 + k
                half, _ = rest(k)
                pe.wait_ge(h_cross, e + 1)
                pe.wait_ge(dn_lo, e + 1)
                if k == 0:
                    pe.wait_ge(t_lo, i + 1)
                if not (first(i) and k == 0):
                    pe.wait_ge(y_a, e)
                    pe.wait_ge(y_b, e)
                for c in range(CH):
                    cols = slice(c * P, (c + 1) * P)
                    for m, (a, b) in enumerate(split3(h_s, w_s[k])):
                        nc.tensor.matmul(py[c][:], a[:, 0, cols], b[:, DNC], start=(m == 0), stop=False)
                    nc.tensor.matmul(py[c][:], h_s[LO][:, 1, cols], t_x[k][:], start=False, stop=False)
                    mm = nc.tensor.matmul(py[c][:], h_s[HI][half, 1, cols], t_x[k][half, :], start=False, stop=True)
                mm.then_inc(downed, 1)

            def step(i, k):
                for f, n in ((gate_up, 1), (turn, 2), (down, 0)):
                    if exists(ahead(i, k, n)[0]):
                        f(*ahead(i, k, n))

            pe.wait_ge(const_in, 32)
            pe.wait_ge(table_ready, 1)
            nc.tensor.transpose(tp[0][:, 0, :], table_f[:], ident[:]).then_inc(table_ready, 1)
            pe.wait_ge(table_ready, 3)
            turn(0, 0)
            gate_up(0, 0)
            turn(0, 1)
            steps(pe, step)

        @block.scalar
        def _(act):
            def gate_up_hi(i, k):
                act.wait_ge(gu_in[k], i * 16 + 16)
                if not first(i):
                    act.wait_ge(gated, i * 2 + (k - 1))
                nc.scalar.copy(w_s[k][HI][:, GUC], w_raw[k][:, GUC]).then_inc(gu_hi, 1)

            def down_hi(i, k):
                act.wait_ge(dn_in[k], i * 16 + 16)
                if not first(i):
                    act.wait_ge(downed, i * 2 + (k - 1))
                nc.scalar.copy(w_s[k][HI][:, DNC], w_raw[k][:, DNC]).then_inc(dn_hi, 1)

            def rests_hi(i):
                act.wait_ge(t_in, i * 16 + 16)
                if not first(i):
                    act.wait_ge(downed, i * 2)
                for k in range(2):
                    half, _ = rest(k)
                    nc.scalar.copy(t_x[k][half, :], t_raw[half, :]).then_inc(t_hi, 1)

            def turn_hi(i, k):
                e = i * 2 + k
                for c in range(CH):
                    act.wait_ge(turned, e * CH + (c + 1))
                    if not (first(i) and k == 0):
                        act.wait_ge(gated, e)
                    nc.scalar.copy(xT[HI][:, :, c * P:(c + 1) * P], tp[c][:]).then_inc(x_hi, 1)

            def silu(i, k):
                e = i * 2 + k
                half, other = rest(k)
                act.wait_ge(gated, e + 1)
                if not (first(i) and k == 0):
                    act.wait_ge(h_rest, e)
                nc.scalar.activation(sg[:], pgu[:, 0, :], ACT.Silu).then_inc(silued, 1)
                nc.scalar.activation(sgt[half, :], prest[other, :], ACT.Silu).then_inc(rest_silued, 1)

            def cross(i, k):
                e = i * 2 + k
                half, other = rest(k)
                act.wait_ge(h_split, e + 1)
                nc.scalar.copy(h_s[LO][other, 1, :], h[half, 1, :]).then_inc(h_cross, 1)

            def rows(i, k):
                act.wait_ge(downed, i * 2 + (k + 1))
                if not first(i):
                    act.wait_ge(y_out[k][0], i * 16)
                nc.scalar.copy(y[k][0][:], py[0][:]).then_inc(y_a, 1)

            def step(i, k):
                for f, n in ((silu, 1), (turn_hi, 2), (gate_up_hi, 3), (rows, 0), (down_hi, 2)):
                    if exists(ahead(i, k, n)[0]):
                        f(*ahead(i, k, n))
                if k == 1 and exists(i + 1):
                    rests_hi(i + 1)
                if exists(ahead(i, k, 1)[0]):
                    cross(*ahead(i, k, 1))

            gate_up_hi(0, 0)
            turn_hi(0, 0)
            gate_up_hi(0, 1)
            down_hi(0, 0)
            down_hi(0, 1)
            rests_hi(0)
            turn_hi(0, 1)
            silu(0, 0)
            gate_up_hi(1, 0)
            cross(0, 0)
            steps(act, step)

        @block.vector
        def _(dve):
            def gate_up_lo(i, k):
                dve.wait_ge(gu_hi, i * 2 + (k + 1))
                nc.vector.tensor_tensor(w_s[k][LO][:, GUC], w_raw[k][:, GUC], w_s[k][HI][:, GUC].bitcast(F32), ALU.subtract
                                        ).then_inc(gu_lo, 1)

            def down_lo(i, k):
                dve.wait_ge(dn_hi, i * 2 + (k + 1))
                nc.vector.tensor_tensor(w_s[k][LO][:, DNC], w_raw[k][:, DNC], w_s[k][HI][:, DNC].bitcast(F32), ALU.subtract
                                        ).then_inc(dn_lo, 1)

            def rests_lo(i):
                dve.wait_ge(t_hi, i * 2 + 2)
                for k in range(2):
                    half, other = rest(k)
                    ins = nc.vector.tensor_tensor(t_x[k][other, :], t_raw[half, :], t_x[k][half, :].bitcast(F32),
                                                  ALU.subtract)
                ins.then_inc(t_lo, 1)

            def turn_lo(i, k):
                for c in range(CH):
                    dve.wait_ge(x_hi, (i * 2 + k) * CH + (c + 1))
                    cols = slice(c * P, (c + 1) * P)
                    nc.vector.tensor_tensor(xT[LO][:, :, cols], tp[c][:], xT[HI][:, :, cols].bitcast(F32), ALU.subtract
                                            ).then_inc(x_lo, 1)

            def gate(i, k):
                e = i * 2 + k
                half, _ = rest(k)
                dve.wait_ge(silued, e + 1)
                if not (first(i) and k == 0):
                    dve.wait_ge(h_cross, e)
                nc.vector.tensor_tensor(h[:, 0, :], pgu[:, 1, :], sg[:], ALU.mult).then_inc(h_main, 1)
                dve.wait_ge(rest_silued, e + 1)
                nc.vector.tensor_tensor(h[half, 1, :], prest[half, :], sgt[half, :], ALU.mult).then_inc(h_rest, 1)

            def rows(i, k):
                dve.wait_ge(downed, i * 2 + (k + 1))
                if not first(i):
                    dve.wait_ge(y_out[k][1], i * 16)
                nc.vector.tensor_copy(y[k][1][:], py[1][:]).then_inc(y_b, 1)

            def step(i, k):
                for f, n in ((gate, 1), (turn_lo, 2), (gate_up_lo, 3), (rows, 0), (down_lo, 2)):
                    if exists(ahead(i, k, n)[0]):
                        f(*ahead(i, k, n))
                if k == 1 and exists(i + 1):
                    rests_lo(i + 1)

            nc.vector.memset(h[:], 0.0)
            dve.wait_ge(const_in, 32)
            nc.vector.tensor_copy(table_f[:], table_i[:]).then_inc(table_ready, 1)
            dve.wait_ge(table_ready, 2)
            nc.vector.tensor_copy(tableT[:].rearrange("p e c -> p (e c)"), tp[0][:, 0, :]).then_inc(table_ready, 1)
            gate_up_lo(0, 0)
            turn_lo(0, 0)
            gate_up_lo(0, 1)
            down_lo(0, 0)
            down_lo(0, 1)
            rests_lo(0)
            turn_lo(0, 1)
            gate(0, 0)
            gate_up_lo(1, 0)
            steps(dve, step)

        @block.gpsimd
        def _(pool):
            def gather(i, k):
                e = i * 2 + k
                if not first(i):
                    pool.wait_ge(turned, e * CH - CH)
                nc.gpsimd.tensor_copy(idx[k][:], tableT[:, bass.ds(e, 1), :].rearrange("p o c -> p (o c)")
                                      ).then_inc(idx_ready, 1)
                wait_alone(pool, passed, idx_ready, e + 1)
                for c in range(CH):
                    nc.gpsimd.indirect_dma_start(
                        out=xg[k][c][:], out_offset=None, in_=x1_d,
                        in_offset=bass.IndirectOffsetOnAxis(ap=idx[k][:, c:c + 1], axis=0)).then_inc(x_in[k][c], 16)

            def split_h(i, k):
                e = i * 2 + k
                if not (first(i) and k == 0):
                    pool.wait_ge(downed, e)
                pool.wait_ge(h_main, e + 1)
                wait_alone(pool, passed, h_rest, e + 1)
                nc.gpsimd.tensor_scalar(h_s[HI][:], h[:], 1.0, 1.0, ALU.mult, ALU.mult).then_inc(h_part, 1)
                wait_alone(pool, passed, h_part, e + 1)
                nc.gpsimd.tensor_tensor(h_s[LO][:], h[:], h_s[HI][:].bitcast(F32), ALU.subtract).then_inc(h_split, 1)

            def step(i, k):
                for f, n in ((split_h, 1), (gather, 4)):
                    if exists(ahead(i, k, n)[0]):
                        f(*ahead(i, k, n))

            pool.wait_ge(table_ready, 3)
            gather(0, 0)
            gather(0, 1)
            gather(1, 0)
            split_h(0, 0)
            gather(1, 1)
            steps(pool, step)


def stage_combine(nc, passed, x1_d, y_d, comb, wcomb, out):
    with ExitStack() as ctx:
        def sb(name, shape, dt=F32):
            return ctx.enter_context(nc.sbuf_tensor("p5_" + name, shape, dt))

        def sem(name):
            return ctx.enter_context(nc.semaphore("p5_" + name))

        eps = sb("eps", [P, 1])
        x1 = [sb(f"x1{k}", [P, C]) for k in range(2)]
        idx = [sb(f"idx{k}", [P, TOPK], U32) for k in range(2)]
        rows = [[sb(f"rows{k}{n}", [P, C]) for n in range(TOPK)] for k in range(2)]
        acc = [[sb(f"acc{k}{n}", [P, C]) for n in range(2)] for k in range(2)]
        total = [sb(f"total{k}", [P, C]) for k in range(2)]
        st, mv = sb("st", [P, 6]), sb("mv", [P, 2])
        sd, rstd = sb("sd", [P, 1]), sb("rstd", [P, 1])
        res = [sb(f"res{k}", [P, C]) for k in range(2)]

        x1_in = [sem(f"x1_in{k}") for k in range(2)]
        rows_in = [[sem(f"rows_in{k}{n}") for n in range(TOPK // 2)] for k in range(2)]
        res_out = [sem(f"res_out{k}") for k in range(2)]
        indexed, chain, summed, var_ready, sd_ready, normed, eps_ready = (
            sem("indexed"), sem("chain"), sem("summed"), sem("var_ready"), sem("sd_ready"), sem("normed"), sem("eps_ready"))

        block = ctx.enter_context(nc.Block())

        @block.sync
        def _(sp):
            for k in range(2):
                sp.dma_start(x1[k][:], x1_d[k * P:(k + 1) * P, :]).then_inc(x1_in[k], 16)

            def step(i, last=False):
                for k in range(2):
                    b = i * 2 + k
                    if not last:
                        sp.wait_ge(summed, b + 1)
                        sp.dma_start(x1[k][:], x1_d[bass.ds((b + 2) * P, P), :]).then_inc(x1_in[k], 16)
                    sp.wait_ge(normed, b + 1)
                    sp.dma_start(out[bass.ds(b * P, P), :], res[k][:]).then_inc(res_out[k], 16)

            with sp.Fori(0, NB // 2 - 1) as i:
                step(i)
            step(NB // 2 - 1, last=True)
            for k in range(2):
                sp.wait_ge(res_out[k], 16 * (NB // 2))

        @block.gpsimd
        def _(pool):
            def step(i, first):
                for k in range(2):
                    b = i * 2 + k
                    if not first:
                        pool.wait_ge(summed, b - 1)
                    wait_alone(pool, passed, indexed, b + 1)
                    for n in range(TOPK):
                        nc.gpsimd.indirect_dma_start(
                            out=rows[k][n][:], out_offset=None, in_=y_d,
                            in_offset=bass.IndirectOffsetOnAxis(ap=idx[k][:, n:n + 1], axis=0)).then_inc(rows_in[k][n // 2], 16)

            loop(pool, NB // 2, step)

        @block.vector
        def _(dve):
            nc.vector.memset(eps[:], EPS).then_inc(eps_ready, 1)
            STEPS = TOPK + 2

            def index(b, k):
                nc.vector.tensor_copy(idx[k][:], comb[:, bass.ds(b, 1), :].rearrange("p o k -> p (o k)")
                                      ).then_inc(indexed, 1)

            for k in range(2):
                index(k, k)

            def step(i, first, last=False):
                for k in range(2):
                    b = i * 2 + k
                    dve.wait_ge(x1_in[k], i * 16 + 16)
                    for n in range(TOPK):
                        if n % 2 == 0:
                            dve.wait_ge(rows_in[k][n // 2], i * 32 + 32)
                        part, weight = acc[k][n % 2], wcomb[:, bass.ds(b, 1), n:n + 1].rearrange("p o k -> p (o k)")
                        if n >= 2:
                            dve.wait_ge(chain, b * STEPS + n - 1)
                        if n == 1:
                            ins = nc.vector.tensor_scalar(part[:], rows[k][n][:], weight, None, ALU.mult)
                        else:
                            ins = nc.vector.scalar_tensor_tensor(part[:], rows[k][n][:], weight, (part if n else x1[k])[:],
                                                                 ALU.mult, ALU.add)
                        ins.then_inc(chain, 1)
                    dve.wait_ge(chain, b * STEPS + TOPK)
                    nc.vector.tensor_tensor(total[k][:], acc[k][0][:], acc[k][1][:], ALU.add).then_inc(summed, 1)
                    dve.wait_ge(summed, b + 1)
                    if not last:
                        index(b + 2, k)
                    nc.vector.bn_stats(st[:], total[k][:]).then_inc(chain, 1)
                    wait_alone(dve, passed, chain, b * STEPS + TOPK + 1)
                    nc.vector.bn_aggr(mv[:], st[:]).then_inc(var_ready, 1)
                    dve.wait_ge(sd_ready, b + 1)
                    nc.vector.reciprocal(rstd[:], sd[:]).then_inc(chain, 1)
                    dve.wait_ge(chain, b * STEPS + TOPK + 2)
                    if not first:
                        dve.wait_ge(res_out[k], i * 16)
                    nc.vector.tensor_scalar(res[k][:], total[k][:], mv[:, 0:1], rstd[:], ALU.subtract, ALU.mult
                                            ).then_inc(normed, 1)

            step(0, True)
            with dve.Fori(1, NB // 2 - 1) as i:
                step(i, False)
            step(NB // 2 - 1, False, last=True)

        @block.scalar
        def _(act):
            act.wait_ge(eps_ready, 1)

            def step(i, first):
                for k in range(2):
                    act.wait_ge(var_ready, i * 2 + k + 1)
                    nc.scalar.activation(sd[:], mv[:, 1:2], ACT.Sqrt, bias=eps[:]).then_inc(sd_ready, 1)

            loop(act, NB // 2, step)


def build(nc, x, wqk, wv, bv, cos, sin, ident, mask, lower, wo, bo, rw, gu, dn, out):
    qk_d = nc.dram_tensor("qk_scratch", [H + HKV, HD, NT, 2, 512], F32, kind="Internal").ap()
    v_d = nc.dram_tensor("v_scratch", [NB, HKV, P, 2, HD], F32, kind="Internal").ap()
    o_d = nc.dram_tensor("o_scratch", [NB, HD, HKV, G, 2, P], F32, kind="Internal").ap()
    x1_d = nc.dram_tensor("x1_scratch", [T, C], F32, kind="Internal").ap()
    slot_d = nc.dram_tensor("slot_scratch", [SLOTS, 1], I32, kind="Internal").ap()
    y_d = nc.dram_tensor("y_scratch", [SLOTS, C], F32, kind="Internal").ap()
    with ExitStack() as ctx:
        comb = ctx.enter_context(nc.sbuf_tensor("comb", [P, NB, TOPK], F32))
        wcomb = ctx.enter_context(nc.sbuf_tensor("wcomb", [P, NB, TOPK], F32))
        passed = ctx.enter_context(nc.semaphore("passed"))
        stage_project(nc, passed, x, wqk, wv, bv, cos, sin, ident, qk_d, v_d)
        with nc.sbuf_tensor("wo_raw", [P, WO_EARLY, C], F32) as wo_raw, nc.semaphore("wo_in") as wo_in:
            stage_attend(nc, passed, ident, mask, qk_d, v_d, o_d, wo, wo_raw, wo_in)
            stage_route(nc, passed, x, wo, bo, rw, ident, lower, o_d, x1_d, slot_d, comb, wcomb, wo_raw, wo_in)
        stage_experts(nc, passed, gu, dn, ident, slot_d, x1_d, y_d)
        stage_combine(nc, passed, x1_d, y_d, comb, wcomb, out)


def constants():
    theta = (1.0 / 10000.0 ** (np.arange(0, HD, 2, dtype=np.float32) / np.float32(HD))).astype(np.float32)
    freqs = (np.arange(T, dtype=np.float32)[:, None] * theta[None, :]).astype(np.float32)
    root = np.float32((1.0 / np.sqrt(H)) ** 0.5)
    cos, sin = (np.cos(freqs) * root).T, (np.sin(freqs) * root).T
    cos = np.concatenate([cos, cos]).astype(np.float32)
    sin = np.concatenate([-sin, sin]).astype(np.float32)
    row, col = np.arange(P)[:, None], np.arange(P)[None, :]
    mask = np.where(col <= row, 0.0, MASKED).astype(np.float32)
    lower = (row < col).astype(np.float32)
    return {"cos": cos, "sin": sin, "ident": np.eye(P, dtype=np.float32), "mask": mask, "lower": lower}


def layout(a):
    x, Wq, bq, Wk, bk, Wv, bv, Wo, bo, rw, gu, dn = a
    wq = Wq.reshape(NC, P, G, HKV, HD // 2, 2).transpose(3, 2, 1, 0, 5, 4).reshape(H, P, NC * HD)
    wk = Wk.reshape(NC, P, HKV, HD // 2, 2).transpose(2, 1, 0, 4, 3).reshape(HKV, P, NC * HD)
    bqh = bq.reshape(G, HKV, HD // 2, 2).transpose(1, 0, 3, 2).reshape(H, HD)
    bkh = bk.reshape(HKV, HD // 2, 2).transpose(0, 2, 1).reshape(HKV, HD)
    wo = Wo.reshape(G, HKV, HD, C).transpose(2, 1, 0, 3).reshape(HD, H, C)
    g, u = gu[:, :, :I], gu[:, :, I:]
    rest = np.concatenate([u[:, :, P:], g[:, :, P:]], 2)
    rest[1::2] = np.concatenate([g[1::2, :, P:], u[1::2, :, P:]], 2)
    cols = np.concatenate([g[:, :, :P], u[:, :, :P], rest], 2)
    cols = cols.reshape(E, NC, P, 3 * P).transpose(0, 2, 1, 3).reshape(E, P, NC * 3 * P)
    return {
        "x": x.reshape(T, C), "wqk": np.concatenate([np.concatenate([wq, wk]), np.concatenate([bqh, bkh])[:, :, None]], 2),
        "wv": Wv.reshape(NC, P, C).transpose(1, 0, 2).reshape(P, NC * C), "bv": bv, "wo": wo, "bo": bo,
        "rw": rw.T.reshape(NC, P, E).transpose(1, 0, 2), "gu": np.concatenate([cols, dn[:, :P, :]], 2),
        "dn": dn[:, P:, :].reshape(E // 2, 2 * IT, C),
    }


_ORDER = ["x", "wqk", "wv", "bv", "cos", "sin", "ident", "mask", "lower", "wo", "bo", "rw", "gu", "dn"]
_INS = ["L0_attn_x", "L0_attn_Wq", "L0_attn_bq", "L0_attn_Wk", "L0_attn_bk", "L0_attn_Wv", "L0_attn_bv", "L0_attn_Wo",
        "L0_attn_bo", "L0_ffn_router_weight", "L0_ffn_gate_up_proj", "L0_ffn_down_proj"]


def kernel(**inputs):
    import concourse.bacc as bacc
    from concourse.bass_utils import run_bass_kernel_spmd

    arrays = layout([np.asarray(inputs[n]) for n in _INS]) | constants()
    nc = bacc.Bacc("TRN2", target_bir_lowering=False, num_devices=1)
    feed, args = {}, []
    for name in _ORDER:
        a = np.ascontiguousarray(arrays[name])
        feed[f"in_{name}"] = a
        args.append(nc.dram_tensor(f"in_{name}", a.shape, mybir.dt.from_np(a.dtype), kind="ExternalInput").ap())
    out = nc.dram_tensor("out", [T, C], F32, kind="ExternalOutput").ap()
    build(nc, *args, out)
    r = run_bass_kernel_spmd(nc, [feed], core_ids=[0])
    return r.results[0]["out"].reshape(1, T, C)
```
